# Optimizing a Trainium2 kernel written in Bass

```python
import numpy as np
import jax
import jax.numpy as jnp

def _softmax(x, axis=-1):
    return jax.nn.softmax(x, axis=axis)

def _gelu(x):
    return jax.nn.gelu(x, approximate=True)

def _silu(x):
    return jax.nn.silu(x)

def _sigmoid(x):
    return jax.nn.sigmoid(x)

def _layernorm(x, axis=-1, eps=1e-05):
    m = jnp.mean(x, axis=axis, keepdims=True)
    v = jnp.var(x, axis=axis, keepdims=True)
    return (x - m) / jnp.sqrt(v + eps)

def _scatter_add(tgt, idx, src, axis=0):
    return tgt.at[idx].add(src)

def _segment_sum(src, seg, n):
    return jax.ops.segment_sum(src, seg, n)
kernel_name = 'mk_lm_tower_d1_tok_ids512_r4_2b89a7'

def setup_inputs(seed: int=0):
    np.random.seed(seed)
    _w = jnp.asarray

    def _rec_inputs():
        import jax
        import jax.numpy as jnp
        _rk = jax.random.key(seed)
        x = jax.random.randint(jax.random.fold_in(_rk, 1), (128, 128), 0, 22, jnp.int32)
        itok_BS_0_21 = jax.random.randint(jax.random.fold_in(_rk, 21), (128, 128), 0, 22, jnp.int32)
        return (x, itok_BS_0_21)
    x, itok_BS_0_21 = _rec_inputs()

    def _L0_tok_setup():
        import jax, jax.numpy as jnp
        import numpy as np
        NEG = -100000000.0

        def nw_value(theta, A):
            N, M = theta.shape
            ii = jnp.arange(N + 1)
            neg1 = jnp.full((1,), NEG, theta.dtype)
            prev2 = jnp.full((N + 1,), NEG, theta.dtype).at[0].set(0.0)
            prev = jnp.full((N + 1,), NEG, theta.dtype)

            def step(carry, d):
                prev, prev2 = carry
                jj = d - ii
                valid = (ii >= 1) & (ii <= N) & (jj >= 1) & (jj <= M)
                th = theta[jnp.clip(ii - 1, 0, N - 1), jnp.clip(jj - 1, 0, M - 1)]
                diag = jnp.concatenate([neg1, prev2[:-1]])
                up = jnp.concatenate([neg1, prev[:-1]]) + A
                left = prev + A
                v = jax.nn.logsumexp(jnp.stack([diag, up, left]), axis=0)
                new = jnp.where(valid, th + v, NEG)
                return ((new, prev), None)
            (last, _), _ = jax.lax.scan(step, (prev, prev2), jnp.arange(2, N + M + 1))
            return last[N]
        key = jax.random.key(seed)
        ks = jax.random.split(key, 7)
        B, N, M = (16, 128, 128)
        n_alpha, n_input, n_embed = (22, 128, 128)
        return {'x': jax.random.randint(ks[0], (B, N), 0, n_alpha, dtype=jnp.int32), 'y': jax.random.randint(ks[1], (B, M), 0, n_alpha, dtype=jnp.int32), 'W_embed': jax.random.normal(ks[2], (n_alpha, n_input), jnp.float32) * 0.1, 'W_proj': jax.random.normal(ks[3], (n_input, n_embed), jnp.float32) * 0.05, 'b_proj': jax.random.normal(ks[4], (n_embed,), jnp.float32) * 0.01, 'W_gap': jax.random.normal(ks[5], (2 * n_embed,), jnp.float32) * 0.05, 'b_gap': jax.random.normal(ks[6], (1,), jnp.float32) * 0.01}
    _L0_tok_all = _L0_tok_setup()
    _L0_tok_in = {k: v for k, v in _L0_tok_all.items() if k in ('W_embed', 'W_proj', 'b_proj', 'W_gap', 'b_gap')}
    del _L0_tok_all

    def _L0_attn_setup():
        import jax, jax.numpy as jnp
        import numpy as np
        B, T, D, H = (8, 256, 128, 8)
        DK = D // H

        def layer_norm(x, g, b, eps=1e-05):
            mu = jnp.mean(x, axis=-1, keepdims=True)
            var = jnp.var(x, axis=-1, keepdims=True)
            return (x - mu) * jax.lax.rsqrt(var + eps) * g + b

        def rel_shift(x):
            b, h, t1, t2 = x.shape
            xp = jnp.pad(x, ((0, 0), (0, 0), (0, 0), (1, 0)))
            xp = xp.reshape(b, h, t2 + 1, t1)[:, :, 1:, :]
            return xp.reshape(b, h, t1, t2)
        key = jax.random.key(seed)
        ks = jax.random.split(key, 6)
        s = 0.02
        return {'inputs': jax.random.normal(ks[0], (B, T, D), jnp.float32), 'ln1_g': jnp.ones((D,), jnp.float32), 'ln1_b': jnp.zeros((D,), jnp.float32), 'ln2_g': jnp.ones((D,), jnp.float32), 'ln2_b': jnp.zeros((D,), jnp.float32), 'W_qkv': jax.random.normal(ks[1], (3 * D, D), jnp.float32) * s, 'W_pos': jax.random.normal(ks[2], (D, D), jnp.float32) * s, 'W_out': jax.random.normal(ks[3], (D, D), jnp.float32) * s, 'b_out': jnp.zeros((D,), jnp.float32), 'pos_bias_u': jax.random.normal(ks[4], (H, DK), jnp.float32) * s, 'pos_bias_v': jax.random.normal(ks[5], (H, DK), jnp.float32) * s}
    _L0_attn_all = _L0_attn_setup()
    _L0_attn_in = {k: v for k, v in _L0_attn_all.items() if k in ('ln1_g', 'ln1_b', 'ln2_g', 'ln2_b', 'W_qkv', 'W_pos', 'W_out', 'b_out', 'pos_bias_u', 'pos_bias_v')}
    del _L0_attn_all

    def _L0_ffn_setup():
        import jax, jax.numpy as jnp
        import numpy as np
        MICRO_BATCHES = 2
        TOP_K = 2
        D = 128
        E = 8
        B, S = (8, 2048)
        key = jax.random.key(seed)
        ks = jax.random.split(key, 12)
        s = 0.02
        return {'x': jax.random.normal(ks[0], (B, S, D), dtype=jnp.float32), 'ln_g': jnp.ones((D,), jnp.float32), 'ln_b': jnp.zeros((D,), jnp.float32), 'attn_w': jax.random.normal(ks[1], (D, D), jnp.float32) * s, 'attn_b': jnp.zeros((D,), jnp.float32), 'gate_w': jax.random.normal(ks[2], (E, D), jnp.float32) * s, 'fc1_w': jax.random.normal(ks[3], (E, 4 * D, D), jnp.float32) * s, 'fc1_b': jnp.zeros((E, 4 * D), jnp.float32), 'fc2_w': jax.random.normal(ks[4], (E, D, 4 * D), jnp.float32) * s, 'fc2_b': jnp.zeros((E, D), jnp.float32), 'next_w': jax.random.normal(ks[5], (D, D), jnp.float32) * s, 'next_b': jnp.zeros((D,), jnp.float32)}
    _L0_ffn_all = _L0_ffn_setup()
    _L0_ffn_in = {k: v for k, v in _L0_ffn_all.items() if k in ('ln_g', 'ln_b', 'attn_w', 'attn_b', 'gate_w', 'fc1_w', 'fc1_b', 'fc2_w', 'fc2_b', 'next_w', 'next_b')}
    del _L0_ffn_all
    return {'x': x, 'itok_BS_0_21': itok_BS_0_21, 'L0_tok_W_embed': _L0_tok_in['W_embed'], 'L0_tok_W_proj': _L0_tok_in['W_proj'], 'L0_tok_b_proj': _L0_tok_in['b_proj'], 'L0_tok_W_gap': _L0_tok_in['W_gap'], 'L0_tok_b_gap': _L0_tok_in['b_gap'], 'L0_attn_ln1_g': _L0_attn_in['ln1_g'], 'L0_attn_ln1_b': _L0_attn_in['ln1_b'], 'L0_attn_ln2_g': _L0_attn_in['ln2_g'], 'L0_attn_ln2_b': _L0_attn_in['ln2_b'], 'L0_attn_W_qkv': _L0_attn_in['W_qkv'], 'L0_attn_W_pos': _L0_attn_in['W_pos'], 'L0_attn_W_out': _L0_attn_in['W_out'], 'L0_attn_b_out': _L0_attn_in['b_out'], 'L0_attn_pos_bias_u': _L0_attn_in['pos_bias_u'], 'L0_attn_pos_bias_v': _L0_attn_in['pos_bias_v'], 'L0_ffn_ln_g': _L0_ffn_in['ln_g'], 'L0_ffn_ln_b': _L0_ffn_in['ln_b'], 'L0_ffn_attn_w': _L0_ffn_in['attn_w'], 'L0_ffn_attn_b': _L0_ffn_in['attn_b'], 'L0_ffn_gate_w': _L0_ffn_in['gate_w'], 'L0_ffn_fc1_w': _L0_ffn_in['fc1_w'], 'L0_ffn_fc1_b': _L0_ffn_in['fc1_b'], 'L0_ffn_fc2_w': _L0_ffn_in['fc2_w'], 'L0_ffn_fc2_b': _L0_ffn_in['fc2_b'], 'L0_ffn_next_w': _L0_ffn_in['next_w'], 'L0_ffn_next_b': _L0_ffn_in['next_b']}

def reference(x, itok_BS_0_21, L0_tok_W_embed, L0_tok_W_proj, L0_tok_b_proj, L0_tok_W_gap, L0_tok_b_gap, L0_attn_ln1_g, L0_attn_ln1_b, L0_attn_ln2_g, L0_attn_ln2_b, L0_attn_W_qkv, L0_attn_W_pos, L0_attn_W_out, L0_attn_b_out, L0_attn_pos_bias_u, L0_attn_pos_bias_v, L0_ffn_ln_g, L0_ffn_ln_b, L0_ffn_attn_w, L0_ffn_attn_b, L0_ffn_gate_w, L0_ffn_fc1_w, L0_ffn_fc1_b, L0_ffn_fc2_w, L0_ffn_fc2_b, L0_ffn_next_w, L0_ffn_next_b):
    import jax
    import jax.numpy as jnp

    def _L0_tok_ref(x, y, W_embed, W_proj, b_proj, W_gap, b_gap):
        import jax, jax.numpy as jnp
        import numpy as np
        NEG = -100000000.0

        def nw_value(theta, A):
            N, M = theta.shape
            ii = jnp.arange(N + 1)
            neg1 = jnp.full((1,), NEG, theta.dtype)
            prev2 = jnp.full((N + 1,), NEG, theta.dtype).at[0].set(0.0)
            prev = jnp.full((N + 1,), NEG, theta.dtype)

            def step(carry, d):
                prev, prev2 = carry
                jj = d - ii
                valid = (ii >= 1) & (ii <= N) & (jj >= 1) & (jj <= M)
                th = theta[jnp.clip(ii - 1, 0, N - 1), jnp.clip(jj - 1, 0, M - 1)]
                diag = jnp.concatenate([neg1, prev2[:-1]])
                up = jnp.concatenate([neg1, prev[:-1]]) + A
                left = prev + A
                v = jax.nn.logsumexp(jnp.stack([diag, up, left]), axis=0)
                new = jnp.where(valid, th + v, NEG)
                return ((new, prev), None)
            (last, _), _ = jax.lax.scan(step, (prev, prev2), jnp.arange(2, N + M + 1))
            return last[N]
        zx = jnp.take(W_embed, x, axis=0) @ W_proj + b_proj
        zy = jnp.take(W_embed, y, axis=0) @ W_proj + b_proj
        theta = jnp.einsum('bid,bjd->bij', zx, zy)
        merged = jnp.concatenate([zx.mean(axis=1), zy.mean(axis=1)], axis=1)
        A = merged @ W_gap + b_gap[0]
        aln = jax.vmap(jax.grad(nw_value, argnums=0))(theta, A)
        return aln

    def _L0_attn_ref(inputs, ln1_g, ln1_b, ln2_g, ln2_b, W_qkv, W_pos, W_out, b_out, pos_bias_u, pos_bias_v):
        import jax, jax.numpy as jnp
        import numpy as np
        B, T, D, H = (8, 256, 128, 8)
        DK = D // H

        def layer_norm(x, g, b, eps=1e-05):
            mu = jnp.mean(x, axis=-1, keepdims=True)
            var = jnp.var(x, axis=-1, keepdims=True)
            return (x - mu) * jax.lax.rsqrt(var + eps) * g + b

        def rel_shift(x):
            b, h, t1, t2 = x.shape
            xp = jnp.pad(x, ((0, 0), (0, 0), (0, 0), (1, 0)))
            xp = xp.reshape(b, h, t2 + 1, t1)[:, :, 1:, :]
            return xp.reshape(b, h, t1, t2)
        b, t, d = inputs.shape
        pos_seq = inputs[0, :, 0]
        inv_freq = 1.0 / 10000.0 ** (jnp.arange(0, d, 2, dtype=jnp.float32) / d)
        sin_inp = pos_seq[:, None] * inv_freq[None, :]
        pos_emb = jnp.concatenate([jnp.sin(sin_inp), jnp.cos(sin_inp)], axis=-1)
        x = layer_norm(inputs, ln1_g, ln1_b)
        xn = layer_norm(x, ln2_g, ln2_b)
        qkv = xn @ W_qkv.T
        q, k, v = jnp.split(qkv, 3, axis=-1)
        q = q.reshape(b, t, H, DK)
        k = k.reshape(b, t, H, DK).transpose(0, 2, 1, 3)
        v = v.reshape(b, t, H, DK).transpose(0, 2, 1, 3)
        p = (pos_emb @ W_pos.T).reshape(t, H, DK)
        qu = (q + pos_bias_u).transpose(0, 2, 1, 3)
        qv = (q + pos_bias_v).transpose(0, 2, 1, 3)
        ac = jnp.einsum('bhqd,bhkd->bhqk', qu, k)
        bd = jnp.einsum('bhqd,khd->bhqk', qv, p)
        bd = rel_shift(bd)
        scores = (ac + bd) / jnp.sqrt(jnp.float32(DK))
        attn = jax.nn.softmax(scores, axis=-1)
        out = jnp.einsum('bhqk,bhkd->bqhd', attn, v).reshape(b, t, d)
        return out @ W_out.T + b_out

    def _L0_ffn_ref(x, ln_g, ln_b, attn_w, attn_b, gate_w, fc1_w, fc1_b, fc2_w, fc2_b, next_w, next_b):
        import jax, jax.numpy as jnp
        import numpy as np
        MICRO_BATCHES = 2
        TOP_K = 2
        D = 128
        E = 8
        B, S = (8, 2048)
        b, s, d = x.shape
        xf = x.reshape(b * s, d)
        mu = jnp.mean(xf, axis=-1, keepdims=True)
        var = jnp.var(xf, axis=-1, keepdims=True)
        normed = (xf - mu) / jnp.sqrt(var + 1e-05) * ln_g + ln_b
        x_attn = normed @ attn_w.T + attn_b + xf
        logits = x_attn @ gate_w.T
        _scores, _indices = jax.lax.top_k(logits, TOP_K)
        e = fc1_w.shape[0]
        t = b * s // (MICRO_BATCHES * e)
        tok = x_attn.reshape(MICRO_BATCHES, e, t, d)
        h = jnp.einsum('meti,ehi->meth', tok, fc1_w) + fc1_b[None, :, None, :]
        h = jax.nn.gelu(h, approximate=False)
        y = jnp.einsum('meth,edh->metd', h, fc2_w) + fc2_b[None, :, None, :]
        yf = y.reshape(b * s, d)
        out = jax.nn.gelu(yf @ next_w.T + next_b, approximate=False)
        return out.reshape(b, s, d)
    h = _L0_tok_ref(x, itok_BS_0_21, L0_tok_W_embed, L0_tok_W_proj, L0_tok_b_proj, L0_tok_W_gap, L0_tok_b_gap)
    h = h + _L0_attn_ref(_layernorm(h, axis=-1), L0_attn_ln1_g, L0_attn_ln1_b, L0_attn_ln2_g, L0_attn_ln2_b, L0_attn_W_qkv, L0_attn_W_pos, L0_attn_W_out, L0_attn_b_out, L0_attn_pos_bias_u, L0_attn_pos_bias_v)
    h = h + _L0_ffn_ref(_layernorm(h, axis=-1), L0_ffn_ln_g, L0_ffn_ln_b, L0_ffn_attn_w, L0_ffn_attn_b, L0_ffn_gate_w, L0_ffn_fc1_w, L0_ffn_fc1_b, L0_ffn_fc2_w, L0_ffn_fc2_b, L0_ffn_next_w, L0_ffn_next_b)
    return h

_drawn_inputs = setup_inputs


def setup_inputs(seed=0):
    import zlib

    import numpy as np

    out = dict(_drawn_inputs(seed))
    spreads = {'L0_attn_ln1_g': (1.0, 0.6),
     'L0_attn_ln1_b': (0.0, 0.1),
     'L0_attn_ln2_g': (1.0, 0.6),
     'L0_attn_ln2_b': (0.0, 0.1),
     'L0_attn_b_out': (0.0, 0.1),
     'L0_ffn_ln_g': (1.0, 0.6),
     'L0_ffn_ln_b': (0.0, 0.8),
     'L0_ffn_attn_b': (0.0, 0.8),
     'L0_ffn_fc1_b': (0.0, 0.357),
     'L0_ffn_fc2_b': (0.0, 0.1),
     'L0_ffn_next_b': (0.0, 0.1)}
    factors = {'L0_tok_b_proj': 8.0,
     'L0_tok_W_gap': 27.372,
     'L0_attn_W_pos': 64.0,
     'L0_attn_pos_bias_u': 57.208,
     'L0_attn_pos_bias_v': 64.0,
     'L0_ffn_attn_w': 4.742}
    for name, (base, spread) in spreads.items():
        noise = np.random.default_rng([zlib.crc32(name.encode()), seed]).standard_normal(out[name].shape)
        drawn = base * np.exp(spread * noise) if base else spread * noise
        out[name] = jnp.asarray(drawn.astype(out[name].dtype))
    for name, factor in factors.items():
        out[name] = (out[name] * factor).astype(out[name].dtype)
    return out
```

```python
import numpy as np

B = 128
N = 128
M = 128
D = 128
V = 22
NEG = -1.0e8
ROWS = 8
NBLK = N // ROWS
CB = 8
NCH = B // CB
KKW = 2 * M + 1
HEADS = 8
DK = D // HEADS
GB = 8
NG = B // GB
FQ = 8
TWO_PI = 2 * np.pi
TWO_PI_HI = float(np.float32(6.28125))
TWO_PI_LO = TWO_PI - TWO_PI_HI
HALF_PI = np.pi / 2
PI_IN = 3.1415925
ROUND = 1.5 * 2 ** 23
EXPERTS = 8
FF = 4 * D
FC = FF // 128
NORM_STEPS = 5
PER_GROUP = 16 + GB + GB + 7


def build(nc, t, out):
    import concourse.bass as bass
    from concourse import mybir
    from contextlib import ExitStack

    f32, bf16, i32 = mybir.dt.float32, mybir.dt.bfloat16, mybir.dt.int32
    ALU, ACT, AX = mybir.AluOpType, mybir.ActivationFunctionType, mybir.AxisListType
    ds = bass.ds

    kk_dram = nc.dram_tensor("kk_dram", (NBLK, B, ROWS * KKW), f32).ap()
    h_dram = nc.dram_tensor("h_dram", (B, N, M), f32).ap()
    h2_dram = nc.dram_tensor("h2_dram", (NG, N, GB * D), f32).ap()
    TR = {"is_transpose": True}

    def view(ap, extra, dims):
        return bass.AP(ap.tensor, ap.offset + extra, [list(ap.ap[0])] + [list(d) for d in dims])

    def backwards(ap):
        dims = [list(q) for q in ap.ap]
        step, count = dims[-1]
        dims[-1] = [-step, count]
        return bass.AP(ap.tensor, ap.offset + step * (count - 1), dims)

    def pairs(eng, count, body, until=None):
        body(0, 0)
        body(1, 1)
        with eng.Fori(1, count // 2) as it:
            body(it * 2, 0)
            body(it * 2 + 1, 1)

    def reused(k):
        return not isinstance(k, int) or k >= 2

    with ExitStack() as ctx:
        def sb(name, shape, dt=f32):
            return ctx.enter_context(nc.sbuf_tensor(name, shape, dt))

        def sem(name):
            return ctx.enter_context(nc.semaphore(name))

        psum = [ctx.enter_context(nc.psum_tensor(f"bank{i}", [128, 1024], f32)) for i in range(4)]

        ident = sb("ident", [128, 128])

        with ExitStack() as p1:
            def sb1(name, shape, dt=f32):
                return p1.enter_context(nc.sbuf_tensor(name, shape, dt))

            big_a = sb1("big_a", [128, N * B])
            big_b = sb1("big_b", [128, N * M])
            embT = sb1("embT", [D, V])
            wproj = sb1("wproj", [D, D])
            bproj = sb1("bproj", [D, 1])
            wgap = sb1("wgap", [D, 2])
            bgap = sb1("bgap", [128, 1])
            iota = sb1("iota", [3 * V, 1])
            toknat = sb1("toknat", [128, 2, 128], i32)
            tokf = sb1("tokf", [128, 2, 128])
            hit = sb1("hit", [128, 128])
            counts = sb1("counts", [128, 2, V])
            ZT = sb1("ZT", [D, V])
            wgapw = sb1("wgapw", [D, 2, 128])
            G3 = sb1("G3", [V, 3 * V], bf16)
            Gr = sb1("Gr", [V, 2, V])
            Asum = sb1("Asum", [128, 2 * V])
            Acol = sb1("Acol", [128, 4])
            neg2A = sb1("neg2A", [128, 1])
            n2first = sb1("n2first", [128, 1])
            tokx = [big_b[0:V, s * CB * N:(s + 1) * CB * N].bitcast(i32) for s in range(2)]
            toky = [big_b[0:3 * V, (2 + s) * CB * M:(3 + s) * CB * M].bitcast(i32) for s in range(2)]
            ox = [big_b[0:V, (8 + s) * CB * N // 2:(9 + s) * CB * N // 2].bitcast(bf16) for s in range(2)]
            oy = [big_b[0:3 * V, (10 + s) * CB * M // 2:(11 + s) * CB * M // 2].bitcast(bf16) for s in range(2)]
            gx = [big_b[0:3 * V, (12 + s) * CB * N // 2:(13 + s) * CB * N // 2].bitcast(bf16) for s in range(2)]
            stage = [sb1(f"stage{s}", [128, ROWS, B]) for s in range(2)]
            Tb = [sb1(f"Tb{s}", [128, ROWS, M]) for s in range(2)]
            P = sb1("P", [128, ROWS + 1, M + 1])
            u = sb1("u", [128, M])
            u2 = sb1("u2", [128, M])
            Wb = sb1("Wb", [128, ROWS, M])
            KK = [sb1(f"KK{s}", [128, ROWS, KKW]) for s in range(2)]
            KL = [sb1(f"KL{s}", [128, ROWS * M + 8]) for s in range(2)]
            Mb = [sb1(f"Mb{s}", [128, ROWS, M]) for s in range(2)]
            prod = sb1("prod", [128, KKW + 7])
            ssum = sb1("ssum", [128, M])
            lnM = sb1("lnM", [128, M])
            carry = sb1("carry", [128, M])
            rec = sb1("rec", [128, M])
            Bb = [sb1(f"Bb{s}", [128, ROWS, M + 1]) for s in range(2)]
            Gb = Tb

            s_const = sem("s_const")
            s_tokn = sem("s_tokn")
            s_tok = [sem(f"s_tok{s}") for s in range(2)]
            s_pre_pe = sem("s_pre_pe")
            s_pre_act = sem("s_pre_act")
            s_pre_v = sem("s_pre_v")
            s_oneh = sem("s_oneh")
            s_gx = sem("s_gx")
            s_gxs = sem("s_gxs")
            s_th = sem("s_th")
            s_ths = sem("s_ths")
            s_stage = sem("s_stage")
            s_tr = sem("s_tr")
            s_T = sem("s_T")
            s_v = sem("s_v")
            s_W = sem("s_W")
            s_raw = sem("s_raw")
            s_exp = sem("s_exp")
            s_mrow = sem("s_mrow")
            s_ln = sem("s_ln")
            s_spill = [sem(f"s_spill{s}") for s in range(2)]
            s_load = [sem(f"s_load{s}") for s in range(2)]
            s_b = sem("s_b")
            s_g = sem("s_g")
            s_h = [sem(f"s_h{s}") for s in range(2)]
            s_carry = sem("s_carry")

            T2 = big_a[:, :].rearrange("p (i b) -> p i b", b=B)

            NCONST = 7

            with nc.Block() as block:
                @block.sync
                def _(sp):
                    for dst, src in ((ident, t["ident"]), (embT, t["embT"]), (wproj, t["wproj"]), (bproj, t["bproj"]),
                                     (wgap, t["wgap"]), (iota, t["iota"])):
                        sp.dma_start(dst[:, :], src).then_inc(s_const, 16)
                    sp.dma_start(bgap[:, :], t["bgap"].partition_broadcast(128)).then_inc(s_const, 16)
                    sp.dma_start(toknat[:, 0, :], t["x"]).then_inc(s_tokn, 16)
                    sp.dma_start(toknat[:, 1, :], t["y"]).then_inc(s_tokn, 16)
                    xf = t["x"].rearrange("b i -> (b i)")
                    yf = t["y"].rearrange("b i -> (b i)")

                    def tokens(c, s):
                        if reused(c):
                            sp.wait_ge(s_oneh, c * 2 - 2)
                        sp.dma_start(tokx[s], xf[ds(c * (CB * N), CB * N)].partition_broadcast(V)).then_inc(s_tok[s], 16)
                        sp.dma_start(toky[s], yf[ds(c * (CB * M), CB * M)].partition_broadcast(3 * V)).then_inc(s_tok[s], 16)

                    pairs(sp, NCH, tokens)

                    def put_away(k, s):
                        sp.wait_ge(s_mrow, k + 1)
                        sp.dma_start(kk_dram[ds(k, 1), :, :].rearrange("k p n -> (k p) n"),
                                     KK[s][:, :, :].rearrange("p r n -> p (r n)")).then_inc(s_spill[s], 16)
                        sp.dma_start(big_a[:, ds(k * (ROWS * M), ROWS * M)], KL[s][:, 0:ROWS * M]).then_inc(s_spill[s], 16)
                        sp.dma_start(big_b[:, ds(k * (ROWS * M), ROWS * M)],
                                     Mb[s][:, :, :].rearrange("p r n -> p (r n)")).then_inc(s_spill[s], 16)

                    pairs(sp, NBLK, put_away)
                    sp.wait_ge(s_spill[0], 48 * NBLK // 2)
                    sp.wait_ge(s_spill[1], 48 * NBLK // 2)
                    sp.wait_ge(s_ln, NBLK)

                    def bring_back(n, s):
                        if reused(n):
                            sp.wait_ge(s_g, n - 1)
                            sp.dma_start(h_dram[:, ds(n * -ROWS + (NBLK + 1) * ROWS, ROWS), :], Gb[s][:, :, :]).then_inc(s_h[s], 16)
                            sp.wait_ge(s_carry, n - 1)
                        k = n * -1 + (NBLK - 1)
                        sp.dma_start(KK[s][:, :, :].rearrange("p r n -> p (r n)"),
                                     kk_dram[ds(k, 1), :, :].rearrange("k p n -> (k p) n")).then_inc(s_load[s], 16)
                        sp.dma_start(KL[s][:, 0:ROWS * M], big_a[:, ds(k * (ROWS * M), ROWS * M)]).then_inc(s_load[s], 16)
                        sp.dma_start(Mb[s][:, :, :].rearrange("p r n -> p (r n)"),
                                     big_b[:, ds(k * (ROWS * M), ROWS * M)]).then_inc(s_load[s], 16)

                    pairs(sp, NBLK, bring_back)
                    for s in range(2):
                        sp.wait_ge(s_g, NBLK - 1 + s)
                        sp.dma_start(h_dram[:, (1 - s) * ROWS:(2 - s) * ROWS, :], Gb[s][:, :, :]).then_inc(s_h[s], 16)
                    sp.wait_ge(s_h[0], 16 * NBLK // 2)
                    sp.wait_ge(s_h[1], 16 * NBLK // 2)

                @block.tensor
                def _(pe):
                    pe.wait_ge(s_const, 16 * NCONST)
                    pe.matmul(psum[0][:, 0:V], wproj[:, :], embT[:, :], start=True, stop=True).then_inc(s_pre_pe, 1)
                    pe.wait_ge(s_pre_act, 1)
                    pe.matmul(psum[1][0:V, 0:V], ZT[:, :], ZT[:, :], start=True, stop=True).then_inc(s_pre_pe, 1)
                    pe.wait_ge(s_pre_v, 1)
                    pe.matmul(psum[2][:, 0:V], wgapw[:, 0, :], ZT[:, :], start=True, stop=True)
                    pe.matmul(psum[2][:, 512:512 + V], wgapw[:, 1, :], ZT[:, :], start=True, stop=True).then_inc(s_pre_pe, 1)
                    pe.wait_ge(s_pre_v, 2)

                    def scores(c, s):
                        pe.wait_ge(s_oneh, c * 2 + 2)
                        for half in range(2):
                            last = pe.matmul(psum[0][0:3 * V, half * 512:(half + 1) * 512], G3[:, :],
                                             ox[s][:, half * 512:(half + 1) * 512], start=True, stop=True)
                        last.then_inc(s_gx, 1)
                        pe.wait_ge(s_gxs, c + 1)
                        if reused(c):
                            pe.wait_ge(s_ths, c - 1)
                        for b in range(CB):
                            last = pe.matmul(psum[2 + s][:, b * N:(b + 1) * N], oy[s][:, b * M:(b + 1) * M],
                                             gx[s][:, b * N:(b + 1) * N], start=True, stop=True)
                        last.then_inc(s_th, 1)

                    pairs(pe, NCH, scores)

                    def turn(k, s):
                        pe.wait_ge(s_stage, k + 1)
                        for r in range(ROWS):
                            last = pe.transpose(psum[s][:, r * M:(r + 1) * M], stage[s][:, r, :], ident[:, :])
                        last.then_inc(s_tr, 1)

                    pairs(pe, NBLK, turn)

                @block.gpsimd
                def _(pool):
                    pool.wait_ge(s_ths, NCH)

                    def stage_rows(k, s):
                        if reused(k):
                            pool.wait_ge(s_T, k - 1)
                        pool.tensor_copy(stage[s][:, :, :].rearrange("p r b -> p (r b)"),
                                         big_a[:, ds(k * (ROWS * B), ROWS * B)]).then_inc(s_stage, 1)

                    pairs(pool, NBLK, stage_rows)

                    def gradient(n, s):
                        pool.wait_ge(s_b, n + 1)
                        if reused(n):
                            pool.wait_ge(s_h[s], 8 * n - 8 * s)
                        pool.tensor_tensor(Gb[s][:, :, :], Mb[s][:, :, :], Bb[s][:, :, 0:M], ALU.mult).then_inc(s_g, 1)

                    pairs(pool, NBLK, gradient)

                @block.scalar
                def _(act):
                    act.preload_act_table_set("natural_log_exp_and_others")
                    act.wait_ge(s_pre_pe, 1)
                    act.activation(ZT[:, :], psum[0][:, 0:V], ACT.Identity, bias=bproj[:, 0:1]).then_inc(s_pre_act, 1)

                    def scores(c, s):
                        act.wait_ge(s_gx, c + 1)
                        if reused(c):
                            act.wait_ge(s_th, c - 1)
                        act.activation(gx[s], psum[0][0:3 * V, :], ACT.Copy).then_inc(s_gxs, 1)
                        act.wait_ge(s_th, c + 1)
                        act.activation(view(big_a[:, ds(c * CB, CB)], 0, [[B, N], [1, CB]]),
                                       psum[2 + s][:, :].rearrange("p (b i) -> p i b", b=CB), ACT.Copy).then_inc(s_ths, 1)

                    pairs(act, NCH, scores)

                    def theta(k, s):
                        act.wait_ge(s_tr, k + 1)
                        act.wait_ge(s_W, k - 1)
                        act.activation(Tb[s][:, :, :], psum[s][:, :].rearrange("p (r j) -> p r j", r=ROWS), ACT.Copy).then_inc(s_T, 1)

                    def coefficients(k, s):
                        act.wait_ge(s_raw, k * 3 + 1)
                        act.activation(KK[s][:, 0, M + 1:2 * M], KK[s][:, 0, M + 1:2 * M], ACT.Exp, bias=n2first[:, 0:1])
                        act.activation(KK[s][:, 1:ROWS, M + 1:2 * M], KK[s][:, 1:ROWS, M + 1:2 * M], ACT.Exp,
                                       bias=neg2A[:, 0:1]).then_inc(s_exp, 1)
                        act.wait_ge(s_raw, k * 3 + 2)
                        act.activation(KK[s][:, :, 0:M], KK[s][:, :, 0:M], ACT.Exp).then_inc(s_exp, 1)
                        act.wait_ge(s_raw, k * 3 + 3)
                        act.activation(KL[s][:, 0:ROWS * M], KL[s][:, 0:ROWS * M], ACT.Exp).then_inc(s_exp, 1)

                    def logarithm(k, s):
                        act.wait_ge(s_mrow, k + 1)
                        act.activation(lnM[:, :], Mb[s][:, ROWS - 1, :], ACT.Ln).then_inc(s_ln, 1)

                    def theta_first(k, s):
                        act.wait_ge(s_tr, k + 1)
                        act.activation(Tb[s][:, :, :], psum[s][:, :].rearrange("p (r j) -> p r j", r=ROWS), ACT.Copy).then_inc(s_T, 1)

                    theta_first(0, 0)
                    coefficients(0, 0)
                    theta_first(1, 1)
                    logarithm(0, 0)
                    with act.Fori(0, NBLK // 2 - 1) as it:
                        for k, s in ((it * 2 + 1, 1), (it * 2 + 2, 0)):
                            coefficients(k, s)
                            theta(k + 1, 1 - s)
                            logarithm(k, s)
                    coefficients(NBLK - 1, 1)
                    logarithm(NBLK - 1, 1)

                @block.vector
                def _(v):
                    n = [0]
                    base = [0]

                    def link(ins):
                        n[0] += 1
                        ins.then_inc(s_v, 1)
                        v.wait_ge(s_v, base[0] + n[0])

                    link(v.memset(P[:, :, :], NEG))
                    link(v.memset(P[:, 0, 1:2], 0.0))
                    link(v.memset(n2first[:, :], NEG))
                    for s in range(2):
                        link(v.memset(KK[s][:, :, :], 0.0))
                        link(v.memset(KL[s][:, ROWS * M:], 0.0))
                        link(v.memset(Bb[s][:, :, :], 0.0))
                    link(v.memset(prod[:, :], 0.0))
                    link(v.memset(carry[:, :], 0.0))
                    link(v.memset(carry[:, M - 1:M], 1.0))
                    v.wait_ge(s_const, 16 * NCONST)
                    v.tensor_copy(wgapw[:, :, :], wgap[:, :].unsqueeze(2).to_broadcast([D, 2, 128])).then_inc(s_pre_v, 1)
                    v.wait_ge(s_tokn, 32)
                    link(v.tensor_copy(tokf[:, :, :], toknat[:, :, :]))
                    for z in range(2):
                        for a in range(V):
                            link(v.tensor_scalar(hit[:, :], tokf[:, z, :], float(a), None, ALU.is_equal, ALU.add,
                                                 accum_out=counts[:, z, a:a + 1]))
                    v.wait_ge(s_pre_pe, 2)
                    g_ps = psum[1][0:V, 0:V]
                    link(v.tensor_copy(G3[:, 0:V], g_ps))
                    link(v.tensor_tensor(Gr[:, 0, :], g_ps, G3[:, 0:V], ALU.subtract))
                    link(v.tensor_copy(G3[:, V:2 * V], Gr[:, 0, :]))
                    link(v.tensor_tensor(Gr[:, 1, :], Gr[:, 0, :], G3[:, V:2 * V], ALU.subtract))
                    link(v.tensor_copy(G3[:, 2 * V:3 * V], Gr[:, 1, :]))
                    v.wait_ge(s_pre_pe, 3)
                    for z in range(2):
                        link(v.tensor_tensor(Asum[:, z * V:(z + 1) * V], psum[2][:, z * 512:z * 512 + V], counts[:, z, :], ALU.mult))
                    link(v.tensor_reduce(Acol[:, 0:1], Asum[:, :], AX.X, ALU.add))
                    link(v.tensor_scalar(Acol[:, 1:2], Acol[:, 0:1], 1.0 / N, bgap[:, 0:1], ALU.mult, ALU.add))
                    link(v.tensor_scalar(neg2A[:, :], Acol[:, 1:2], -2.0, None, ALU.mult))
                    v.nop().then_inc(s_pre_v, 1)

                    def one_hot(c, s):
                        v.wait_ge(s_tok[s], c * 16 + (32 - 16 * s))
                        if reused(c):
                            v.wait_ge(s_th, c - 1)
                        v.tensor_scalar(ox[s], tokx[s], iota[0:V, 0:1], None, ALU.is_equal).then_inc(s_oneh, 1)
                        v.tensor_scalar(oy[s], toky[s], iota[:, 0:1], None, ALU.is_equal).then_inc(s_oneh, 1)

                    pairs(v, NCH, one_hot)

                    pre = n[0]
                    PER = 3 * ROWS + 1 + (3 * ROWS - 1) + 2
                    def forward(k, s):
                        n[0] = 0
                        base[0] = k * PER + pre
                        v.wait_ge(s_T, k + 1)
                        for r in range(ROWS):
                            link(v.scalar_tensor_tensor(u[:, :], P[:, r, 0:M], (n2first if r == 0 else neg2A)[:, 0:1],
                                                        P[:, r, 1:M + 1], ALU.add, ALU.max))
                            link(v.tensor_tensor(u2[:, :], u[:, :], Tb[s][:, r, :], ALU.add))
                            link(v.tensor_tensor_scan(P[:, r + 1, 1:M + 1], Tb[s][:, r, :], u2[:, :], NEG, ALU.add, ALU.max))
                        link(v.tensor_tensor(Wb[:, :, :], Tb[s][:, :, :], P[:, 1:, 1:], ALU.subtract))
                        if reused(k):
                            v.wait_ge(s_spill[s], k * 24 - 24 * s)
                        v.tensor_tensor(KK[s][:, :, M + 1:2 * M], Wb[:, :, 1:M], P[:, 0:ROWS, 1:M], ALU.add).then_inc(s_raw, 1)
                        v.tensor_tensor(KK[s][:, :, 0:M], Wb[:, :, :], P[:, 0:ROWS, 1:], ALU.add).then_inc(s_raw, 1)
                        v.tensor_tensor(KL[s][:, 0:ROWS * M].rearrange("p (r n) -> p r n", r=ROWS), Wb[:, :, :],
                                        P[:, 1:, 0:M], ALU.add).then_inc(s_raw, 1)
                        v.nop().then_inc(s_W, 1)
                        v.wait_ge(s_exp, k * 3 + 2)
                        for r in range(ROWS):
                            if r == 0:
                                src = KK[s][:, 0, :]
                            else:
                                link(v.tensor_tensor(view(prod[:, :], 0, [[M + 1, 2], [1, M]]),
                                                     view(KK[s][:, r, :], 0, [[M + 1, 2], [1, M]]),
                                                     Mb[s][:, r - 1:r, :].to_broadcast([128, 2, M]), ALU.mult))
                                src = prod[:, :]
                            link(v.tensor_tensor(ssum[:, :], src[:, 0:M], src[:, M:2 * M], ALU.add))
                            if r == 0:
                                v.wait_ge(s_exp, k * 3 + 3)
                            link(v.tensor_tensor_scan(Mb[s][:, r, :], KL[s][:, r * M:(r + 1) * M], ssum[:, :], 0.0,
                                                      ALU.mult, ALU.add))
                        v.nop().then_inc(s_mrow, 1)
                        link(v.tensor_copy(n2first[:, :], neg2A[:, :]))
                        v.wait_ge(s_ln, k + 1)
                        link(v.tensor_tensor(P[:, 0, 1:], P[:, ROWS, 1:], lnM[:, :], ALU.add))
                        assert n[0] == PER, (n[0], PER)

                    pairs(v, NBLK, forward)
                    pre2 = pre + PER * NBLK
                    PER2 = 2 + 3 * ROWS

                    def backward(k, s):
                        n[0] = 0
                        base[0] = k * PER2 + pre2
                        v.wait_ge(s_load[s], k * 24 + (48 - 24 * s))
                        link(v.reciprocal(rec[:, :], Mb[s][:, ROWS - 1, :]))
                        link(v.tensor_tensor(ssum[:, :], carry[:, :], rec[:, :], ALU.mult))
                        for r in range(ROWS - 1, -1, -1):
                            link(v.tensor_tensor_scan(backwards(Bb[s][:, r, 0:M]), backwards(KL[s][:, r * M + 1:(r + 1) * M + 1]),
                                                      backwards(ssum[:, :]), 0.0, ALU.mult, ALU.add))
                            if r == 0:
                                v.nop().then_inc(s_b, 1)
                            link(v.tensor_tensor(view(prod[:, :], 0, [[M + 1, 2], [1, M]]),
                                                 view(KK[s][:, r, :], 0, [[M + 1, 2], [1, M]]),
                                                 view(Bb[s][:, r, :], 0, [[1, 2], [1, M]]), ALU.mult))
                            link(v.tensor_tensor((ssum if r else carry)[:, :], prod[:, 0:M], prod[:, M + 1:2 * M + 1], ALU.add))
                        v.nop().then_inc(s_carry, 1)
                        assert n[0] == PER2, (n[0], PER2)

                    pairs(v, NBLK, backward)

        with ExitStack() as p2:
            def sb2(name, shape, dt=f32):
                return p2.enter_context(nc.sbuf_tensor(name, shape, dt))

            wqkvT = sb2("wqkvT", [D, 3 * D])
            wposT = sb2("wposT", [D, D])
            woutT = sb2("woutT", [D, D])
            bout = sb2("bout", [128, D])
            g1 = sb2("g1", [128, D])
            b1 = sb2("b1", [128, D])
            cols = sb2("cols", [128, 4])
            invf = sb2("invf", [128, D // 2])
            upto = sb2("upto", [128, N])
            beyond = sb2("beyond", [128, N], i32)
            PP = sb2("PP", [128, 2 * N])
            Hx = sb2("Hx", [128, GB, D])
            Hr = sb2("Hr", [128, GB, D])
            Y = sb2("Y", [128, GB, D])
            Xn = sb2("Xn", [128, GB, D])
            st = sb2("st", [128, GB, 6])
            mv = sb2("mv", [128, GB, 2])
            base_ = sb2("powbase", [128, 3, GB])
            rs = sb2("rs", [128, 3, GB])
            rr = sb2("rr", [128, 3, GB])
            mhalf = sb2("mhalf", [128, GB])
            trig = sb2("trig", [128, 5, D])
            peT = sb2("peT", [128, N])
            XT = sb2("XT", [D, GB * N])
            QU = sb2("QU", [D, GB * N])
            QV = sb2("QV", [D, N * GB])
            KT = sb2("KT", [D, GB * N])
            Vb = sb2("Vb", [128, GB, HEADS, DK + 1])
            QVm = sb2("QVm", [D, HEADS, N * GB])
            KTm = sb2("KTm", [D, HEADS, GB * N])
            BD = sb2("BD", [128, HEADS * GB, N + 1])
            nm = sb2("nm", [128, 2, HEADS])
            idle = sb2("idle", [128, 1])
            mx = sb2("mx", [128, 2, HEADS])
            E = [sb2(f"E{s}", [128, HEADS, N]) for s in range(2)]
            PT = [sb2(f"PT{s}", [128, HEADS, N]) for s in range(2)]
            rd = sb2("rd", [128, HEADS])
            On = sb2("On", [128, GB, D])
            OT = sb2("OT", [D, GB * N])

            s_c2 = sem("s_c2")
            s_hx = sem("s_hx")
            s_hr = sem("s_hr")
            s_v2 = sem("s_v2")
            s_powin = sem("s_powin")
            s_pow = sem("s_pow")
            s_y0 = sem("s_y0")
            s_y = sem("s_y")
            s_xn = sem("s_xn")
            s_xtp = sem("s_xtp")
            s_xt = sem("s_xt")
            s_v2w = sem("s_v2w")
            s_pos = sem("s_pos")
            s_posact = sem("s_posact")
            s_pospe = sem("s_pospe")
            s_qkv = sem("s_qkv")
            s_quk = sem("s_quk")
            s_qvv = sem("s_qvv")
            s_mq = sem("s_mq")
            s_mk = sem("s_mk")
            s_f = sem("s_f")
            s_fd = sem("s_fd")
            s_s = sem("s_s")
            s_m = sem("s_m")
            s_e = sem("s_e")
            s_pt = sem("s_pt")
            s_pe = sem("s_pe")
            s_o = sem("s_o")
            s_n = sem("s_n")
            s_ot = sem("s_ot")
            s_ots = sem("s_ots")
            s_op = sem("s_op")
            s_res = sem("s_res")
            s_h2 = sem("s_h2")
            s_h2o = sem("s_h2o")

            NC2 = 10

            def groups(eng, body):
                with eng.Fori(0, NG - 1) as g:
                    body(g, True)
                body(NG - 1, False)

            with nc.Block() as block:
                @block.sync
                def _(sp):
                    for dst, src in ((wqkvT[:, :], t["wqkvT"]), (wposT[:, :], t["wposT"]), (woutT[:, :], t["woutT"]),
                                     (cols[:, :], t["cols"]), (upto[:, :], t["upto"]), (beyond[:, :], t["beyond"]),
                                     (bout[:, :], t["b_out"].partition_broadcast(128)), (g1[:, :], t["ln1_g"].partition_broadcast(128)),
                                     (b1[:, :], t["ln1_b"].partition_broadcast(128)), (invf[:, :], t["invf"].partition_broadcast(128))):
                        sp.dma_start(dst, src).then_inc(s_c2, 16)

                    def load(dst, g, done):
                        sp.dma_start(dst[:, :, :], h_dram[ds(g * GB, GB), :, :].rearrange("b i d -> i b d")).then_inc(done, 16)

                    load(Hx, 0, s_hx)
                    load(Hr, 0, s_hr)

                    def group(g, more):
                        if more:
                            sp.wait_ge(s_y0, g + 1)
                            load(Hx, g + 1, s_hx)
                        sp.wait_ge(s_qvv, g * 2 + 1)
                        for h in range(HEADS):
                            sp.dma_start(QVm[h * DK:(h + 1) * DK, h, :], QV[h * DK:(h + 1) * DK, :]).then_inc(s_mq, 16)
                        sp.wait_ge(s_quk, g * 2 + 2)
                        for h in range(HEADS):
                            sp.dma_start(KTm[h * DK:(h + 1) * DK, h, :], KT[h * DK:(h + 1) * DK, :]).then_inc(s_mk, 16)
                        sp.wait_ge(s_h2, g + 2)
                        sp.dma_start(h2_dram[ds(g, 1), :, :].rearrange("g i n -> (g i) n"),
                                     Hr[:, :, :].rearrange("p b d -> p (b d)")).then_inc(s_h2o, 16)
                        sp.wait_ge(s_h2o, g * 16 + 16)
                        if more:
                            load(Hr, g + 1, s_hr)

                    groups(sp, group)

                @block.gpsimd
                def _(pool):
                    pool.memset(mhalf[:, :], -0.5).then_inc(s_v2w, 1)
                    pool.memset(QVm[:, :, :], 0.0).then_inc(s_v2w, 1)
                    pool.memset(KTm[:, :, :], 0.0).then_inc(s_v2w, 1)
                    pool.wait_ge(s_v2w, 3)
                    pool.wait_ge(s_c2, 16 * NC2)

                    def powers(g, c):
                        pool.wait_ge(s_powin, g * 3 + c + 1)
                        pool.tensor_tensor(rs[:, c, :], base_[:, c, :], mhalf[:, :], ALU.pow).then_inc(s_pow, 1)

                    def norm(g):
                        powers(g, 0)
                        powers(g, 1)
                        pool.wait_ge(s_y0, g + 1)
                        pool.tensor_tensor(Y[:, :, :], Y[:, :, :], g1[:, :].unsqueeze(1).to_broadcast([128, GB, D]), ALU.mult).then_inc(s_y, 1)
                        pool.wait_ge(s_y, g * 2 + 1)
                        pool.tensor_tensor(Y[:, :, :], Y[:, :, :], b1[:, :].unsqueeze(1).to_broadcast([128, GB, D]), ALU.add).then_inc(s_y, 1)
                        powers(g, 2)

                    norm(0)

                    def group(g, more):
                        pool.wait_ge(s_hr, g * 16 + 16)
                        pool.tensor_tensor(Hr[:, :, :], Hr[:, :, :], bout[:, :].unsqueeze(1).to_broadcast([128, GB, D]), ALU.add).then_inc(s_res, 1)
                        if more:
                            norm(g + 1)

                    groups(pool, group)

                @block.tensor
                def _(pe):
                    pe.wait_ge(s_c2, 16 * NC2)
                    pe.wait_ge(s_posact, 1)
                    pe.transpose(psum[0][:, 0:N], trig[:, 0, :], ident[:, :]).then_inc(s_pospe, 1)
                    pe.wait_ge(s_posact, 2)
                    pe.matmul(psum[1][:, 0:N], wposT[:, :], peT[:, :], start=True, stop=True).then_inc(s_pospe, 1)
                    pe.wait_ge(s_posact, 4)
                    pe.wait_ge(s_v2w, 3)

                    def group(g, more):
                        pe.wait_ge(s_xn, g + 1)
                        for b in range(GB):
                            last = pe.transpose(psum[0][:, b * N:(b + 1) * N], Xn[:, b, :], ident[:, :])
                        last.then_inc(s_xtp, 1)
                        pe.wait_ge(s_xt, g + 1)
                        pe.wait_ge(s_h2, g + 1)
                        for z in range(2):
                            for half in range(2):
                                last = pe.matmul(psum[1 + z][:, half * 512:(half + 1) * 512], wqkvT[:, z * D:(z + 1) * D],
                                                 XT[:, half * 512:(half + 1) * 512], start=True, stop=True)
                            last.then_inc(s_qkv, 1)
                        for b in range(GB):
                            last = pe.matmul(psum[3][:, b * D:(b + 1) * D], XT[:, b * N:(b + 1) * N], wqkvT[:, 2 * D:3 * D],
                                             start=True, stop=True)
                        last.then_inc(s_qkv, 1)
                        pe.wait_ge(s_mq, g * 128 + 128)
                        for f in range(N // FQ):
                            if f >= 2:
                                pe.wait_ge(s_fd, g * (N // FQ) + f - 1)
                            for q in range(FQ):
                                i = f * FQ + q
                                last = pe.matmul(psum[0][:, (f % 2) * 512 + q * 64:(f % 2) * 512 + (q + 1) * 64],
                                                 PP[:, N - 1 - i:2 * N - 1 - i],
                                                 QVm[:, :, i * GB:(i + 1) * GB], start=True, stop=True)
                            last.then_inc(s_f, 1)
                        pe.wait_ge(s_mk, g * 128 + 128)
                        pe.wait_ge(s_quk, g * 2 + 2)
                        pe.wait_ge(s_qvv, g * 2 + 2)
                        pe.wait_ge(s_fd, g * (N // FQ) + N // FQ)

                        def scores(b):
                            if b >= 2:
                                pe.wait_ge(s_e, g * GB + b - 1)
                            tile = psum[1 + b % 2]
                            for half in range(2):
                                pe.matmul(tile[:, half * 512:(half + 1) * 512], QU[:, b * N:(b + 1) * N],
                                          KTm[:, 4 * half:4 * half + 4, b * N:(b + 1) * N], start=True, stop=False)
                                for h in range(4 * half, 4 * half + 4):
                                    last = pe.matmul(tile[:, h * N:(h + 1) * N], BD[:, h * GB + b, 1:N + 1], ident[:, :],
                                                     start=False, stop=(h % 4 == 3), **TR)
                            last.then_inc(s_s, 1)

                        def outputs(b):
                            pe.wait_ge(s_e, g * GB + b + 1)
                            for half in range(2):
                                if b or half:
                                    pe.wait_ge(s_pe, g * 16 + 2 * b + half)
                                for h in range(4):
                                    last = pe.transpose(psum[3][:, h * N:(h + 1) * N], E[b % 2][:, 4 * half + h, :], ident[:, :])
                                last.then_inc(s_pt, 1)
                            pe.wait_ge(s_pe, g * 16 + 2 * b + 2)
                            if b:
                                pe.wait_ge(s_n, g * GB + b)
                            for h in range(HEADS):
                                o = 512 + (b % 2) * 256 + h * (DK + 1)
                                last = pe.matmul(psum[3][:, o:o + DK + 1], PT[b % 2][:, h, :], Vb[:, b, h, :], start=True, stop=True)
                            last.then_inc(s_o, 1)

                        scores(0)
                        for b in range(GB):
                            if b + 1 < GB:
                                scores(b + 1)
                            outputs(b)
                        pe.wait_ge(s_n, g * GB + GB)
                        for b in range(GB):
                            last = pe.transpose(psum[0][:, b * N:(b + 1) * N], On[:, b, :], ident[:, :])
                        last.then_inc(s_ot, 1)
                        pe.wait_ge(s_ots, g + 1)
                        for b in range(GB):
                            last = pe.matmul(psum[1][:, b * D:(b + 1) * D], OT[:, b * N:(b + 1) * N], woutT[:, :], start=True, stop=True)
                        last.then_inc(s_op, 1)

                    groups(pe, group)

                @block.scalar
                def _(act):
                    act.wait_ge(s_c2, 16 * NC2)
                    act.wait_ge(s_pos, 1)
                    act.activation(trig[:, 0, :], trig[:, 4, :], ACT.Sin).then_inc(s_posact, 1)
                    act.wait_ge(s_pospe, 1)
                    act.activation(peT[:, :], psum[0][:, 0:N], ACT.Copy).then_inc(s_posact, 1)
                    act.wait_ge(s_pospe, 2)
                    act.activation(PP[:, 0:N], psum[1][:, 0:N], ACT.Copy).then_inc(s_posact, 1)
                    act.activation(PP[:, N:2 * N], psum[1][:, 0:N], ACT.Copy).then_inc(s_posact, 1)

                    def group(g, more):
                        act.wait_ge(s_xtp, g + 1)
                        act.activation(XT[:, :], psum[0][:, :], ACT.Identity, scale=cols[:, 0:1], bias=cols[:, 1:2]).then_inc(s_xt, 1)
                        act.wait_ge(s_qkv, g * 3 + 1)
                        act.activation(QU[:, :], psum[1][:, :], ACT.Identity, bias=cols[:, 2:3]).then_inc(s_quk, 1)
                        act.wait_ge(s_qkv, g * 3 + 2)
                        act.activation(KT[:, :], psum[2][:, :], ACT.Copy).then_inc(s_quk, 1)
                        for b in range(GB):
                            act.wait_ge(s_m, g * GB + b + 1)
                            if b >= 2:
                                act.wait_ge(s_pt, g * 16 + 2 * b - 2)
                            for h in range(HEADS):
                                last = act.activation(E[b % 2][:, h, :], psum[1 + b % 2][:, h * N:(h + 1) * N], ACT.Exp,
                                                      bias=nm[:, b % 2, h:h + 1], scale=DK ** -0.5)
                            last.then_inc(s_e, 1)
                            for half in range(2):
                                act.wait_ge(s_pt, g * 16 + 2 * b + half + 1)
                                if half == 0 and b >= 2:
                                    act.wait_ge(s_o, g * GB + b - 1)
                                act.activation(PT[b % 2][:, 4 * half:4 * half + 4, :],
                                               psum[3][:, 0:512].rearrange("p (h n) -> p h n", h=4), ACT.Copy).then_inc(s_pe, 1)
                        act.wait_ge(s_ot, g + 1)
                        act.activation(OT[:, :], psum[0][:, :], ACT.Copy).then_inc(s_ots, 1)

                    groups(act, group)

                @block.vector
                def _(v):
                    n, start = [0], [0]

                    def link(ins):
                        n[0] += 1
                        ins.then_inc(s_v2, 1)
                        v.wait_ge(s_v2, start[0] + n[0])

                    def moments(src):
                        for b in range(GB):
                            last = v.bn_stats(st[:, b, :], src[:, b, :])
                        link(last)
                        v.memset(idle[:, :], 0.0)
                        for b in range(GB):
                            last = v.bn_aggr(mv[:, b, :], st[:, b, :])
                        link(last)

                    def norm_1(g):
                        v.wait_ge(s_hx, g * 16 + 16)
                        moments(Hx)
                        v.tensor_scalar(base_[:, 0, :], mv[:, :, 1], 1e-5, None, ALU.add).then_inc(s_powin, 1)

                    def norm_2(g):
                        v.wait_ge(s_pow, g * 3 + 1)
                        link(v.tensor_tensor(rr[:, 0, :], mv[:, :, 1], rs[:, 0, :], ALU.mult))
                        link(v.tensor_tensor(rr[:, 1, :], rr[:, 0, :], rs[:, 0, :], ALU.mult))
                        v.tensor_scalar(base_[:, 1, :], rr[:, 1, :], 1e-5, None, ALU.add).then_inc(s_powin, 1)

                    def norm_3(g):
                        v.wait_ge(s_pow, g * 3 + 2)
                        link(v.tensor_tensor(rr[:, 2, :], rs[:, 0, :], rs[:, 1, :], ALU.mult))
                        for b in range(GB):
                            last = v.tensor_scalar(Y[:, b, :], Hx[:, b, :], mv[:, b, 0:1], rr[:, 2, b:b + 1], ALU.subtract, ALU.mult)
                        last.then_inc(s_y0, 1)

                    def norm_4(g):
                        v.wait_ge(s_y, g * 2 + 2)
                        moments(Y)
                        v.tensor_scalar(base_[:, 2, :], mv[:, :, 1], 1e-5, None, ALU.add).then_inc(s_powin, 1)

                    def norm_5(g):
                        v.wait_ge(s_pow, g * 3 + 3)
                        for b in range(GB):
                            last = v.tensor_scalar(Xn[:, b, :], Y[:, b, :], mv[:, b, 0:1], rs[:, 2, b:b + 1], ALU.subtract, ALU.mult)
                        last.then_inc(s_xn, 1)

                    v.wait_ge(s_c2, 16 * NC2)
                    link(v.memset(Vb[:, :, :, :], 1.0))
                    link(v.memset(BD[:, :, :], 0.0))
                    v.nop().then_inc(s_h2, 1)
                    norm_1(0)
                    norm_2(0)
                    link(v.tensor_scalar(rr[:, 2, 0:1], Hx[:, 0, 0:1], mv[:, 0, 0:1], rs[:, 0, 0:1], ALU.subtract, ALU.mult))
                    H2 = D // 2
                    x_, k_ = trig[:, 1, 0:H2], trig[:, 2, 0:H2]
                    a_ = trig[:, 3, 0:H2]
                    sin_, cos_ = trig[:, 4, 0:H2], trig[:, 4, H2:D]
                    link(v.tensor_scalar(x_, invf[:, :], rr[:, 2, 0:1], None, ALU.mult))
                    link(v.tensor_scalar(k_, x_, 1.0 / TWO_PI, ROUND, ALU.mult, ALU.add))
                    link(v.tensor_scalar(k_, k_, ROUND, None, ALU.subtract))
                    link(v.scalar_tensor_tensor(a_, k_, -TWO_PI_HI, x_, ALU.mult, ALU.add))
                    link(v.scalar_tensor_tensor(a_, k_, -TWO_PI_LO, a_, ALU.mult, ALU.add))
                    link(v.tensor_scalar(sin_, a_, PI_IN, -PI_IN, ALU.min, ALU.max))
                    link(v.tensor_scalar(x_, a_, HALF_PI, None, ALU.add))
                    link(v.tensor_scalar(k_, x_, PI_IN, -TWO_PI, ALU.is_gt, ALU.mult))
                    link(v.tensor_tensor(x_, x_, k_, ALU.add))
                    link(v.tensor_scalar(cos_, x_, PI_IN, -PI_IN, ALU.min, ALU.max))
                    v.nop().then_inc(s_pos, 1)
                    norm_3(0)
                    norm_4(0)
                    norm_5(0)
                    pre = n[0]
                    PER = [None]

                    def group(g, more):
                        n[0] = 0
                        start[0] = g * PER_GROUP + pre
                        v.wait_ge(s_quk, g * 2 + 1)
                        v.tensor_scalar(QV[:, :].rearrange("p (i b) -> p b i", b=GB), psum[1][:, :].rearrange("p (b i) -> p b i", b=GB),
                                        cols[:, 3:4], None, ALU.add).then_inc(s_qvv, 1)
                        v.wait_ge(s_qkv, g * 3 + 3)
                        v.tensor_copy(Vb[:, :, :, 0:DK].rearrange("p b h e -> p (b h) e"),
                                      psum[3][:, :].rearrange("p (n e) -> p n e", e=DK)).then_inc(s_qvv, 1)

                        def position(f):
                            return psum[0][:, (f % 2) * 512:(f % 2) * 512 + 512].rearrange("p (i n) -> p i n", i=FQ)

                        for f in range(N // FQ):
                            if f:
                                v.wait_ge(s_fd, g * (N // FQ) + f)
                            v.wait_ge(s_f, g * (N // FQ) + f + 1)
                            link(v.tensor_tensor(BD[:, :, 1 + f * FQ:1 + (f + 1) * FQ].rearrange("p n i -> p i n"), position(f),
                                                 upto[:, f * FQ:(f + 1) * FQ].unsqueeze(2).to_broadcast([128, FQ, 64]), ALU.mult))
                            v.memset(idle[:, :], 0.0)
                            v.copy_predicated(BD[:, :, f * FQ:(f + 1) * FQ].rearrange("p n i -> p i n"),
                                              beyond[:, f * FQ:(f + 1) * FQ].unsqueeze(2).to_broadcast([128, FQ, 64]),
                                              position(f)).then_inc(s_fd, 1)

                        def maxima(b):
                            v.wait_ge(s_s, g * GB + b + 1)
                            link(v.tensor_reduce(mx[:, b % 2, :], psum[1 + b % 2][:, :].rearrange("p (h k) -> p h k", h=HEADS), AX.X, ALU.max))
                            if b >= 2:
                                v.wait_ge(s_e, g * GB + b - 1)
                            v.tensor_scalar(nm[:, b % 2, :], mx[:, b % 2, :], -DK ** -0.5, None, ALU.mult).then_inc(s_m, 1)

                        def divide(b):
                            v.wait_ge(s_o, g * GB + b + 1)
                            o = 512 + (b % 2) * 256
                            sums = psum[3][:, o:o + HEADS * (DK + 1)].rearrange("p (h e) -> p h e", h=HEADS)
                            link(v.reciprocal(rd[:, :], sums[:, :, DK]))
                            v.tensor_tensor(On[:, b, :].rearrange("p (h e) -> p h e", h=HEADS), sums[:, :, 0:DK],
                                            rd[:, :].unsqueeze(2).to_broadcast([128, HEADS, DK]), ALU.mult).then_inc(s_n, 1)

                        maxima(0)
                        for b in range(GB):
                            if b + 1 < GB:
                                maxima(b + 1)
                            if more and b in (0, 2, 3, 6):
                                {0: norm_1, 2: norm_2, 3: norm_3, 6: norm_4}[b](g + 1)
                            divide(b)
                        if more:
                            norm_5(g + 1)
                        v.wait_ge(s_res, g + 1)
                        v.wait_ge(s_op, g + 1)
                        v.tensor_tensor(Hr[:, :, :], psum[1][:, :].rearrange("p (b d) -> p b d", b=GB), Hr[:, :, :], ALU.add).then_inc(s_h2, 1)
                        if more:
                            assert n[0] == PER_GROUP, n[0]

                    groups(v, group)



        with ExitStack() as p3:
            def sb3(name, shape, dt=f32):
                return p3.enter_context(nc.sbuf_tensor(name, shape, dt))

            attnT = sb3("attnT", [D, D])
            nextT = sb3("nextT", [D, D])
            nextb = sb3("nextb", [128, D])
            fcols = sb3("fcols", [128, 3])
            W1 = [sb3(f"W1{s}", [D, FF]) for s in range(2)]
            W2 = [sb3(f"W2{s}", [128, FC, D]) for s in range(2)]
            c1 = [sb3(f"c1{s}", [128, FC]) for s in range(2)]
            c2 = [sb3(f"c2{s}", [128, 1]) for s in range(2)]
            H3 = [sb3(f"H3{s}", [128, GB, D]) for s in range(2)]
            XF = sb3("XF", [128, GB, D])
            NN = sb3("NN", [128, GB, D])
            XFT = sb3("XFT", [D, GB * N])
            NT = sb3("NT", [D, GB * N])
            XA = [sb3(f"XA{s}", [D, GB * N]) for s in range(2)]
            HG = [sb3(f"HG{s}", [128, FC, 512]) for s in range(2)]
            YT = [sb3(f"YT{s}", [D, 512]) for s in range(2)]
            Z = [sb3(f"Z{s}", [128, 4, D]) for s in range(2)]
            st3 = sb3("st3", [128, GB, 6])
            mv3 = sb3("mv3", [128, GB, 2])
            pw3 = sb3("pw3", [128, 2, GB])
            rs3 = sb3("rs3", [128, 2, GB])
            rr3 = sb3("rr3", [128, 3, GB])
            mhalf3 = sb3("mhalf3", [128, GB])
            idle3 = sb3("idle3", [128, 1])

            s_c3 = sem("s_c3")
            s_mh = sem("s_mh")
            s_h3 = [sem(f"s_h3{s}") for s in range(2)]
            s_w = [sem(f"s_w{s}") for s in range(2)]
            s_v3 = sem("s_v3")
            s_pi3 = sem("s_pi3")
            s_po3 = sem("s_po3")
            s_nf = sem("s_nf")
            s_tp = sem("s_tp")
            s_ft = sem("s_ft")
            s_at = sem("s_at")
            s_xa = sem("s_xa")
            s_f1 = sem("s_f1")
            s_gl = sem("s_gl")
            s_y3 = sem("s_y3")
            s_yt = sem("s_yt")
            s_nx = sem("s_nx")
            s_z = sem("s_z")
            s_zg = sem("s_zg")
            s_r3 = sem("s_r3")
            s_out = [sem(f"s_out{s}") for s in range(2)]

            NC3 = 4

            def steps(eng, body):
                body(0, 0, 0, True)
                body(1, 1, 0, True)
                with eng.Fori(1, EXPERTS - 1) as e:
                    body(e * 2, 0, e, True)
                    body(e * 2 + 1, 1, e, True)
                body(NG - 2, 0, EXPERTS - 1, True)
                body(NG - 1, 1, EXPERTS - 1, False)

            out_g = out.rearrange("(g b) i d -> g i b d", b=GB)

            with nc.Block() as block:
                @block.sync
                def _(sp):
                    for dst, src in ((attnT[:, :], t["attnT"]), (nextT[:, :], t["nextT"]), (fcols[:, :], t["fcols"]),
                                     (nextb[:, :], t["next_b"].partition_broadcast(128))):
                        sp.dma_start(dst, src).then_inc(s_c3, 16)

                    def weights(e, s):
                        sp.dma_start(W1[s][:, :], t["fc1T"][ds(e, 1), :, :].rearrange("e d h -> (e d) h")).then_inc(s_w[s], 16)
                        sp.dma_start(W2[s][:, :, :], t["fc2T"][ds(e, 1), :, :, :].rearrange("e h c d -> (e h) c d")).then_inc(s_w[s], 16)
                        sp.dma_start(c1[s][:, :], t["fc1b"][ds(e, 1), :, :].rearrange("e h c -> (e h) c")).then_inc(s_w[s], 16)
                        sp.dma_start(c2[s][:, :], t["fc2b"][ds(e, 1), :, :].rearrange("e h c -> (e h) c")).then_inc(s_w[s], 16)

                    def load(e, s):
                        sp.dma_start(H3[s][:, :, :].rearrange("p b d -> p (b d)"),
                                     h2_dram[ds(e + EXPERTS * s, 1), :, :].rearrange("g i n -> (g i) n")).then_inc(s_h3[s], 16)

                    for s in range(2):
                        load(0, s)
                        weights(0, s)

                    def step(k, s, e, more):
                        again = not (isinstance(e, int) and e == EXPERTS - 1)
                        if again:
                            sp.wait_ge(s_yt, k * 2 + 2)
                            weights(e + 1, s)
                        sp.wait_ge(s_r3, k * 2 + 2)
                        sp.dma_start(out_g[ds(e + EXPERTS * s, 1), :, :, :].rearrange("g i b d -> (g i) b d"), H3[s][:, :, :]).then_inc(s_out[s], 16)
                        if again:
                            sp.wait_ge(s_out[s], e * 16 + 16)
                            load(e + 1, s)

                    steps(sp, step)
                    sp.wait_ge(s_out[0], 16 * EXPERTS)
                    sp.wait_ge(s_out[1], 16 * EXPERTS)

                @block.gpsimd
                def _(pool):
                    pool.memset(mhalf3[:, :], -0.5).then_inc(s_mh, 1)
                    pool.wait_ge(s_mh, 1)

                    def norm(k):
                        for c in range(2):
                            pool.wait_ge(s_pi3, k * 2 + c + 1)
                            pool.tensor_tensor(rs3[:, c, :], pw3[:, c, :], mhalf3[:, :], ALU.pow).then_inc(s_po3, 1)

                    norm(0)

                    def step(k, s, e, more):
                        if more:
                            norm(k + 1)
                        for half in range(2):
                            pool.wait_ge(s_zg, k * 2 + half + 1)
                            pool.tensor_tensor(H3[s][:, 4 * half:4 * half + 4, :], Z[half][:, :, :], H3[s][:, 4 * half:4 * half + 4, :],
                                               ALU.add).then_inc(s_r3, 1)

                    steps(pool, step)

                @block.tensor
                def _(pe):
                    def turn(k):
                        pe.wait_ge(s_nf, k + 1)
                        if not (isinstance(k, int) and k == 0):
                            pe.wait_ge(s_xa, k)
                        for z, src in enumerate((XF, NN)):
                            for b in range(GB):
                                last = pe.transpose(psum[z][:, b * N:(b + 1) * N], src[:, b, :], ident[:, :])
                            last.then_inc(s_tp, 1)

                    def project(k):
                        pe.wait_ge(s_ft, k * 2 + 2)
                        for half in range(2):
                            last = pe.matmul(psum[0][:, half * 512:(half + 1) * 512], attnT[:, :], NT[:, half * 512:(half + 1) * 512],
                                             start=True, stop=True)
                        last.then_inc(s_at, 1)

                    def hidden(k, s, half, c):
                        i = 4 * half + c
                        if i >= 2 or not (isinstance(k, int) and k == 0):
                            pe.wait_ge(s_gl, k * 8 + (i - 1))
                        pe.matmul(psum[3][:, (c % 2) * 512:(c % 2) * 512 + 512], W1[s][:, c * 128:(c + 1) * 128],
                                  XA[s][:, half * 512:(half + 1) * 512], start=True, stop=True).then_inc(s_f1, 1)

                    def second(k, s, half, c):
                        pe.wait_ge(s_gl, k * 8 + (4 * half + c + 1))
                        if c == 0 and (half or not (isinstance(k, int) and k == 0)):
                            pe.wait_ge(s_yt, k * 2 + half)
                        last = pe.matmul(psum[2][:, 0:512], W2[s][:, c, :], HG[half][:, c, :], start=(c == 0), stop=(c == FC - 1))
                        if c == FC - 1:
                            last.then_inc(s_y3, 1)

                    def final(k, s, half):
                        pe.wait_ge(s_yt, k * 2 + half + 1)
                        if half or not (isinstance(k, int) and k == 0):
                            pe.wait_ge(s_z, k * 2 + half)
                        for b in range(4):
                            last = pe.matmul(psum[2][:, 512 + b * D:512 + (b + 1) * D], YT[half][:, b * N:(b + 1) * N], nextT[:, :],
                                             start=True, stop=True)
                        last.then_inc(s_nx, 1)

                    pe.wait_ge(s_c3, 16 * NC3)
                    turn(0)
                    project(0)

                    def step(k, s, e, more):
                        pe.wait_ge(s_w[s], e * 64 + 64)
                        pe.wait_ge(s_xa, k + 1)
                        for half in range(2):
                            hidden(k, s, half, 0)
                            hidden(k, s, half, 1)
                            if half:
                                final(k, s, 0)
                            second(k, s, half, 0)
                            hidden(k, s, half, 2)
                            second(k, s, half, 1)
                            hidden(k, s, half, 3)
                            second(k, s, half, 2)
                            second(k, s, half, 3)
                            if more:
                                project(k + 1) if half else turn(k + 1)
                        final(k, s, 1)

                    steps(pe, step)

                @block.scalar
                def _(act):
                    act.preload_act_table_set("gelu_and_others")
                    act.wait_ge(s_c3, 16 * NC3)

                    def front(k):
                        act.wait_ge(s_tp, k * 2 + 1)
                        act.activation(XFT[:, :], psum[0][:, :], ACT.Copy).then_inc(s_ft, 1)
                        act.wait_ge(s_tp, k * 2 + 2)
                        act.activation(NT[:, :], psum[1][:, :], ACT.Identity, scale=fcols[:, 0:1], bias=fcols[:, 1:2]).then_inc(s_ft, 1)

                    front(0)

                    def step(k, s, e, more):
                        for half in range(2):
                            for c in range(FC):
                                act.wait_ge(s_f1, k * 8 + (4 * half + c + 1))
                                if c == 0 and not (isinstance(k, int) and k == 0):
                                    act.wait_ge(s_y3, k * 2 + half - 1)
                                act.activation(HG[half][:, c, :], psum[3][:, (c % 2) * 512:(c % 2) * 512 + 512], ACT.Gelu,
                                               bias=c1[s][:, c:c + 1]).then_inc(s_gl, 1)
                            if not half and more:
                                front(k + 1)
                            if half:
                                for z in range(2):
                                    act.wait_ge(s_z, k * 2 + z + 1)
                                    act.activation(Z[z][:, :, :], Z[z][:, :, :], ACT.Gelu).then_inc(s_zg, 1)

                    steps(act, step)

                @block.vector
                def _(v):
                    n, start = [0], [0]

                    def link(ins):
                        n[0] += 1
                        ins.then_inc(s_v3, 1)
                        v.wait_ge(s_v3, start[0] + n[0])

                    def norm(k, s, e):
                        v.wait_ge(s_h3[s], e * 16 + 16)
                        for b in range(GB):
                            last = v.bn_stats(st3[:, b, :], H3[s][:, b, :])
                        link(last)
                        v.memset(idle3[:, :], 0.0)
                        for b in range(GB):
                            last = v.bn_aggr(mv3[:, b, :], st3[:, b, :])
                        link(last)
                        v.tensor_scalar(pw3[:, 0, :], mv3[:, :, 1], 1e-5, None, ALU.add).then_inc(s_pi3, 1)
                        v.wait_ge(s_po3, k * 2 + 1)
                        link(v.tensor_tensor(rr3[:, 0, :], mv3[:, :, 1], rs3[:, 0, :], ALU.mult))
                        link(v.tensor_tensor(rr3[:, 1, :], rr3[:, 0, :], rs3[:, 0, :], ALU.mult))
                        v.tensor_scalar(pw3[:, 1, :], rr3[:, 1, :], 1e-5, None, ALU.add).then_inc(s_pi3, 1)
                        if not (isinstance(k, int) and k == 0):
                            v.wait_ge(s_tp, k * 2)
                        for b in range(GB):
                            v.tensor_scalar(XF[:, b, :], H3[s][:, b, :], mv3[:, b, 0:1], rs3[:, 0, b:b + 1], ALU.subtract, ALU.mult)
                        v.wait_ge(s_po3, k * 2 + 2)
                        link(v.tensor_tensor(rr3[:, 2, :], rs3[:, 0, :], rs3[:, 1, :], ALU.mult))
                        for b in range(GB):
                            last = v.tensor_scalar(NN[:, b, :], H3[s][:, b, :], mv3[:, b, 0:1], rr3[:, 2, b:b + 1], ALU.subtract, ALU.mult)
                        last.then_inc(s_nf, 1)

                    def attended(k, s):
                        v.wait_ge(s_at, k + 1)
                        v.scalar_tensor_tensor(XA[s][:, :], psum[0][:, :], fcols[:, 2:3], XFT[:, :], ALU.add, ALU.add).then_inc(s_xa, 1)

                    def second(k, s, half):
                        v.wait_ge(s_y3, k * 2 + half + 1)
                        if not (isinstance(k, int) and k == 0):
                            v.wait_ge(s_nx, k * 2 + half - 1)
                        v.tensor_scalar(YT[half][:, :], psum[2][:, 0:512], c2[s][:, 0:1], None, ALU.add).then_inc(s_yt, 1)

                    def final(k, half):
                        v.wait_ge(s_nx, k * 2 + half + 1)
                        if not (isinstance(k, int) and k == 0):
                            v.wait_ge(s_r3, k * 2 + half - 1)
                        v.tensor_tensor(Z[half][:, :, :], psum[2][:, 512:1024].rearrange("p (b d) -> p b d", b=4),
                                        nextb[:, :].unsqueeze(1).to_broadcast([128, 4, D]), ALU.add).then_inc(s_z, 1)

                    v.wait_ge(s_c3, 16 * NC3)
                    norm(0, 0, 0)
                    attended(0, 0)
                    pre = n[0]

                    def step(k, s, e, more):
                        n[0] = 0
                        start[0] = k * NORM_STEPS + pre
                        second(k, s, 0)
                        if more:
                            norm(k + 1, 1 - s, e + s)
                        final(k, 0)
                        second(k, s, 1)
                        if more:
                            attended(k + 1, 1 - s)
                            assert n[0] == NORM_STEPS, n[0]
                        final(k, 1)

                    steps(v, step)
    return nc


def kernel(**inputs):
    import concourse.bacc as bacc
    from concourse import mybir
    from concourse.bass_utils import run_bass_kernel_spmd

    c = lambda a: np.ascontiguousarray(a)
    a = {k: np.asarray(v) for k, v in inputs.items()}
    arrays = {
        "x": c(a["x"]), "y": c(a["itok_BS_0_21"]),
        "ident": np.eye(128, dtype=np.float32),
        "iota": (np.arange(3 * V) % V).astype(np.float32).reshape(3 * V, 1),
        "embT": c(a["L0_tok_W_embed"].T), "wproj": c(a["L0_tok_W_proj"]),
        "bproj": c(a["L0_tok_b_proj"].reshape(D, 1)),
        "wgap": c(a["L0_tok_W_gap"].reshape(2, D).T), "bgap": c(a["L0_tok_b_gap"]),
        "wqkvT": c(a["L0_attn_W_qkv"].T), "wposT": c(a["L0_attn_W_pos"].T), "woutT": c(a["L0_attn_W_out"].T),
        "cols": c(np.stack([a["L0_attn_ln2_g"], a["L0_attn_ln2_b"], a["L0_attn_pos_bias_u"].reshape(D),
                            a["L0_attn_pos_bias_v"].reshape(D)], axis=1)),
        "attnT": c(a["L0_ffn_attn_w"].T), "nextT": c(a["L0_ffn_next_w"].T), "next_b": c(a["L0_ffn_next_b"]),
        "fcols": c(np.stack([a["L0_ffn_ln_g"], a["L0_ffn_ln_b"], a["L0_ffn_attn_b"]], axis=1)),
        "fc1T": c(a["L0_ffn_fc1_w"].transpose(0, 2, 1)),
        "fc2T": c(a["L0_ffn_fc2_w"].reshape(EXPERTS, D, FC, 128).transpose(0, 3, 2, 1)),
        "fc1b": c(a["L0_ffn_fc1_b"].reshape(EXPERTS, FC, 128).transpose(0, 2, 1)),
        "fc2b": c(a["L0_ffn_fc2_b"].reshape(EXPERTS, D, 1)),
        "b_out": c(a["L0_attn_b_out"]), "ln1_g": c(a["L0_attn_ln1_g"]), "ln1_b": c(a["L0_attn_ln1_b"]),
        "invf": (1.0 / 10000.0 ** (np.arange(0, D, 2, dtype=np.float32) / D)).astype(np.float32),
        "upto": np.triu(np.ones((N, N), np.float32)), "beyond": np.tril(np.ones((N, N), np.int32), -1),
    }
    nc = bacc.Bacc("TRN2", target_bir_lowering=False, num_devices=1)
    feeds, t = {}, {}
    for k, v in arrays.items():
        feeds[k + "_in"] = v
        t[k] = nc.dram_tensor(k + "_in", v.shape, mybir.dt.from_np(v.dtype), kind="ExternalInput").ap()
    out = nc.dram_tensor("out_dram", (B, N, M), mybir.dt.float32, kind="ExternalOutput").ap()
    build(nc, t, out)
    r = run_bass_kernel_spmd(nc, [feeds], core_ids=[0])
    return r.results[0]["out_dram"]
```

```python
import numpy as np

B = 128
N = 128
M = 128
D = 128
V = 22
NEG = -1.0e8
ROWS = 8
NBLK = N // ROWS
CB = 8
NCH = B // CB
KKW = 2 * M + 1
HEADS = 8
DK = D // HEADS
GB = 8
NG = B // GB
TWO_PI = 2 * np.pi
TWO_PI_HI = float(np.float32(6.28125))
TWO_PI_LO = TWO_PI - TWO_PI_HI
HALF_PI = np.pi / 2
PI_IN = 3.1415925
ROUND = 1.5 * 2 ** 23
EXPERTS = 8
FF = 4 * D
FC = FF // 128
NORM_STEPS = 5
PER_GROUP = GB + GB + 7


def build(nc, t, out):
    import concourse.bass as bass
    from concourse import mybir
    from contextlib import ExitStack

    f32, bf16, i32 = mybir.dt.float32, mybir.dt.bfloat16, mybir.dt.int32
    ALU, ACT, AX = mybir.AluOpType, mybir.ActivationFunctionType, mybir.AxisListType
    ds = bass.ds

    kk_dram = nc.dram_tensor("kk_dram", (NBLK, B, ROWS * KKW), f32).ap()
    h_dram = nc.dram_tensor("h_dram", (B, N, M), f32).ap()
    h2_dram = nc.dram_tensor("h2_dram", (NG, N, GB * D), f32).ap()
    f_dram = nc.dram_tensor("f_dram", (GB, N * (N + 1) * HEADS), f32).ap()

    def view(ap, extra, dims):
        return bass.AP(ap.tensor, ap.offset + extra, [list(ap.ap[0])] + [list(d) for d in dims])

    def backwards(ap):
        dims = [list(q) for q in ap.ap]
        step, count = dims[-1]
        dims[-1] = [-step, count]
        return bass.AP(ap.tensor, ap.offset + step * (count - 1), dims)

    def pairs(eng, count, body, until=None):
        body(0, 0)
        body(1, 1)
        with eng.Fori(1, count // 2) as it:
            body(it * 2, 0)
            body(it * 2 + 1, 1)

    def reused(k):
        return not isinstance(k, int) or k >= 2

    with ExitStack() as ctx:
        def sb(name, shape, dt=f32):
            return ctx.enter_context(nc.sbuf_tensor(name, shape, dt))

        def sem(name):
            return ctx.enter_context(nc.semaphore(name))

        psum = [ctx.enter_context(nc.psum_tensor(f"bank{i}", [128, 1024], f32)) for i in range(4)]

        ident = sb("ident", [128, 128])

        with ExitStack() as p1:
            def sb1(name, shape, dt=f32):
                return p1.enter_context(nc.sbuf_tensor(name, shape, dt))

            big_a = sb1("big_a", [128, N * B])
            big_b = sb1("big_b", [128, N * M])
            embT = sb1("embT", [D, V])
            wproj = sb1("wproj", [D, D])
            bproj = sb1("bproj", [D, 1])
            wgap = sb1("wgap", [D, 2])
            bgap = sb1("bgap", [128, 1])
            iota = sb1("iota", [3 * V, 1])
            toknat = sb1("toknat", [128, 2, 128], i32)
            tokf = sb1("tokf", [128, 2, 128])
            hit = sb1("hit", [128, 128])
            counts = sb1("counts", [128, 2, V])
            ZT = sb1("ZT", [D, V])
            wgapw = sb1("wgapw", [D, 2, 128])
            G3 = sb1("G3", [V, 3 * V], bf16)
            Gr = sb1("Gr", [V, 2, V])
            gapz = sb1("gapz", [128, 2 * V])
            Asum = sb1("Asum", [128, 2 * V])
            Acol = sb1("Acol", [128, 4])
            neg2A = sb1("neg2A", [128, 1])
            n2first = sb1("n2first", [128, 1])
            tokx = [big_b[0:V, s * CB * N:(s + 1) * CB * N].bitcast(i32) for s in range(2)]
            toky = [big_b[0:3 * V, (2 + s) * CB * M:(3 + s) * CB * M].bitcast(i32) for s in range(2)]
            ox = [big_b[0:V, (8 + s) * CB * N // 2:(9 + s) * CB * N // 2].bitcast(bf16) for s in range(2)]
            oy = [big_b[0:3 * V, (10 + s) * CB * M // 2:(11 + s) * CB * M // 2].bitcast(bf16) for s in range(2)]
            gx = [big_b[0:3 * V, (12 + s) * CB * N // 2:(13 + s) * CB * N // 2].bitcast(bf16) for s in range(2)]
            stage = [sb1(f"stage{s}", [128, ROWS, B]) for s in range(2)]
            Tb = [sb1(f"Tb{s}", [128, ROWS, M]) for s in range(2)]
            P = sb1("P", [128, ROWS + 1, M + 1])
            u = sb1("u", [128, M])
            Wb = sb1("Wb", [128, ROWS, M])
            KK = [sb1(f"KK{s}", [128, ROWS, KKW]) for s in range(2)]
            KL = [sb1(f"KL{s}", [128, ROWS * M + 8]) for s in range(2)]
            Mb = [sb1(f"Mb{s}", [128, ROWS, M]) for s in range(2)]
            prod = sb1("prod", [128, KKW + 7])
            ssum = sb1("ssum", [128, M])
            lnM = sb1("lnM", [128, M])
            carry = sb1("carry", [128, M])
            rec = sb1("rec", [128, M])
            Bb = [sb1(f"Bb{s}", [128, ROWS, M + 1]) for s in range(2)]
            Gb = Tb

            s_const = sem("s_const")
            s_tokn = sem("s_tokn")
            s_tok = [sem(f"s_tok{s}") for s in range(2)]
            s_pre_pe = sem("s_pre_pe")
            s_pre_act = sem("s_pre_act")
            s_pre_v = sem("s_pre_v")
            s_oneh = sem("s_oneh")
            s_gx = sem("s_gx")
            s_gxs = sem("s_gxs")
            s_th = sem("s_th")
            s_ths = sem("s_ths")
            s_stage = sem("s_stage")
            s_tr = sem("s_tr")
            s_T = sem("s_T")
            s_v = sem("s_v")
            s_zero = sem("s_zero")
            s_W = sem("s_W")
            s_raw = sem("s_raw")
            s_exp = sem("s_exp")
            s_mrow = sem("s_mrow")
            s_ln = sem("s_ln")
            s_spill = [sem(f"s_spill{s}") for s in range(2)]
            s_load = [sem(f"s_load{s}") for s in range(2)]
            s_b = sem("s_b")
            s_g = sem("s_g")
            s_h = [sem(f"s_h{s}") for s in range(2)]
            s_carry = sem("s_carry")

            T2 = big_a[:, :].rearrange("p (i b) -> p i b", b=B)

            NCONST = 7

            with nc.Block() as block:
                @block.sync
                def _(sp):
                    for dst, src in ((ident, t["ident"]), (embT, t["embT"]), (wproj, t["wproj"]), (bproj, t["bproj"]),
                                     (wgap, t["wgap"]), (iota, t["iota"])):
                        sp.dma_start(dst[:, :], src).then_inc(s_const, 16)
                    sp.dma_start(bgap[:, :], t["bgap"].partition_broadcast(128)).then_inc(s_const, 16)
                    sp.dma_start(toknat[:, 0, :], t["x"]).then_inc(s_tokn, 16)
                    sp.dma_start(toknat[:, 1, :], t["y"]).then_inc(s_tokn, 16)
                    xf = t["x"].rearrange("b i -> (b i)")
                    yf = t["y"].rearrange("b i -> (b i)")

                    def tokens(c, s):
                        if reused(c):
                            sp.wait_ge(s_oneh, c * 2 - 2)
                        sp.dma_start(tokx[s], xf[ds(c * (CB * N), CB * N)].partition_broadcast(V)).then_inc(s_tok[s], 16)
                        sp.dma_start(toky[s], yf[ds(c * (CB * M), CB * M)].partition_broadcast(3 * V)).then_inc(s_tok[s], 16)

                    pairs(sp, NCH, tokens)

                    def put_away(k, s):
                        sp.wait_ge(s_mrow, k + 1)
                        sp.dma_start(kk_dram[ds(k, 1), :, :].rearrange("k p n -> (k p) n"),
                                     KK[s][:, :, :].rearrange("p r n -> p (r n)")).then_inc(s_spill[s], 16)
                        sp.dma_start(big_a[:, ds(k * (ROWS * M), ROWS * M)], KL[s][:, 0:ROWS * M]).then_inc(s_spill[s], 16)
                        sp.dma_start(big_b[:, ds(k * (ROWS * M), ROWS * M)],
                                     Mb[s][:, :, :].rearrange("p r n -> p (r n)")).then_inc(s_spill[s], 16)

                    pairs(sp, NBLK, put_away)
                    sp.wait_ge(s_spill[0], 48 * NBLK // 2)
                    sp.wait_ge(s_spill[1], 48 * NBLK // 2)
                    sp.wait_ge(s_ln, NBLK)

                    def bring_back(n, s):
                        if reused(n):
                            sp.wait_ge(s_g, n - 1)
                            sp.dma_start(h_dram[:, ds(n * -ROWS + (NBLK + 1) * ROWS, ROWS), :], Gb[s][:, :, :]).then_inc(s_h[s], 16)
                            sp.wait_ge(s_carry, n - 1)
                        k = n * -1 + (NBLK - 1)
                        sp.dma_start(KK[s][:, :, :].rearrange("p r n -> p (r n)"),
                                     kk_dram[ds(k, 1), :, :].rearrange("k p n -> (k p) n")).then_inc(s_load[s], 16)
                        sp.dma_start(KL[s][:, 0:ROWS * M], big_a[:, ds(k * (ROWS * M), ROWS * M)]).then_inc(s_load[s], 16)
                        sp.dma_start(Mb[s][:, :, :].rearrange("p r n -> p (r n)"),
                                     big_b[:, ds(k * (ROWS * M), ROWS * M)]).then_inc(s_load[s], 16)

                    pairs(sp, NBLK, bring_back)
                    for s in range(2):
                        sp.wait_ge(s_g, NBLK - 1 + s)
                        sp.dma_start(h_dram[:, (1 - s) * ROWS:(2 - s) * ROWS, :], Gb[s][:, :, :]).then_inc(s_h[s], 16)
                    sp.wait_ge(s_h[0], 16 * NBLK // 2)
                    sp.wait_ge(s_h[1], 16 * NBLK // 2)

                @block.tensor
                def _(pe):
                    pe.wait_ge(s_const, 16 * NCONST)
                    pe.matmul(psum[0][:, 0:V], wproj[:, :], embT[:, :], start=True, stop=True).then_inc(s_pre_pe, 1)
                    pe.wait_ge(s_pre_act, 1)
                    pe.matmul(psum[1][0:V, 0:V], ZT[:, :], ZT[:, :], start=True, stop=True).then_inc(s_pre_pe, 1)
                    pe.wait_ge(s_pre_v, 1)
                    pe.matmul(psum[2][:, 0:V], wgapw[:, 0, :], ZT[:, :], start=True, stop=True)
                    pe.matmul(psum[2][:, 512:512 + V], wgapw[:, 1, :], ZT[:, :], start=True, stop=True).then_inc(s_pre_pe, 1)
                    pe.wait_ge(s_pre_v, 2)

                    def letters(c, s):
                        pe.wait_ge(s_oneh, c * 2 + 2)
                        if reused(c):
                            pe.wait_ge(s_gxs, c - 1)
                        for half in range(2):
                            last = pe.matmul(psum[s][0:3 * V, half * 512:(half + 1) * 512], G3[:, :],
                                             ox[s][:, half * 512:(half + 1) * 512], start=True, stop=True)
                        last.then_inc(s_gx, 1)

                    def scores(c, s):
                        pe.wait_ge(s_gxs, c + 1)
                        if reused(c):
                            pe.wait_ge(s_ths, c - 1)
                        for b in range(CB):
                            last = pe.matmul(psum[2 + s][:, b * N:(b + 1) * N], oy[s][:, b * M:(b + 1) * M],
                                             gx[s][:, b * N:(b + 1) * N], start=True, stop=True)
                        last.then_inc(s_th, 1)

                    letters(0, 0)
                    letters(1, 1)
                    scores(0, 0)
                    with pe.Fori(1, NCH // 2) as it:
                        letters(it * 2, 0)
                        scores(it * 2 - 1, 1)
                        letters(it * 2 + 1, 1)
                        scores(it * 2, 0)
                    scores(NCH - 1, 1)

                    def turn(k, s):
                        pe.wait_ge(s_stage, k + 1)
                        for r in range(ROWS):
                            last = pe.transpose(psum[s][:, r * M:(r + 1) * M], stage[s][:, r, :], ident[:, :])
                        last.then_inc(s_tr, 1)

                    def exponents(k):
                        for q in range(ROWS // 2):
                            tile = psum[2 + q % 2]
                            pe.wait_ge(s_W, k * 4 + q + 1)
                            if q >= 2 or not (isinstance(k, int) and k == 0):
                                pe.wait_ge(s_exp, k * 4 + (q - 1))
                            pe.matmul(tile[:, 0:512], ident[:, :], view(Wb[:, 2 * q, :], 0, [[0, 2], [M, 2], [1, M]]), start=True, stop=False)
                            pe.matmul(tile[:, 0:512], ident[:, :], view(P[:, 2 * q, :], 0, [[1, 2], [M + 1, 2], [1, M]]), start=False, stop=True)
                            pe.matmul(tile[:, 512:768], ident[:, :], Wb[:, 2 * q:2 * q + 2, :], start=True, stop=False)
                            pe.matmul(tile[:, 512:768], ident[:, :], P[:, 2 * q + 1:2 * q + 3, 0:M], start=False, stop=True).then_inc(s_raw, 1)

                    turn(0, 0)
                    turn(1, 1)
                    exponents(0)
                    with pe.Fori(0, NBLK // 2 - 1) as it:
                        turn(it * 2 + 2, 0)
                        exponents(it * 2 + 1)
                        turn(it * 2 + 3, 1)
                        exponents(it * 2 + 2)
                    exponents(NBLK - 1)

                @block.gpsimd
                def _(pool):
                    pool.memset(P[:, :, :], NEG).then_inc(s_zero, 1)
                    for s in range(2):
                        pool.memset(KK[s][:, :, :], 0.0).then_inc(s_zero, 1)
                        pool.memset(Bb[s][:, :, :], 0.0).then_inc(s_zero, 1)
                    pool.wait_ge(s_ths, NCH)

                    def stage_rows(k, s):
                        if reused(k):
                            pool.wait_ge(s_T, k - 1)
                        pool.tensor_copy(stage[s][:, :, :].rearrange("p r b -> p (r b)"),
                                         big_a[:, ds(k * (ROWS * B), ROWS * B)]).then_inc(s_stage, 1)

                    pairs(pool, NBLK, stage_rows)

                    def gradient(n, s):
                        pool.wait_ge(s_b, n + 1)
                        if reused(n):
                            pool.wait_ge(s_h[s], 8 * n - 8 * s)
                        pool.tensor_tensor(Gb[s][:, :, :], Mb[s][:, :, :], Bb[s][:, :, 0:M], ALU.mult).then_inc(s_g, 1)

                    pairs(pool, NBLK, gradient)

                @block.scalar
                def _(act):
                    act.preload_act_table_set("natural_log_exp_and_others")
                    act.wait_ge(s_pre_pe, 1)
                    act.activation(ZT[:, :], psum[0][:, 0:V], ACT.Identity, bias=bproj[:, 0:1]).then_inc(s_pre_act, 1)

                    def letters(c, s):
                        act.wait_ge(s_gx, c + 1)
                        if reused(c):
                            act.wait_ge(s_th, c - 1)
                        act.activation(gx[s], psum[s][0:3 * V, :], ACT.Copy).then_inc(s_gxs, 1)

                    def scores(c, s):
                        act.wait_ge(s_th, c + 1)
                        act.activation(view(big_a[:, ds(c * CB, CB)], 0, [[B, N], [1, CB]]),
                                       psum[2 + s][:, :].rearrange("p (b i) -> p i b", b=CB), ACT.Copy).then_inc(s_ths, 1)

                    letters(0, 0)
                    letters(1, 1)
                    scores(0, 0)
                    with act.Fori(1, NCH // 2) as it:
                        letters(it * 2, 0)
                        scores(it * 2 - 1, 1)
                        letters(it * 2 + 1, 1)
                        scores(it * 2, 0)
                    scores(NCH - 1, 1)

                    def theta(k, s):
                        act.wait_ge(s_tr, k + 1)
                        act.wait_ge(s_W, k * 4 - 4)
                        act.activation(Tb[s][:, :, :], psum[s][:, :].rearrange("p (r j) -> p r j", r=ROWS), ACT.Copy).then_inc(s_T, 1)

                    def coefficients(k, s):
                        if reused(k):
                            act.wait_ge(s_spill[s], k * 24 - 24 * s)
                        for q in range(ROWS // 2):
                            act.wait_ge(s_raw, k * 4 + q + 1)
                            r = 2 * q
                            raw = psum[2 + q % 2][:, 0:768].rearrange("p (z r n) -> p z r n", z=3, r=2)
                            if q == 0:
                                act.activation(KK[s][:, 0, M + 1:2 * M], raw[:, 0, 0, 1:M], ACT.Exp, bias=n2first[:, 0:1])
                                act.activation(KK[s][:, 1, M + 1:2 * M], raw[:, 0, 1, 1:M], ACT.Exp, bias=neg2A[:, 0:1])
                            else:
                                act.activation(KK[s][:, r:r + 2, M + 1:2 * M], raw[:, 0, :, 1:M], ACT.Exp, bias=neg2A[:, 0:1])
                            act.activation(KK[s][:, r:r + 2, 0:M], raw[:, 1, :, :], ACT.Exp)
                            act.activation(KL[s][:, r * M:(r + 2) * M].rearrange("p (r n) -> p r n", r=2), raw[:, 2, :, :],
                                           ACT.Exp).then_inc(s_exp, 1)

                    def logarithm(k, s):
                        act.wait_ge(s_mrow, k + 1)
                        act.activation(lnM[:, :], Mb[s][:, ROWS - 1, :], ACT.Ln).then_inc(s_ln, 1)

                    def theta_first(k, s):
                        act.wait_ge(s_tr, k + 1)
                        act.activation(Tb[s][:, :, :], psum[s][:, :].rearrange("p (r j) -> p r j", r=ROWS), ACT.Copy).then_inc(s_T, 1)

                    theta_first(0, 0)
                    coefficients(0, 0)
                    theta_first(1, 1)
                    logarithm(0, 0)
                    with act.Fori(0, NBLK // 2 - 1) as it:
                        for k, s in ((it * 2 + 1, 1), (it * 2 + 2, 0)):
                            coefficients(k, s)
                            theta(k + 1, 1 - s)
                            logarithm(k, s)
                    coefficients(NBLK - 1, 1)
                    logarithm(NBLK - 1, 1)

                @block.vector
                def _(v):
                    n = [0]
                    base = [0]

                    def link(ins):
                        n[0] += 1
                        ins.then_inc(s_v, 1)
                        v.wait_ge(s_v, base[0] + n[0])

                    v.wait_ge(s_const, 16 * NCONST)
                    v.tensor_copy(wgapw[:, :, :], wgap[:, :].unsqueeze(2).to_broadcast([D, 2, 128])).then_inc(s_pre_v, 1)
                    v.wait_ge(s_pre_pe, 2)
                    g_ps = psum[1][0:V, 0:V]
                    link(v.tensor_copy(G3[:, 0:V], g_ps))
                    link(v.tensor_tensor(Gr[:, 0, :], g_ps, G3[:, 0:V], ALU.subtract))
                    link(v.tensor_copy(G3[:, V:2 * V], Gr[:, 0, :]))
                    link(v.tensor_tensor(Gr[:, 1, :], Gr[:, 0, :], G3[:, V:2 * V], ALU.subtract))
                    link(v.tensor_copy(G3[:, 2 * V:3 * V], Gr[:, 1, :]))
                    v.wait_ge(s_pre_pe, 3)
                    v.tensor_copy(gapz[:, :].rearrange("p (z a) -> p z a", z=2),
                                  psum[2][:, :].rearrange("p (z n) -> p z n", z=2)[:, :, 0:V]).then_inc(s_pre_v, 1)

                    def one_hot(c, s):
                        v.wait_ge(s_tok[s], c * 16 + (32 - 16 * s))
                        if reused(c):
                            v.wait_ge(s_th, c - 1)
                        v.tensor_scalar(ox[s], tokx[s], iota[0:V, 0:1], None, ALU.is_equal).then_inc(s_oneh, 1)
                        v.tensor_scalar(oy[s], toky[s], iota[:, 0:1], None, ALU.is_equal).then_inc(s_oneh, 1)

                    pairs(v, NCH, one_hot)
                    v.wait_ge(s_pre_v, 2)
                    v.wait_ge(s_tokn, 32)
                    link(v.tensor_copy(tokf[:, :, :], toknat[:, :, :]))
                    for z in range(2):
                        for a in range(V):
                            link(v.tensor_scalar(hit[:, :], tokf[:, z, :], float(a), None, ALU.is_equal, ALU.add,
                                                 accum_out=counts[:, z, a:a + 1]))
                    link(v.tensor_tensor(Asum[:, :].rearrange("p (z a) -> p z a", z=2), gapz[:, :].rearrange("p (z a) -> p z a", z=2),
                                         counts[:, :, :], ALU.mult))
                    link(v.tensor_reduce(Acol[:, 0:1], Asum[:, :], AX.X, ALU.add))
                    link(v.tensor_scalar(Acol[:, 1:2], Acol[:, 0:1], 1.0 / N, bgap[:, 0:1], ALU.mult, ALU.add))
                    link(v.tensor_scalar(neg2A[:, :], Acol[:, 1:2], -2.0, None, ALU.mult))
                    v.wait_ge(s_zero, 5)
                    link(v.memset(P[:, 0, 1:2], 0.0))
                    link(v.memset(n2first[:, :], NEG))
                    for s in range(2):
                        link(v.memset(KL[s][:, ROWS * M:], 0.0))
                    link(v.memset(prod[:, :], 0.0))
                    link(v.memset(carry[:, :], 0.0))
                    link(v.memset(carry[:, M - 1:M], 1.0))

                    pre = n[0]
                    PER = 2 * ROWS + (3 * ROWS - 1) + 2
                    def forward(k, s):
                        n[0] = 0
                        base[0] = k * PER + pre
                        v.wait_ge(s_T, k + 1)
                        for r in range(ROWS):
                            link(v.scalar_tensor_tensor(u[:, :], P[:, r, 0:M], (n2first if r == 0 else neg2A)[:, 0:1],
                                                        P[:, r, 1:M + 1], ALU.add, ALU.max))
                            link(v.tensor_tensor_scan(P[:, r + 1, 1:M + 1], u[:, :], Tb[s][:, r, :], NEG, ALU.max, ALU.add))
                            if r % 2:
                                v.tensor_tensor(Wb[:, r - 1:r + 1, :], Tb[s][:, r - 1:r + 1, :], P[:, r:r + 2, 1:],
                                                ALU.subtract).then_inc(s_W, 1)
                        for r in range(ROWS):
                            if r % 2 == 0:
                                v.wait_ge(s_exp, k * 4 + (r // 2 + 1))
                            if r == 0:
                                src = KK[s][:, 0, :]
                            else:
                                link(v.tensor_tensor(view(prod[:, :], 0, [[M + 1, 2], [1, M]]),
                                                     view(KK[s][:, r, :], 0, [[M + 1, 2], [1, M]]),
                                                     Mb[s][:, r - 1:r, :].to_broadcast([128, 2, M]), ALU.mult))
                                src = prod[:, :]
                            link(v.tensor_tensor(ssum[:, :], src[:, 0:M], src[:, M:2 * M], ALU.add))
                            link(v.tensor_tensor_scan(Mb[s][:, r, :], KL[s][:, r * M:(r + 1) * M], ssum[:, :], 0.0,
                                                      ALU.mult, ALU.add))
                        v.nop().then_inc(s_mrow, 1)
                        link(v.tensor_copy(n2first[:, :], neg2A[:, :]))
                        v.wait_ge(s_ln, k + 1)
                        link(v.tensor_tensor(P[:, 0, 1:], P[:, ROWS, 1:], lnM[:, :], ALU.add))
                        assert n[0] == PER, (n[0], PER)

                    pairs(v, NBLK, forward)
                    pre2 = pre + PER * NBLK
                    PER2 = 2 + 3 * ROWS

                    def backward(k, s):
                        n[0] = 0
                        base[0] = k * PER2 + pre2
                        v.wait_ge(s_load[s], k * 24 + (48 - 24 * s))
                        link(v.reciprocal(rec[:, :], Mb[s][:, ROWS - 1, :]))
                        link(v.tensor_tensor(ssum[:, :], carry[:, :], rec[:, :], ALU.mult))
                        for r in range(ROWS - 1, -1, -1):
                            link(v.tensor_tensor_scan(backwards(Bb[s][:, r, 0:M]), backwards(KL[s][:, r * M + 1:(r + 1) * M + 1]),
                                                      backwards(ssum[:, :]), 0.0, ALU.mult, ALU.add))
                            if r == 0:
                                v.nop().then_inc(s_b, 1)
                            link(v.tensor_tensor(view(prod[:, :], 0, [[M + 1, 2], [1, M]]),
                                                 view(KK[s][:, r, :], 0, [[M + 1, 2], [1, M]]),
                                                 view(Bb[s][:, r, :], 0, [[1, 2], [1, M]]), ALU.mult))
                            link(v.tensor_tensor((ssum if r else carry)[:, :], prod[:, 0:M], prod[:, M + 1:2 * M + 1], ALU.add))
                        v.nop().then_inc(s_carry, 1)
                        assert n[0] == PER2, (n[0], PER2)

                    pairs(v, NBLK, backward)

        with ExitStack() as p2:
            def sb2(name, shape, dt=f32):
                return p2.enter_context(nc.sbuf_tensor(name, shape, dt))

            wqkvT = sb2("wqkvT", [D, 3 * D])
            wposT = sb2("wposT", [D, D])
            woutT = sb2("woutT", [D, D])
            bout = sb2("bout", [128, D])
            g1 = sb2("g1", [128, D])
            b1 = sb2("b1", [128, D])
            cols = sb2("cols", [128, 4])
            invf = sb2("invf", [128, D // 2])
            headof = sb2("headof", [D, HEADS])
            Pm = sb2("Pm", [D, N, HEADS])
            Hx = sb2("Hx", [128, GB, D])
            Hr = sb2("Hr", [128, GB, D])
            Y = sb2("Y", [128, GB, D])
            Xn = sb2("Xn", [128, GB, D])
            st = sb2("st", [128, GB, 6])
            mv = sb2("mv", [128, GB, 2])
            base_ = sb2("powbase", [128, 3, GB])
            rs = sb2("rs", [128, 3, GB])
            rr = sb2("rr", [128, 3, GB])
            mhalf = sb2("mhalf", [128, GB])
            trig = sb2("trig", [128, 5, D])
            peT = sb2("peT", [128, N])
            XT = sb2("XT", [D, GB * N])
            QU = [sb2(f"QU{s}", [D, GB * N]) for s in range(2)]
            QV = [sb2(f"QV{s}", [D, GB * N]) for s in range(2)]
            KT = sb2("KT", [D, GB * N])
            Vb = [sb2(f"Vb{s}", [128, GB, HEADS, DK + 1]) for s in range(2)]
            KTm = [sb2(f"KTm{s}", [D, HEADS, GB * N]) for s in range(2)]
            FS = [sb2(f"FS{s}", [128, N + 1, HEADS]) for s in range(2)]
            BD = [sb2(f"BD{s}", [128, N, HEADS]) for s in range(4)]
            S = [sb2(f"S{s}", [128, HEADS, N]) for s in range(2)]
            nm = sb2("nm", [128, 2, HEADS])
            idle = sb2("idle", [128, 1])
            mx = sb2("mx", [128, 2, HEADS])
            E = [sb2(f"E{s}", [128, HEADS, N]) for s in range(2)]
            PT = [sb2(f"PT{s}", [128, HEADS, N]) for s in range(2)]
            rd = sb2("rd", [128, HEADS])
            On = sb2("On", [128, GB, D])
            OT = sb2("OT", [D, 4 * N])

            s_c2 = sem("s_c2")
            s_hx = sem("s_hx")
            s_hr = sem("s_hr")
            s_v2 = sem("s_v2")
            s_powin = sem("s_powin")
            s_pow = sem("s_pow")
            s_y0 = sem("s_y0")
            s_y = sem("s_y")
            s_xn = sem("s_xn")
            s_v2w = sem("s_v2w")
            s_pos = sem("s_pos")
            s_posact = sem("s_posact")
            s_pospe = sem("s_pospe")
            s_xtp = sem("s_xtp")
            s_xt = sem("s_xt")
            s_q = sem("s_q")
            s_qs = sem("s_qs")
            s_k = sem("s_k")
            s_ks = sem("s_ks")
            s_vp = sem("s_vp")
            s_vs = sem("s_vs")
            s_mk = [sem(f"s_mk{s}") for s in range(2)]
            s_f = sem("s_f")
            s_fs = sem("s_fs")
            s_fw = [sem(f"s_fw{s}") for s in range(2)]
            s_bd = [sem(f"s_bd{s}") for s in range(4)]
            s_s = sem("s_s")
            s_a = sem("s_a")
            s_m = sem("s_m")
            s_e = sem("s_e")
            s_pt = sem("s_pt")
            s_pe = sem("s_pe")
            s_o = sem("s_o")
            s_n = sem("s_n")
            s_ot = sem("s_ot")
            s_ots = sem("s_ots")
            s_op = sem("s_op")
            s_res = sem("s_res")
            s_h2 = sem("s_h2")
            s_h2o = sem("s_h2o")

            NC2 = 10
            AHEAD = 4
            sums_bank = psum[3][:, 0:512]
            work_bank = psum[3][:, 512:1024]

            def rounds(eng, body):
                body(0, 0)
                body(1, 1)
                with eng.Fori(1, NG // 2 - 1) as it:
                    body(it * 2, 0)
                    body(it * 2 + 1, 1)
                body(NG - 2, 0)
                body(NG - 1, 1)

            def before(g, bound):
                return not isinstance(g, int) or g < bound

            def after(eng, done, count):
                if not (isinstance(count, int) and count <= 0):
                    eng.wait_ge(done, count)

            with nc.Block() as block:
                @block.sync
                def _(sp):
                    for dst, src in ((wqkvT[:, :], t["wqkvT"]), (wposT[:, :], t["wposT"]), (woutT[:, :], t["woutT"]),
                                     (cols[:, :], t["cols"]), (headof[:, :], t["headof"]),
                                     (bout[:, :], t["b_out"].partition_broadcast(128)), (g1[:, :], t["ln1_g"].partition_broadcast(128)),
                                     (b1[:, :], t["ln1_b"].partition_broadcast(128)), (invf[:, :], t["invf"].partition_broadcast(128))):
                        sp.dma_start(dst, src).then_inc(s_c2, 16)

                    def load(dst, first, done):
                        sp.dma_start(dst[:, :, :], h_dram[ds(first, GB), :, :].rearrange("b i d -> i b d")).then_inc(done, 16)

                    def put_scores(g, b):
                        sp.wait_ge(s_fs, g * GB + b + 1)
                        sp.dma_start(f_dram[b % GB, :].rearrange("(q n) -> q n", q=N),
                                     FS[b % 2][:, :, :].rearrange("p c h -> p (c h)")).then_inc(s_fw[b % 2], 16)

                    def get_scores(g, b):
                        sp.wait_ge(s_fw[b % 2], g * 64 + (b // 2) * 16 + 16)
                        sp.dma_start(BD[b % 4][:, :, :].rearrange("p k h -> p (k h)"),
                                     f_dram[b % GB, N * HEADS:].rearrange("(q n) -> q n", q=N)).then_inc(s_bd[b % 4], 16)

                    def mask_keys(g, s):
                        sp.wait_ge(s_ks, g * 2 + 2)
                        for h in range(HEADS):
                            sp.dma_start(KTm[s][h * DK:(h + 1) * DK, h, :], KT[h * DK:(h + 1) * DK, :]).then_inc(s_mk[s], 16)

                    sp.dma_start(ident[:, :], t["ident"]).then_inc(s_c2, 16)
                    load(Hx, 0, s_hx)
                    load(Hr, 0, s_hr)
                    sp.wait_ge(s_v2w, 5)
                    sp.wait_ge(s_y0, 1)
                    load(Hx, GB, s_hx)
                    mask_keys(0, 0)
                    for b in range(AHEAD):
                        put_scores(0, b)
                        if b:
                            get_scores(0, b - 1)

                    def round_(g, s):
                        for b in range(GB):
                            if b < 5 or before(g, NG - 1):
                                get_scores(g, b + 3)
                            if b < 4 or before(g, NG - 1):
                                put_scores(g, b + AHEAD)
                            if b == 3 and not (isinstance(g, int) and g == 0):
                                written = sp.snap(g - 1)
                                sp.wait_ge(s_h2, g * 2)
                                sp.dma_start(h2_dram[ds(written, 1), :, :].rearrange("g i n -> (g i) n"),
                                             Hr[:, :, :].rearrange("p b d -> p (b d)")).then_inc(s_h2o, 16)
                            if b == 4 and not (isinstance(g, int) and g == 0):
                                first = sp.snap(g * GB)
                                sp.wait_ge(s_h2o, g * 16)
                                load(Hr, first, s_hr)
                            if b == 5 and before(g, NG - 1):
                                mask_keys(g + 1, 1 - s)
                            if b == 0 and before(g, NG - 2):
                                first = sp.snap((g + 2) * GB)
                                sp.wait_ge(s_y0, g + 2)
                                load(Hx, first, s_hx)

                    rounds(sp, round_)
                    sp.wait_ge(s_h2, NG * 2)
                    sp.dma_start(h2_dram[NG - 1, :, :], Hr[:, :, :].rearrange("p b d -> p (b d)")).then_inc(s_h2o, 16)
                    sp.wait_ge(s_h2o, NG * 16)

                @block.gpsimd
                def _(pool):
                    pool.memset(mhalf[:, :], -0.5).then_inc(s_v2w, 1)
                    for s in range(2):
                        pool.memset(FS[s][:, 0, :], 0.0).then_inc(s_v2w, 1)
                    for s in range(2):
                        pool.memset(KTm[s][:, :, :], 0.0).then_inc(s_v2w, 1)
                    pool.wait_ge(s_v2w, 5)
                    pool.wait_ge(s_c2, 16 * NC2)

                    def powers(g, c):
                        pool.wait_ge(s_powin, g * 3 + c + 1)
                        pool.tensor_tensor(rs[:, c, :], base_[:, c, :], mhalf[:, :], ALU.pow).then_inc(s_pow, 1)

                    def affine(g):
                        pool.wait_ge(s_y0, g + 1)
                        pool.tensor_tensor(Y[:, :, :], Y[:, :, :], g1[:, :].unsqueeze(1).to_broadcast([128, GB, D]), ALU.mult).then_inc(s_y, 1)
                        pool.wait_ge(s_y, g * 2 + 1)
                        pool.tensor_tensor(Y[:, :, :], Y[:, :, :], b1[:, :].unsqueeze(1).to_broadcast([128, GB, D]), ALU.add).then_inc(s_y, 1)

                    def residual(g):
                        pool.wait_ge(s_hr, g * 16 + 16)
                        pool.tensor_tensor(Hr[:, :, :], Hr[:, :, :], bout[:, :].unsqueeze(1).to_broadcast([128, GB, D]), ALU.add).then_inc(s_res, 1)

                    for g in range(2):
                        powers(g, 0)
                        powers(g, 1)
                        affine(g)
                        powers(g, 2)

                    def round_(g, s):
                        more = before(g, NG - 2)
                        if more:
                            powers(g + 2, 0)
                        residual(g)
                        if more:
                            powers(g + 2, 1)
                            affine(g + 2)
                            powers(g + 2, 2)

                    rounds(pool, round_)

                @block.tensor
                def _(pe):
                    pe.wait_ge(s_c2, 16 * NC2)
                    pe.wait_ge(s_posact, 1)
                    pe.transpose(psum[0][:, 0:N], trig[:, 0, :], ident[:, :]).then_inc(s_pospe, 1)
                    pe.wait_ge(s_posact, 2)
                    pe.matmul(psum[1][:, 0:N], wposT[:, :], peT[:, :], start=True, stop=True).then_inc(s_pospe, 1)

                    def turn_x(g, half):
                        if half == 0:
                            pe.wait_ge(s_xn, g + 1)
                            after(pe, s_h2, g * 2 - 3)
                        else:
                            pe.wait_ge(s_xt, g * 2 + 1)
                        for b in range(4):
                            last = pe.transpose(work_bank[:, b * N:(b + 1) * N], Xn[:, 4 * half + b, :], ident[:, :])
                        last.then_inc(s_xtp, 1)

                    def queries(g, half):
                        if half == 0:
                            pe.wait_ge(s_xt, g * 2 + 2)
                            after(pe, s_h2, g * 2 - 2)
                        else:
                            pe.wait_ge(s_qs, g * 2 + 1)
                        pe.matmul(work_bank, wqkvT[:, 0:D], XT[:, half * 512:(half + 1) * 512], start=True, stop=True).then_inc(s_q, 1)

                    def keys(g, half):
                        if half == 0:
                            pe.wait_ge(s_qs, g * 2 + 2)
                        else:
                            pe.wait_ge(s_ks, g * 2 + 1)
                        pe.matmul(work_bank, wqkvT[:, D:2 * D], XT[:, half * 512:(half + 1) * 512], start=True, stop=True).then_inc(s_k, 1)

                    def values(g, half):
                        if half == 0:
                            pe.wait_ge(s_ks, g * 2 + 2)
                        else:
                            pe.wait_ge(s_vs, g * 2 + 1)
                        for b in range(4):
                            last = pe.matmul(work_bank[:, b * D:(b + 1) * D], XT[:, (4 * half + b) * N:(4 * half + b + 1) * N],
                                             wqkvT[:, 2 * D:3 * D], start=True, stop=True)
                        last.then_inc(s_vp, 1)

                    def turn_o(g, half):
                        pe.wait_ge(s_n, g * GB + 4 * half + 4)
                        if half == 0:
                            pe.wait_ge(s_vs, g * 2 + 4 if before(g, NG - 1) else g * 2 + 2)
                        elif before(g, NG - 2):
                            pe.wait_ge(s_xt, g * 2 + 6)
                        else:
                            pe.wait_ge(s_h2, g * 2 + 1)
                        for b in range(4):
                            last = pe.transpose(work_bank[:, b * N:(b + 1) * N], On[:, 4 * half + b, :], ident[:, :])
                        last.then_inc(s_ot, 1)

                    def project(g, half):
                        pe.wait_ge(s_ots, g * 2 + half + 1)
                        for b in range(4):
                            last = pe.matmul(work_bank[:, b * D:(b + 1) * D], OT[:, b * N:(b + 1) * N], woutT[:, :], start=True, stop=True)
                        last.then_inc(s_op, 1)

                    def position_scores(g, s, b):
                        after(pe, s_fs, g * GB + b)
                        pe.wait_ge(s_qs, g * 2 + b // 4 + 1)
                        for half in range(2):
                            last = pe.matmul(psum[0][:, half * 512:(half + 1) * 512], QV[s][:, b * N:(b + 1) * N],
                                             Pm[:, half * 64:(half + 1) * 64, :], start=True, stop=True)
                        last.then_inc(s_f, 1)

                    def content_scores(g, s, b):
                        after(pe, s_a, g * GB + b)
                        if b == 0:
                            pe.wait_ge(s_qs, g * 2 + 2)
                            pe.wait_ge(s_mk[s], (g - s) * 64 + 128)
                        for half in range(2):
                            last = pe.matmul(psum[1][:, half * 512:(half + 1) * 512], QU[s][:, b * N:(b + 1) * N],
                                             KTm[s][:, 4 * half:4 * half + 4, b * N:(b + 1) * N], start=True, stop=True)
                        last.then_inc(s_s, 1)

                    def turn_e(g, b):
                        after(pe, s_pe, g * GB + b)
                        pe.wait_ge(s_e, g * GB + b + 1)
                        for h in range(HEADS):
                            last = pe.transpose(psum[2][:, h * N:(h + 1) * N], E[b % 2][:, h, :], ident[:, :])
                        last.then_inc(s_pt, 1)

                    def weighted(g, s, b):
                        pe.wait_ge(s_pe, g * GB + b + 1)
                        pe.wait_ge(s_vs, g * 2 + 2)
                        after(pe, s_n, g * GB + b)
                        for h in range(HEADS):
                            last = pe.matmul(sums_bank[:, h * (DK + 1):(h + 1) * (DK + 1)], PT[b % 2][:, h, :], Vb[s][:, b, h, :],
                                             start=True, stop=True)
                        last.then_inc(s_o, 1)

                    for step in (turn_x, queries, keys, values):
                        step(0, 0)
                        step(0, 1)
                    pe.wait_ge(s_pos, 2)
                    for b in range(AHEAD):
                        position_scores(0, 0, b)
                    content_scores(0, 0, 0)

                    def round_(g, s):
                        more = before(g, NG - 1)
                        earlier = not (isinstance(g, int) and g == 0)
                        for b in range(GB):
                            if b + 1 < GB:
                                content_scores(g, s, b + 1)
                            elif more:
                                content_scores(g + 1, 1 - s, 0)
                            if more and b in (1, 3, 4, 5):
                                {1: turn_x, 3: queries, 4: keys, 5: values}[b](g + 1, 1)
                            if earlier and b == 2:
                                project(g - 1, 1)
                            if b == 6:
                                project(g, 0)
                            if b:
                                weighted(g, s, b - 1)
                            elif earlier:
                                weighted(g - 1, 1 - s, GB - 1)
                            if b < 4:
                                position_scores(g, s, b + AHEAD)
                            elif more:
                                position_scores(g + 1, 1 - s, b - AHEAD)
                            turn_e(g, b)
                            if more and b in (0, 2, 3, 4):
                                {0: turn_x, 2: queries, 3: keys, 4: values}[b](g + 1, 0)
                            if earlier and b == 1:
                                turn_o(g - 1, 1)
                            if b == 5:
                                turn_o(g, 0)

                    rounds(pe, round_)
                    weighted(NG - 1, 1, GB - 1)
                    turn_o(NG - 1, 1)
                    project(NG - 1, 1)

                @block.scalar
                def _(act):
                    act.wait_ge(s_c2, 16 * NC2)
                    act.wait_ge(s_pos, 1)
                    act.activation(trig[:, 0, :], trig[:, 4, :], ACT.Sin).then_inc(s_posact, 1)
                    act.wait_ge(s_pospe, 1)
                    act.activation(peT[:, :], psum[0][:, 0:N], ACT.Copy).then_inc(s_posact, 1)
                    act.preload_act_table_set("natural_log_exp_and_others")

                    def copy_x(g, half):
                        act.wait_ge(s_xtp, g * 2 + half + 1)
                        act.activation(XT[:, half * 512:(half + 1) * 512], work_bank, ACT.Identity,
                                       scale=cols[:, 0:1], bias=cols[:, 1:2]).then_inc(s_xt, 1)

                    def copy_q(g, s, half):
                        act.wait_ge(s_q, g * 2 + half + 1)
                        act.activation(QU[s][:, half * 512:(half + 1) * 512], work_bank, ACT.Identity, bias=cols[:, 2:3])
                        act.activation(QV[s][:, half * 512:(half + 1) * 512], work_bank, ACT.Identity, bias=cols[:, 3:4]).then_inc(s_qs, 1)

                    def copy_k(g, half):
                        act.wait_ge(s_k, g * 2 + half + 1)
                        act.activation(KT[:, half * 512:(half + 1) * 512], work_bank, ACT.Copy).then_inc(s_ks, 1)

                    def copy_o(g, half):
                        act.wait_ge(s_ot, g * 2 + half + 1)
                        act.activation(OT[:, :], work_bank, ACT.Copy).then_inc(s_ots, 1)

                    def exponentials(g, b):
                        act.wait_ge(s_m, g * GB + b + 1)
                        after(act, s_pt, g * GB + b - 1)
                        for h in range(HEADS):
                            last = act.activation(E[b % 2][:, h, :], S[b % 2][:, h, :], ACT.Exp, bias=nm[:, b % 2, h:h + 1], scale=DK ** -0.5)
                        last.then_inc(s_e, 1)

                    def copy_f(g, b):
                        act.wait_ge(s_f, g * GB + b + 1)
                        after(act, s_fw[b % 2], g * 64 + (b // 2) * 16)
                        act.activation(FS[b % 2][:, 1:N + 1, :], psum[0][:, :].rearrange("p (c h) -> p c h", h=HEADS),
                                       ACT.Copy).then_inc(s_fs, 1)

                    def copy_e(g, b):
                        act.wait_ge(s_pt, g * GB + b + 1)
                        after(act, s_o, g * GB + b - 1)
                        act.activation(PT[b % 2][:, :, :], psum[2][:, :].rearrange("p (h n) -> p h n", h=HEADS), ACT.Copy).then_inc(s_pe, 1)

                    copy_x(0, 0)
                    copy_x(0, 1)
                    copy_q(0, 0, 0)
                    copy_q(0, 0, 1)
                    copy_k(0, 0)
                    copy_k(0, 1)
                    for b in range(AHEAD):
                        copy_f(0, b)
                    exponentials(0, 0)

                    def round_(g, s):
                        more = before(g, NG - 1)
                        earlier = not (isinstance(g, int) and g == 0)
                        for b in range(GB):
                            if more and b == 1:
                                copy_x(g + 1, 1)
                            if more and b == 3:
                                copy_q(g + 1, 1 - s, 1)
                            if more and b == 4:
                                copy_k(g + 1, 1)
                            if b + 1 < GB:
                                exponentials(g, b + 1)
                            elif more:
                                exponentials(g + 1, 0)
                            if b < 4 or more:
                                copy_f(g, b + AHEAD)
                            copy_e(g, b)
                            if more and b == 0:
                                copy_x(g + 1, 0)
                            if earlier and b == 1:
                                copy_o(g - 1, 1)
                            if more and b == 2:
                                copy_q(g + 1, 1 - s, 0)
                            if more and b == 3:
                                copy_k(g + 1, 0)
                            if b == 5:
                                copy_o(g, 0)

                    rounds(act, round_)
                    copy_o(NG - 1, 1)

                @block.vector
                def _(v):
                    n, start = [0], [0]

                    def link(ins):
                        n[0] += 1
                        ins.then_inc(s_v2, 1)
                        v.wait_ge(s_v2, start[0] + n[0])

                    def moments(src):
                        for b in range(GB):
                            last = v.bn_stats(st[:, b, :], src[:, b, :])
                        link(last)
                        v.memset(idle[:, :], 0.0)
                        for b in range(GB):
                            last = v.bn_aggr(mv[:, b, :], st[:, b, :])
                        link(last)

                    def norm_1(g):
                        v.wait_ge(s_hx, g * 16 + 16)
                        moments(Hx)
                        v.tensor_scalar(base_[:, 0, :], mv[:, :, 1], 1e-5, None, ALU.add).then_inc(s_powin, 1)

                    def norm_2(g):
                        v.wait_ge(s_pow, g * 3 + 1)
                        link(v.tensor_tensor(rr[:, 0, :], mv[:, :, 1], rs[:, 0, :], ALU.mult))
                        link(v.tensor_tensor(rr[:, 1, :], rr[:, 0, :], rs[:, 0, :], ALU.mult))
                        v.tensor_scalar(base_[:, 1, :], rr[:, 1, :], 1e-5, None, ALU.add).then_inc(s_powin, 1)

                    def norm_3(g):
                        v.wait_ge(s_pow, g * 3 + 2)
                        link(v.tensor_tensor(rr[:, 2, :], rs[:, 0, :], rs[:, 1, :], ALU.mult))
                        for b in range(GB):
                            last = v.tensor_scalar(Y[:, b, :], Hx[:, b, :], mv[:, b, 0:1], rr[:, 2, b:b + 1], ALU.subtract, ALU.mult)
                        last.then_inc(s_y0, 1)

                    def norm_4(g):
                        v.wait_ge(s_y, g * 2 + 2)
                        moments(Y)
                        v.tensor_scalar(base_[:, 2, :], mv[:, :, 1], 1e-5, None, ALU.add).then_inc(s_powin, 1)

                    def norm_5(g):
                        v.wait_ge(s_pow, g * 3 + 3)
                        after(v, s_xtp, g * 2)
                        for b in range(GB):
                            last = v.tensor_scalar(Xn[:, b, :], Y[:, b, :], mv[:, b, 0:1], rs[:, 2, b:b + 1], ALU.subtract, ALU.mult)
                        last.then_inc(s_xn, 1)

                    def copy_v(g, s, half):
                        v.wait_ge(s_vp, g * 2 + half + 1)
                        v.tensor_copy(Vb[s][:, 4 * half:4 * half + 4, :, 0:DK].rearrange("p b h e -> p (b h) e"),
                                      work_bank.rearrange("p (n e) -> p n e", e=DK)).then_inc(s_vs, 1)

                    def add_scores(g, b):
                        v.wait_ge(s_s, g * GB + b + 1)
                        v.wait_ge(s_bd[b % 4], g * 32 + (b // 4) * 16 + 16)
                        after(v, s_e, g * GB + b - 1)
                        v.tensor_tensor(S[b % 2][:, :, :], psum[1][:, :].rearrange("p (h k) -> p h k", h=HEADS),
                                        BD[b % 4][:, :, :].rearrange("p k h -> p h k"), ALU.add).then_inc(s_a, 1)
                        v.wait_ge(s_a, g * GB + b + 1)
                        link(v.tensor_reduce(mx[:, b % 2, :], S[b % 2][:, :, :], AX.X, ALU.max))
                        v.tensor_scalar(nm[:, b % 2, :], mx[:, b % 2, :], -DK ** -0.5, None, ALU.mult).then_inc(s_m, 1)

                    def divide(g, b):
                        v.wait_ge(s_o, g * GB + b + 1)
                        sums = sums_bank[:, 0:HEADS * (DK + 1)].rearrange("p (h e) -> p h e", h=HEADS)
                        link(v.reciprocal(rd[:, :], sums[:, :, DK]))
                        v.tensor_tensor(On[:, b, :].rearrange("p (h e) -> p h e", h=HEADS), sums[:, :, 0:DK],
                                        rd[:, :].unsqueeze(2).to_broadcast([128, HEADS, DK]), ALU.mult).then_inc(s_n, 1)

                    def residual(g, half):
                        v.wait_ge(s_res, g + 1)
                        v.wait_ge(s_op, g * 2 + half + 1)
                        rows = Hr[:, 4 * half:4 * half + 4, :]
                        v.tensor_tensor(rows, work_bank.rearrange("p (b d) -> p b d", b=4), rows, ALU.add).then_inc(s_h2, 1)

                    v.wait_ge(s_c2, 16 * NC2)
                    v.wait_ge(s_v2w, 1)
                    for s in range(2):
                        link(v.memset(Vb[s][:, :, :, :], 1.0))
                    norm_1(0)
                    norm_2(0)
                    link(v.tensor_scalar(rr[:, 2, 0:1], Hx[:, 0, 0:1], mv[:, 0, 0:1], rs[:, 0, 0:1], ALU.subtract, ALU.mult))
                    H2 = D // 2
                    x_, k_ = trig[:, 1, 0:H2], trig[:, 2, 0:H2]
                    a_ = trig[:, 3, 0:H2]
                    sin_, cos_ = trig[:, 4, 0:H2], trig[:, 4, H2:D]
                    link(v.tensor_scalar(x_, invf[:, :], rr[:, 2, 0:1], None, ALU.mult))
                    link(v.tensor_scalar(k_, x_, 1.0 / TWO_PI, ROUND, ALU.mult, ALU.add))
                    link(v.tensor_scalar(k_, k_, ROUND, None, ALU.subtract))
                    link(v.scalar_tensor_tensor(a_, k_, -TWO_PI_HI, x_, ALU.mult, ALU.add))
                    link(v.scalar_tensor_tensor(a_, k_, -TWO_PI_LO, a_, ALU.mult, ALU.add))
                    link(v.tensor_scalar(sin_, a_, PI_IN, -PI_IN, ALU.min, ALU.max))
                    link(v.tensor_scalar(x_, a_, HALF_PI, None, ALU.add))
                    link(v.tensor_scalar(k_, x_, PI_IN, -TWO_PI, ALU.is_gt, ALU.mult))
                    link(v.tensor_tensor(x_, x_, k_, ALU.add))
                    link(v.tensor_scalar(cos_, x_, PI_IN, -PI_IN, ALU.min, ALU.max))
                    v.nop().then_inc(s_pos, 1)
                    norm_3(0)
                    norm_4(0)
                    norm_5(0)
                    v.wait_ge(s_pospe, 2)
                    for h in range(HEADS):
                        last = v.tensor_scalar(Pm[:, :, h], psum[1][:, 0:N], headof[:, h:h + 1], None, ALU.mult)
                    last.then_inc(s_pos, 1)
                    copy_v(0, 0, 0)
                    copy_v(0, 0, 1)
                    norm_1(1)
                    norm_2(1)
                    norm_3(1)
                    add_scores(0, 0)
                    norm_4(1)
                    norm_5(1)
                    done = [n[0]]

                    def round_(g, s):
                        if isinstance(g, int):
                            start[0] = done[0] if g < 2 else done[0] + (g - 2) * per_round[0] - passed[0]
                        else:
                            start[0] = (g - 2) * per_round[0] + done[0]
                        n[0] = 0
                        more = before(g, NG - 1)
                        more_2 = before(g, NG - 2)
                        earlier = not (isinstance(g, int) and g == 0)
                        for b in range(GB):
                            if b + 1 < GB:
                                add_scores(g, b + 1)
                            elif more:
                                add_scores(g + 1, 0)
                            if b:
                                divide(g, b - 1)
                            elif earlier:
                                divide(g - 1, GB - 1)
                            if earlier and b == 2:
                                residual(g - 1, 1)
                            if more and b == 5:
                                copy_v(g + 1, 1 - s, 1)
                            if b == 6:
                                residual(g, 0)
                            if more_2 and b == 4:
                                norm_1(g + 2)
                            if more_2 and b == 5:
                                norm_2(g + 2)
                                norm_3(g + 2)
                            if more_2 and b == 6:
                                norm_4(g + 2)
                            if more_2 and b == 7:
                                norm_5(g + 2)
                            if more and b == 4:
                                copy_v(g + 1, 1 - s, 0)
                        if isinstance(g, int) and g < 2:
                            done[0] += n[0]
                        elif more_2:
                            assert n[0] == per_round[0], n[0]
                        elif more:
                            passed[0] = per_round[0] - n[0]

                    per_round, passed = [PER_GROUP], [0]
                    rounds(v, round_)
                    start[0] += n[0]
                    n[0] = 0
                    divide(NG - 1, GB - 1)
                    residual(NG - 1, 1)


        with ExitStack() as p3:
            def sb3(name, shape, dt=f32):
                return p3.enter_context(nc.sbuf_tensor(name, shape, dt))

            attnT = sb3("attnT", [D, D])
            nextT = sb3("nextT", [D, D])
            nextb = sb3("nextb", [128, D])
            fcols = sb3("fcols", [128, 3])
            W1 = [sb3(f"W1{s}", [D, FF]) for s in range(2)]
            W2 = [sb3(f"W2{s}", [128, FC, D]) for s in range(2)]
            c1 = [sb3(f"c1{s}", [128, FC]) for s in range(2)]
            c2 = [sb3(f"c2{s}", [128, 1]) for s in range(2)]
            Hn = [sb3(f"Hn{s}", [128, GB, D]) for s in range(2)]
            H3 = [sb3(f"H3{s}", [128, GB, D]) for s in range(2)]
            XF = sb3("XF", [128, GB, D])
            NN = sb3("NN", [128, GB, D])
            XFT = sb3("XFT", [D, GB * N])
            NT = sb3("NT", [D, GB * N])
            XA = [sb3(f"XA{s}", [D, GB * N]) for s in range(2)]
            HG = [sb3(f"HG{s}", [128, FC, 512]) for s in range(2)]
            YT = [sb3(f"YT{s}", [D, 512]) for s in range(2)]
            Z = [sb3(f"Z{s}", [128, 4, D]) for s in range(2)]
            st3 = sb3("st3", [128, GB, 6])
            mv3 = sb3("mv3", [128, GB, 2])
            pw3 = sb3("pw3", [128, 2, GB])
            rs3 = sb3("rs3", [128, 2, GB])
            rr3 = sb3("rr3", [128, 3, GB])
            mhalf3 = sb3("mhalf3", [128, GB])
            idle3 = sb3("idle3", [128, 1])

            s_c3 = sem("s_c3")
            s_mh = sem("s_mh")
            s_hn = [sem(f"s_hn{s}") for s in range(2)]
            s_h3 = [sem(f"s_h3{s}") for s in range(2)]
            s_w = [sem(f"s_w{s}") for s in range(2)]
            s_v3 = sem("s_v3")
            s_pi3 = sem("s_pi3")
            s_po3 = sem("s_po3")
            s_nf = sem("s_nf")
            s_tp = sem("s_tp")
            s_ft = sem("s_ft")
            s_at = sem("s_at")
            s_xa = sem("s_xa")
            s_f1 = sem("s_f1")
            s_gl = sem("s_gl")
            s_y3 = sem("s_y3")
            s_yt = sem("s_yt")
            s_nx = sem("s_nx")
            s_z = sem("s_z")
            s_zg = sem("s_zg")
            s_r3 = sem("s_r3")
            s_out = [sem(f"s_out{s}") for s in range(2)]

            NC3 = 4

            def steps(eng, body):
                body(0, 0, 0, True)
                body(1, 1, 0, True)
                with eng.Fori(1, EXPERTS - 1) as e:
                    body(e * 2, 0, e, True)
                    body(e * 2 + 1, 1, e, True)
                body(NG - 2, 0, EXPERTS - 1, True)
                body(NG - 1, 1, EXPERTS - 1, False)

            out_g = out.rearrange("(g b) i d -> g i b d", b=GB)

            with nc.Block() as block:
                @block.sync
                def _(sp):
                    for dst, src in ((attnT[:, :], t["attnT"]), (nextT[:, :], t["nextT"]), (fcols[:, :], t["fcols"]),
                                     (nextb[:, :], t["next_b"].partition_broadcast(128))):
                        sp.dma_start(dst, src).then_inc(s_c3, 16)

                    def weights(e, s):
                        sp.dma_start(W1[s][:, :], t["fc1T"][ds(e, 1), :, :].rearrange("e d h -> (e d) h")).then_inc(s_w[s], 16)
                        sp.dma_start(W2[s][:, :, :], t["fc2T"][ds(e, 1), :, :, :].rearrange("e h c d -> (e h) c d")).then_inc(s_w[s], 16)
                        sp.dma_start(c1[s][:, :], t["fc1b"][ds(e, 1), :, :].rearrange("e h c -> (e h) c")).then_inc(s_w[s], 16)
                        sp.dma_start(c2[s][:, :], t["fc2b"][ds(e, 1), :, :].rearrange("e h c -> (e h) c")).then_inc(s_w[s], 16)

                    def load(dst, e, s, done):
                        sp.dma_start(dst[s][:, :, :].rearrange("p b d -> p (b d)"),
                                     h2_dram[ds(e + EXPERTS * s, 1), :, :].rearrange("g i n -> (g i) n")).then_inc(done[s], 16)

                    for s in range(2):
                        load(Hn, 0, s, s_hn)
                    for s in range(2):
                        weights(0, s)
                        load(H3, 0, s, s_h3)

                    def step(k, s, e, more):
                        again = not (isinstance(e, int) and e == EXPERTS - 1)
                        if again:
                            sp.wait_ge(s_nf, k * 2 + 2)
                            load(Hn, e + 1, s, s_hn)
                            sp.wait_ge(s_yt, k * 2 + 2)
                            weights(e + 1, s)
                        sp.wait_ge(s_r3, k * 2 + 2)
                        sp.dma_start(out_g[ds(e + EXPERTS * s, 1), :, :, :].rearrange("g i b d -> (g i) b d"), H3[s][:, :, :]).then_inc(s_out[s], 16)
                        if again:
                            sp.wait_ge(s_out[s], e * 16 + 16)
                            load(H3, e + 1, s, s_h3)

                    steps(sp, step)
                    sp.wait_ge(s_out[0], 16 * EXPERTS)
                    sp.wait_ge(s_out[1], 16 * EXPERTS)

                @block.gpsimd
                def _(pool):
                    pool.memset(mhalf3[:, :], -0.5).then_inc(s_mh, 1)
                    pool.wait_ge(s_mh, 1)

                    def norm(k):
                        for c in range(2):
                            pool.wait_ge(s_pi3, k * 2 + c + 1)
                            pool.tensor_tensor(rs3[:, c, :], pw3[:, c, :], mhalf3[:, :], ALU.pow).then_inc(s_po3, 1)

                    norm(0)
                    norm(1)

                    def step(k, s, e, more):
                        pool.wait_ge(s_h3[s], e * 16 + 16)
                        for half in range(2):
                            pool.wait_ge(s_zg, k * 2 + half + 1)
                            pool.tensor_tensor(H3[s][:, 4 * half:4 * half + 4, :], Z[half][:, :, :], H3[s][:, 4 * half:4 * half + 4, :],
                                               ALU.add).then_inc(s_r3, 1)
                        if not (isinstance(e, int) and e == EXPERTS - 1):
                            norm(k + 2)

                    steps(pool, step)

                @block.tensor
                def _(pe):
                    def turn(k):
                        if not (isinstance(k, int) and k == 0):
                            pe.wait_ge(s_xa, k)
                        for z, src in enumerate((XF, NN)):
                            pe.wait_ge(s_nf, k * 2 + z + 1)
                            for b in range(GB):
                                last = pe.transpose(psum[z][:, b * N:(b + 1) * N], src[:, b, :], ident[:, :])
                            last.then_inc(s_tp, 1)

                    def project(k):
                        pe.wait_ge(s_ft, k * 2 + 2)
                        for half in range(2):
                            last = pe.matmul(psum[0][:, half * 512:(half + 1) * 512], attnT[:, :], NT[:, half * 512:(half + 1) * 512],
                                             start=True, stop=True)
                        last.then_inc(s_at, 1)

                    def hidden(k, s, half, c):
                        i = 4 * half + c
                        if i >= 2 or not (isinstance(k, int) and k == 0):
                            pe.wait_ge(s_gl, k * 8 + (i - 1))
                        pe.matmul(psum[3][:, (c % 2) * 512:(c % 2) * 512 + 512], W1[s][:, c * 128:(c + 1) * 128],
                                  XA[s][:, half * 512:(half + 1) * 512], start=True, stop=True).then_inc(s_f1, 1)

                    def second(k, s, half, c):
                        pe.wait_ge(s_gl, k * 8 + (4 * half + c + 1))
                        if c == 0 and (half or not (isinstance(k, int) and k == 0)):
                            pe.wait_ge(s_yt, k * 2 + half)
                        last = pe.matmul(psum[2][:, 0:512], W2[s][:, c, :], HG[half][:, c, :], start=(c == 0), stop=(c == FC - 1))
                        if c == FC - 1:
                            last.then_inc(s_y3, 1)

                    def final(k, s, half):
                        pe.wait_ge(s_yt, k * 2 + half + 1)
                        if half or not (isinstance(k, int) and k == 0):
                            pe.wait_ge(s_z, k * 2 + half)
                        for b in range(4):
                            last = pe.matmul(psum[2][:, 512 + b * D:512 + (b + 1) * D], YT[half][:, b * N:(b + 1) * N], nextT[:, :],
                                             start=True, stop=True)
                        last.then_inc(s_nx, 1)

                    pe.wait_ge(s_c3, 16 * NC3)
                    turn(0)
                    project(0)

                    def step(k, s, e, more):
                        pe.wait_ge(s_w[s], e * 64 + 64)
                        pe.wait_ge(s_xa, k + 1)
                        for half in range(2):
                            hidden(k, s, half, 0)
                            hidden(k, s, half, 1)
                            if half:
                                final(k, s, 0)
                            second(k, s, half, 0)
                            hidden(k, s, half, 2)
                            second(k, s, half, 1)
                            hidden(k, s, half, 3)
                            second(k, s, half, 2)
                            second(k, s, half, 3)
                            if more:
                                project(k + 1) if half else turn(k + 1)
                        final(k, s, 1)

                    steps(pe, step)

                @block.scalar
                def _(act):
                    act.preload_act_table_set("gelu_and_others")
                    act.wait_ge(s_c3, 16 * NC3)

                    def front(k):
                        act.wait_ge(s_tp, k * 2 + 1)
                        act.activation(XFT[:, :], psum[0][:, :], ACT.Copy).then_inc(s_ft, 1)
                        act.wait_ge(s_tp, k * 2 + 2)
                        act.activation(NT[:, :], psum[1][:, :], ACT.Identity, scale=fcols[:, 0:1], bias=fcols[:, 1:2]).then_inc(s_ft, 1)

                    front(0)

                    def step(k, s, e, more):
                        for half in range(2):
                            for c in range(FC):
                                act.wait_ge(s_f1, k * 8 + (4 * half + c + 1))
                                if c == 0 and not (isinstance(k, int) and k == 0):
                                    act.wait_ge(s_y3, k * 2 + half - 1)
                                act.activation(HG[half][:, c, :], psum[3][:, (c % 2) * 512:(c % 2) * 512 + 512], ACT.Gelu,
                                               bias=c1[s][:, c:c + 1]).then_inc(s_gl, 1)
                            if not half and more:
                                front(k + 1)
                            if half:
                                for z in range(2):
                                    act.wait_ge(s_z, k * 2 + z + 1)
                                    act.activation(Z[z][:, :, :], Z[z][:, :, :], ACT.Gelu).then_inc(s_zg, 1)

                    steps(act, step)

                @block.vector
                def _(v):
                    n, start = [0], [0]

                    def link(ins):
                        n[0] += 1
                        ins.then_inc(s_v3, 1)
                        v.wait_ge(s_v3, start[0] + n[0])

                    def norm(k, s, e):
                        v.wait_ge(s_hn[s], e * 16 + 16)
                        for b in range(GB):
                            last = v.bn_stats(st3[:, b, :], Hn[s][:, b, :])
                        link(last)
                        v.memset(idle3[:, :], 0.0)
                        for b in range(GB):
                            last = v.bn_aggr(mv3[:, b, :], st3[:, b, :])
                        link(last)
                        v.tensor_scalar(pw3[:, 0, :], mv3[:, :, 1], 1e-5, None, ALU.add).then_inc(s_pi3, 1)
                        v.wait_ge(s_po3, k * 2 + 1)
                        link(v.tensor_tensor(rr3[:, 0, :], mv3[:, :, 1], rs3[:, 0, :], ALU.mult))
                        link(v.tensor_tensor(rr3[:, 1, :], rr3[:, 0, :], rs3[:, 0, :], ALU.mult))
                        v.tensor_scalar(pw3[:, 1, :], rr3[:, 1, :], 1e-5, None, ALU.add).then_inc(s_pi3, 1)
                        if not (isinstance(k, int) and k == 0):
                            v.wait_ge(s_tp, k * 2)
                        for b in range(GB):
                            last = v.tensor_scalar(XF[:, b, :], Hn[s][:, b, :], mv3[:, b, 0:1], rs3[:, 0, b:b + 1], ALU.subtract, ALU.mult)
                        last.then_inc(s_nf, 1)

                    def norm_again(k, s):
                        v.wait_ge(s_po3, k * 2 + 2)
                        link(v.tensor_tensor(rr3[:, 2, :], rs3[:, 0, :], rs3[:, 1, :], ALU.mult))
                        for b in range(GB):
                            last = v.tensor_scalar(NN[:, b, :], Hn[s][:, b, :], mv3[:, b, 0:1], rr3[:, 2, b:b + 1], ALU.subtract, ALU.mult)
                        last.then_inc(s_nf, 1)

                    def attended(k, s):
                        v.wait_ge(s_at, k + 1)
                        v.scalar_tensor_tensor(XA[s][:, :], psum[0][:, :], fcols[:, 2:3], XFT[:, :], ALU.add, ALU.add).then_inc(s_xa, 1)

                    def second(k, s, half):
                        v.wait_ge(s_y3, k * 2 + half + 1)
                        if not (isinstance(k, int) and k == 0):
                            v.wait_ge(s_nx, k * 2 + half - 1)
                        v.tensor_scalar(YT[half][:, :], psum[2][:, 0:512], c2[s][:, 0:1], None, ALU.add).then_inc(s_yt, 1)

                    def final(k, half):
                        v.wait_ge(s_nx, k * 2 + half + 1)
                        if not (isinstance(k, int) and k == 0):
                            v.wait_ge(s_r3, k * 2 + half - 1)
                        v.tensor_tensor(Z[half][:, :, :], psum[2][:, 512:1024].rearrange("p (b d) -> p b d", b=4),
                                        nextb[:, :].unsqueeze(1).to_broadcast([128, 4, D]), ALU.add).then_inc(s_z, 1)

                    v.wait_ge(s_c3, 16 * NC3)
                    norm(0, 0, 0)
                    norm_again(0, 0)
                    attended(0, 0)
                    norm(1, 1, 0)
                    pre = n[0]

                    def step(k, s, e, more):
                        n[0] = 0
                        start[0] = k * NORM_STEPS + pre
                        second(k, s, 0)
                        if more:
                            norm_again(k + 1, 1 - s)
                        final(k, 0)
                        second(k, s, 1)
                        if more:
                            attended(k + 1, 1 - s)
                        final(k, 1)
                        if not (isinstance(e, int) and e == EXPERTS - 1):
                            norm(k + 2, s, e + 1)
                            assert n[0] == NORM_STEPS, n[0]

                    steps(v, step)
    return nc


def kernel(**inputs):
    import concourse.bacc as bacc
    from concourse import mybir
    from concourse.bass_utils import run_bass_kernel_spmd

    c = lambda a: np.ascontiguousarray(a)
    a = {k: np.asarray(v) for k, v in inputs.items()}
    arrays = {
        "x": c(a["x"]), "y": c(a["itok_BS_0_21"]),
        "ident": np.eye(128, dtype=np.float32),
        "iota": (np.arange(3 * V) % V).astype(np.float32).reshape(3 * V, 1),
        "embT": c(a["L0_tok_W_embed"].T), "wproj": c(a["L0_tok_W_proj"]),
        "bproj": c(a["L0_tok_b_proj"].reshape(D, 1)),
        "wgap": c(a["L0_tok_W_gap"].reshape(2, D).T), "bgap": c(a["L0_tok_b_gap"]),
        "wqkvT": c(a["L0_attn_W_qkv"].T), "wposT": c(a["L0_attn_W_pos"].T), "woutT": c(a["L0_attn_W_out"].T),
        "cols": c(np.stack([a["L0_attn_ln2_g"], a["L0_attn_ln2_b"], a["L0_attn_pos_bias_u"].reshape(D),
                            a["L0_attn_pos_bias_v"].reshape(D)], axis=1)),
        "attnT": c(a["L0_ffn_attn_w"].T), "nextT": c(a["L0_ffn_next_w"].T), "next_b": c(a["L0_ffn_next_b"]),
        "fcols": c(np.stack([a["L0_ffn_ln_g"], a["L0_ffn_ln_b"], a["L0_ffn_attn_b"]], axis=1)),
        "fc1T": c(a["L0_ffn_fc1_w"].transpose(0, 2, 1)),
        "fc2T": c(a["L0_ffn_fc2_w"].reshape(EXPERTS, D, FC, 128).transpose(0, 3, 2, 1)),
        "fc1b": c(a["L0_ffn_fc1_b"].reshape(EXPERTS, FC, 128).transpose(0, 2, 1)),
        "fc2b": c(a["L0_ffn_fc2_b"].reshape(EXPERTS, D, 1)),
        "b_out": c(a["L0_attn_b_out"]), "ln1_g": c(a["L0_attn_ln1_g"]), "ln1_b": c(a["L0_attn_ln1_b"]),
        "invf": (1.0 / 10000.0 ** (np.arange(0, D, 2, dtype=np.float32) / D)).astype(np.float32),
        "headof": np.kron(np.eye(HEADS), np.ones((DK, 1))).astype(np.float32),
    }
    nc = bacc.Bacc("TRN2", target_bir_lowering=False, num_devices=1)
    feeds, t = {}, {}
    for k, v in arrays.items():
        feeds[k + "_in"] = v
        t[k] = nc.dram_tensor(k + "_in", v.shape, mybir.dt.from_np(v.dtype), kind="ExternalInput").ap()
    out = nc.dram_tensor("out_dram", (B, N, M), mybir.dt.float32, kind="ExternalOutput").ap()
    build(nc, t, out)
    r = run_bass_kernel_spmd(nc, [feeds], core_ids=[0])
    return r.results[0]["out_dram"]
```

```python
import numpy as np

B = 128
N = 128
M = 128
D = 128
V = 22
NEG = -1.0e8
ROWS = 8
NBLK = N // ROWS
CB = 8
NCH = B // CB
KKW = 2 * M + 1
HEADS = 8
DK = D // HEADS
GB = 8
NG = B // GB
TWO_PI = 2 * np.pi
TWO_PI_HI = float(np.float32(6.28125))
TWO_PI_LO = TWO_PI - TWO_PI_HI
HALF_PI = np.pi / 2
PI_IN = 3.1415925
ROUND = 1.5 * 2 ** 23
EXPERTS = 8
FF = 4 * D
FC = FF // 128
NORM_STEPS = 5
Q_PARTS = (0, 0, 1, 1, 0, 2)
P_PARTS = (0, 1, 0, 1, 2, 0)
PAIRS = len(Q_PARTS)
PER_GROUP = 6 + GB + GB + 7


def build(nc, t, out):
    import concourse.bass as bass
    from concourse import mybir
    from contextlib import ExitStack

    f32, bf16, i32 = mybir.dt.float32, mybir.dt.bfloat16, mybir.dt.int32
    ALU, ACT, AX = mybir.AluOpType, mybir.ActivationFunctionType, mybir.AxisListType
    ds = bass.ds

    kk_dram = nc.dram_tensor("kk_dram", (NBLK, B, ROWS * KKW), f32).ap()
    h_dram = nc.dram_tensor("h_dram", (B, N, M), f32).ap()
    h2_dram = nc.dram_tensor("h2_dram", (NG, N, GB * D), f32).ap()
    qs_dram = nc.dram_tensor("qs_dram", (2, 3, D, 4 * N), bf16).ap()
    ps_dram = nc.dram_tensor("ps_dram", (3, D, N), bf16).ap()
    f_dram = nc.dram_tensor("f_dram", (GB, N * (N + 1) * HEADS), f32).ap()

    def view(ap, extra, dims):
        return bass.AP(ap.tensor, ap.offset + extra, [list(ap.ap[0])] + [list(d) for d in dims])

    def backwards(ap):
        dims = [list(q) for q in ap.ap]
        step, count = dims[-1]
        dims[-1] = [-step, count]
        return bass.AP(ap.tensor, ap.offset + step * (count - 1), dims)

    def pairs(eng, count, body, until=None):
        body(0, 0)
        body(1, 1)
        with eng.Fori(1, count // 2) as it:
            body(it * 2, 0)
            body(it * 2 + 1, 1)

    def reused(k):
        return not isinstance(k, int) or k >= 2

    with ExitStack() as ctx:
        def sb(name, shape, dt=f32):
            return ctx.enter_context(nc.sbuf_tensor(name, shape, dt))

        def sem(name):
            return ctx.enter_context(nc.semaphore(name))

        psum = [ctx.enter_context(nc.psum_tensor(f"bank{i}", [128, 1024], f32)) for i in range(4)]

        ident = sb("ident", [128, 128])

        with ExitStack() as p1:
            def sb1(name, shape, dt=f32):
                return p1.enter_context(nc.sbuf_tensor(name, shape, dt))

            big_a = sb1("big_a", [128, N * B])
            big_b = sb1("big_b", [128, N * M])
            embT = sb1("embT", [D, V])
            wproj = sb1("wproj", [D, D])
            bproj = sb1("bproj", [D, 1])
            wgap = sb1("wgap", [D, 2])
            bgap = sb1("bgap", [128, 1])
            iota = sb1("iota", [3 * V, 1])
            counts = sb1("counts", [128, 2, V])
            ZT = sb1("ZT", [D, V])
            G3 = sb1("G3", [V, 3 * V], bf16)
            Gr = sb1("Gr", [V, 2, V])
            gapz = sb1("gapz", [128, 2 * V])
            Asum = sb1("Asum", [128, 2 * V])
            Acol = sb1("Acol", [128, 4])
            neg2A = sb1("neg2A", [128, 1])
            border = sb1("border", [128, 1])
            tokx = [big_b[0:V, s * CB * N:(s + 1) * CB * N].bitcast(i32) for s in range(2)]
            toky = [big_b[0:3 * V, (2 + s) * CB * M:(3 + s) * CB * M].bitcast(i32) for s in range(2)]
            ox = [big_b[0:V, (8 + s) * CB * N // 2:(9 + s) * CB * N // 2].bitcast(bf16) for s in range(2)]
            oy = [big_b[0:3 * V, (10 + s) * CB * M // 2:(11 + s) * CB * M // 2].bitcast(bf16) for s in range(2)]
            gx = [big_b[0:3 * V, (12 + s) * CB * N // 2:(13 + s) * CB * N // 2].bitcast(bf16) for s in range(2)]
            o = 14 * CB * N
            toknat = big_b[:, o:o + 256].bitcast(i32).rearrange("p (z n) -> p z n", z=2)
            tokf = big_b[:, o + 256:o + 512].rearrange("p (z n) -> p z n", z=2)
            wgapw = big_b[:, o + 512:o + 768].rearrange("p (z n) -> p z n", z=2)
            hit = big_b[:, 8 * CB * N:8 * CB * N + 2 * V * 128].rearrange("p (a n) -> p a n", n=128)
            early = sb1("early", [128, 2 * ROWS * B])
            stage = [early[:, s * ROWS * B:(s + 1) * ROWS * B].rearrange("p (r b) -> p r b", b=B) for s in range(2)]
            late = sb1("late", [128, (ROWS + 1) * (M + 1) + ROWS * M])
            KLi = [early[:, :], late[:, 0:2 * ROWS * M]]
            Tb = [sb1(f"Tb{s}", [128, ROWS, M]) for s in range(2)]
            P = late[:, 0:(ROWS + 1) * (M + 1)].rearrange("p (r n) -> p r n", n=M + 1)
            u = sb1("u", [128, M])
            Wb = late[:, (ROWS + 1) * (M + 1):].rearrange("p (r n) -> p r n", n=M)
            KK = [sb1(f"KK{s}", [128, ROWS, KKW]) for s in range(2)]
            KL = [sb1(f"KL{s}", [128, ROWS * M + 8]) for s in range(2)]
            Mb = [sb1(f"Mb{s}", [128, ROWS, M]) for s in range(2)]
            prod = sb1("prod", [128, KKW + 7])
            first = sb1("first", [128, 2 * M])
            ssum = sb1("ssum", [128, M])
            lnM = sb1("lnM", [128, M])
            carry = sb1("carry", [128, M])
            rec = sb1("rec", [128, M])
            Bb = [sb1(f"Bb{s}", [128, ROWS, 2 * (M + 1)]) for s in range(2)]
            Gb = Tb

            s_const = sem("s_const")
            s_tokn = sem("s_tokn")
            s_tok = [sem(f"s_tok{s}") for s in range(2)]
            s_pre_pe = sem("s_pre_pe")
            s_pre_act = sem("s_pre_act")
            s_pre_v = sem("s_pre_v")
            s_oneh = sem("s_oneh")
            s_gx = sem("s_gx")
            s_gxs = sem("s_gxs")
            s_th = sem("s_th")
            s_ths = sem("s_ths")
            s_stage = sem("s_stage")
            s_tr = sem("s_tr")
            s_T = sem("s_T")
            s_v = sem("s_v")
            s_zero = sem("s_zero")
            s_W = sem("s_W")
            s_raw = sem("s_raw")
            s_left = sem("s_left")
            s_exp = sem("s_exp")
            s_mrow = sem("s_mrow")
            s_ln = sem("s_ln")
            s_spill = [sem(f"s_spill{s}") for s in range(2)]
            s_load = [sem(f"s_load{s}") for s in range(2)]
            s_fwd = sem("s_fwd")
            s_one = sem("s_one")
            s_kli = sem("s_kli")
            s_b = sem("s_b")
            s_g = sem("s_g")
            s_h = [sem(f"s_h{s}") for s in range(2)]
            s_carry = sem("s_carry")

            T2 = big_a[:, :].rearrange("p (i b) -> p i b", b=B)

            NCONST = 7

            with nc.Block() as block:
                @block.sync
                def _(sp):
                    for dst, src in ((ident, t["ident"]), (embT, t["embT"]), (wproj, t["wproj"]), (bproj, t["bproj"]),
                                     (wgap, t["wgap"]), (iota, t["iota"])):
                        sp.dma_start(dst[:, :], src).then_inc(s_const, 16)
                    sp.dma_start(bgap[:, :], t["bgap"].partition_broadcast(128)).then_inc(s_const, 16)
                    sp.dma_start(toknat[:, 0, :], t["x"]).then_inc(s_tokn, 16)
                    sp.dma_start(toknat[:, 1, :], t["y"]).then_inc(s_tokn, 16)
                    xf = t["x"].rearrange("b i -> (b i)")
                    yf = t["y"].rearrange("b i -> (b i)")

                    def tokens(c, s):
                        if reused(c):
                            sp.wait_ge(s_oneh, c * 2 - 2)
                        sp.dma_start(tokx[s], xf[ds(c * (CB * N), CB * N)].partition_broadcast(V)).then_inc(s_tok[s], 16)
                        sp.dma_start(toky[s], yf[ds(c * (CB * M), CB * M)].partition_broadcast(3 * V)).then_inc(s_tok[s], 16)

                    pairs(sp, NCH, tokens)

                    def put_away(k, s):
                        sp.wait_ge(s_mrow, k + 1)
                        sp.dma_start(kk_dram[ds(k, 1), :, :].rearrange("k p n -> (k p) n"),
                                     KK[s][:, :, :].rearrange("p r n -> p (r n)")).then_inc(s_spill[s], 16)
                        sp.dma_start(big_a[:, ds(k * (ROWS * M), ROWS * M)], KL[s][:, 0:ROWS * M]).then_inc(s_spill[s], 16)
                        sp.dma_start(big_b[:, ds(k * (ROWS * M), ROWS * M)],
                                     Mb[s][:, :, :].rearrange("p r n -> p (r n)")).then_inc(s_spill[s], 16)

                    pairs(sp, NBLK - 2, put_away)
                    sp.wait_ge(s_spill[0], 48 * (NBLK // 2 - 1))
                    sp.wait_ge(s_spill[1], 48 * (NBLK // 2 - 1))
                    sp.wait_ge(s_ln, NBLK)

                    def bring_back(n, s):
                        sp.wait_ge(s_g, n - 1)
                        sp.dma_start(h_dram[:, ds(n * -ROWS + (NBLK + 1) * ROWS, ROWS), :], Gb[s][:, :, :]).then_inc(s_h[s], 16)
                        sp.wait_ge(s_carry, n - 1)
                        k = n * -1 + (NBLK - 1)
                        sp.dma_start(KK[s][:, :, :].rearrange("p r n -> p (r n)"),
                                     kk_dram[ds(k, 1), :, :].rearrange("k p n -> (k p) n")).then_inc(s_load[s], 16)
                        sp.dma_start(KL[s][:, 0:ROWS * M], big_a[:, ds(k * (ROWS * M), ROWS * M)]).then_inc(s_load[s], 16)
                        sp.dma_start(Mb[s][:, :, :].rearrange("p r n -> p (r n)"),
                                     big_b[:, ds(k * (ROWS * M), ROWS * M)]).then_inc(s_load[s], 16)

                    with sp.Fori(1, NBLK // 2) as it:
                        bring_back(it * 2, 1)
                        bring_back(it * 2 + 1, 0)
                    for n in range(2):
                        sp.wait_ge(s_g, NBLK - 1 + n)
                        sp.dma_start(h_dram[:, (1 - n) * ROWS:(2 - n) * ROWS, :], Gb[1 - n][:, :, :]).then_inc(s_h[1 - n], 16)
                    sp.wait_ge(s_h[0], 16 * NBLK // 2)
                    sp.wait_ge(s_h[1], 16 * NBLK // 2)

                @block.tensor
                def _(pe):
                    pe.wait_ge(s_const, 16 * NCONST)
                    pe.matmul(psum[0][:, 0:V], wproj[:, :], embT[:, :], start=True, stop=True).then_inc(s_pre_pe, 1)
                    pe.wait_ge(s_pre_act, 1)
                    pe.matmul(psum[1][0:V, 0:V], ZT[:, :], ZT[:, :], start=True, stop=True).then_inc(s_pre_pe, 1)
                    pe.wait_ge(s_pre_v, 1)
                    pe.matmul(psum[2][:, 0:V], wgapw[:, 0, :], ZT[:, :], start=True, stop=True)
                    pe.matmul(psum[2][:, 512:512 + V], wgapw[:, 1, :], ZT[:, :], start=True, stop=True).then_inc(s_pre_pe, 1)
                    pe.wait_ge(s_pre_v, 2)

                    def letters(c, s):
                        pe.wait_ge(s_oneh, c * 2 + 1)
                        if reused(c):
                            pe.wait_ge(s_gxs, c - 1)
                        for half in range(2):
                            last = pe.matmul(psum[s][0:3 * V, half * 512:(half + 1) * 512], G3[:, :],
                                             ox[s][:, half * 512:(half + 1) * 512], start=True, stop=True)
                        last.then_inc(s_gx, 1)

                    def scores(c, s):
                        pe.wait_ge(s_gxs, c + 1)
                        pe.wait_ge(s_oneh, c * 2 + 2)
                        if reused(c):
                            pe.wait_ge(s_ths, c - 1)
                        for b in range(CB):
                            last = pe.matmul(psum[2 + s][:, b * N:(b + 1) * N], oy[s][:, b * M:(b + 1) * M],
                                             gx[s][:, b * N:(b + 1) * N], start=True, stop=True)
                        last.then_inc(s_th, 1)

                    letters(0, 0)
                    letters(1, 1)
                    scores(0, 0)
                    with pe.Fori(1, NCH // 2) as it:
                        letters(it * 2, 0)
                        scores(it * 2 - 1, 1)
                        letters(it * 2 + 1, 1)
                        scores(it * 2, 0)
                    scores(NCH - 1, 1)

                    def turn(k, s):
                        pe.wait_ge(s_stage, k + 1)
                        for r in range(ROWS):
                            last = pe.transpose(psum[s][:, r * M:(r + 1) * M], stage[s][:, r, :], ident[:, :])
                        last.then_inc(s_tr, 1)

                    def exponents(k):
                        for q in range(ROWS // 2):
                            tile = psum[2 + q % 2]
                            pe.wait_ge(s_W, k * 4 + q + 1)
                            if q >= 2 or not (isinstance(k, int) and k == 0):
                                pe.wait_ge(s_exp, k * 4 + (q - 1))
                            pe.matmul(tile[:, 0:512], ident[:, :], view(Wb[:, 2 * q, :], 0, [[0, 2], [M, 2], [1, M]]), start=True, stop=False)
                            pe.matmul(tile[:, 0:512], ident[:, :], view(P[:, 2 * q, :], 0, [[1, 2], [M + 1, 2], [1, M]]),
                                      start=False, stop=True).then_inc(s_raw, 1)

                    turn(0, 0)
                    turn(1, 1)
                    exponents(0)
                    with pe.Fori(0, NBLK // 2 - 1) as it:
                        turn(it * 2 + 2, 0)
                        exponents(it * 2 + 1)
                        turn(it * 2 + 3, 1)
                        exponents(it * 2 + 2)
                    exponents(NBLK - 1)

                @block.gpsimd
                def _(pool):
                    pool.memset(P[:, :, :], NEG).then_inc(s_zero, 1)
                    for s in range(2):
                        pool.memset(KK[s][:, :, :], 0.0).then_inc(s_zero, 1)
                        pool.memset(Bb[s][:, :, :], 0.0).then_inc(s_zero, 1)
                    pool.wait_ge(s_ths, NCH)

                    def stage_rows(k, s):
                        if reused(k):
                            pool.wait_ge(s_T, k - 1)
                        pool.tensor_copy(stage[s][:, :, :].rearrange("p r b -> p (r b)"),
                                         big_a[:, ds(k * (ROWS * B), ROWS * B)]).then_inc(s_stage, 1)

                    def exponents(k, s):
                        if reused(k):
                            pool.wait_ge(s_spill[s], k * 24 - 24 * s)
                        for q in range(ROWS // 2):
                            pool.wait_ge(s_W, k * 4 + q + 1)
                            pool.tensor_tensor(KL[s][:, 2 * q * M:(2 * q + 2) * M].rearrange("p (r n) -> p r n", r=2),
                                               Wb[:, 2 * q:2 * q + 2, :], P[:, 2 * q + 1:2 * q + 3, 0:M], ALU.add).then_inc(s_left, 1)

                    stage_rows(0, 0)
                    stage_rows(1, 1)
                    exponents(0, 0)
                    stage_rows(2, 0)
                    exponents(1, 1)
                    with pool.Fori(1, NBLK // 2 - 1) as it:
                        stage_rows(it * 2 + 1, 1)
                        exponents(it * 2, 0)
                        stage_rows(it * 2 + 2, 0)
                        exponents(it * 2 + 1, 1)
                    stage_rows(NBLK - 1, 1)
                    exponents(NBLK - 2, 0)
                    exponents(NBLK - 1, 1)

                    pool.wait_ge(s_T, NBLK)
                    pool.memset(KLi[0][:, 0::2], 1.0).then_inc(s_one, 1)
                    pool.wait_ge(s_fwd, 1)
                    pool.memset(KLi[1][:, 0::2], 1.0).then_inc(s_one, 1)

                    def gradient(n, s):
                        pool.wait_ge(s_b, n + 1)
                        if reused(n):
                            pool.wait_ge(s_h[1 - s], 8 * n - 8 * s)
                        pool.tensor_tensor(Gb[1 - s][:, :, :], Mb[1 - s][:, :, :], Bb[1 - s][:, :, 0:2 * M:2], ALU.mult).then_inc(s_g, 1)

                    pairs(pool, NBLK, gradient)

                @block.scalar
                def _(act):
                    act.preload_act_table_set("natural_log_exp_and_others")
                    act.wait_ge(s_pre_pe, 1)
                    act.activation(ZT[:, :], psum[0][:, 0:V], ACT.Identity, bias=bproj[:, 0:1]).then_inc(s_pre_act, 1)

                    def letters(c, s):
                        act.wait_ge(s_gx, c + 1)
                        if reused(c):
                            act.wait_ge(s_th, c - 1)
                        act.activation(gx[s], psum[s][0:3 * V, :], ACT.Copy).then_inc(s_gxs, 1)

                    def scores(c, s):
                        act.wait_ge(s_th, c + 1)
                        act.activation(view(big_a[:, ds(c * CB, CB)], 0, [[B, N], [1, CB]]),
                                       psum[2 + s][:, :].rearrange("p (b i) -> p i b", b=CB), ACT.Copy).then_inc(s_ths, 1)

                    letters(0, 0)
                    letters(1, 1)
                    scores(0, 0)
                    with act.Fori(1, NCH // 2) as it:
                        letters(it * 2, 0)
                        scores(it * 2 - 1, 1)
                        letters(it * 2 + 1, 1)
                        scores(it * 2, 0)
                    scores(NCH - 1, 1)

                    def theta(k, s):
                        act.wait_ge(s_tr, k + 1)
                        act.wait_ge(s_W, k * 4 - 4)
                        act.activation(Tb[s][:, :, :], psum[s][:, :].rearrange("p (r j) -> p r j", r=ROWS), ACT.Copy).then_inc(s_T, 1)

                    def coefficients(k, s):
                        if reused(k):
                            act.wait_ge(s_spill[s], k * 24 - 24 * s)
                        for q in range(ROWS // 2):
                            act.wait_ge(s_raw, k * 4 + q + 1)
                            r = 2 * q
                            raw = psum[2 + q % 2][:, 0:512].rearrange("p (z r n) -> p z r n", z=2, r=2)
                            if q == 0 and isinstance(k, int) and k == 0:
                                act.activation(KK[s][:, 0, M + 1:2 * M], raw[:, 0, 0, 1:M], ACT.Exp, bias=border[:, 0:1])
                                act.activation(KK[s][:, 1, M + 1:2 * M], raw[:, 0, 1, 1:M], ACT.Exp, bias=neg2A[:, 0:1])
                            else:
                                act.activation(KK[s][:, r:r + 2, M + 1:2 * M], raw[:, 0, :, 1:M], ACT.Exp, bias=neg2A[:, 0:1])
                            act.activation(KK[s][:, r:r + 2, 0:M], raw[:, 1, :, :], ACT.Exp)
                            act.wait_ge(s_left, k * 4 + q + 1)
                            act.activation(KL[s][:, r * M:(r + 2) * M], KL[s][:, r * M:(r + 2) * M], ACT.Exp).then_inc(s_exp, 1)

                    def logarithm(k, s):
                        act.wait_ge(s_mrow, k + 1)
                        act.activation(lnM[:, :], Mb[s][:, ROWS - 1, :], ACT.Ln).then_inc(s_ln, 1)

                    def theta_first(k, s):
                        act.wait_ge(s_tr, k + 1)
                        act.activation(Tb[s][:, :, :], psum[s][:, :].rearrange("p (r j) -> p r j", r=ROWS), ACT.Copy).then_inc(s_T, 1)

                    theta_first(0, 0)
                    coefficients(0, 0)
                    theta_first(1, 1)
                    logarithm(0, 0)
                    with act.Fori(0, NBLK // 2 - 1) as it:
                        for k, s in ((it * 2 + 1, 1), (it * 2 + 2, 0)):
                            coefficients(k, s)
                            theta(k + 1, 1 - s)
                            logarithm(k, s)
                    coefficients(NBLK - 1, 1)
                    logarithm(NBLK - 1, 1)

                    def spread(n, s):
                        if reused(n):
                            act.wait_ge(s_load[1 - s], n * 24 - 24 * s)
                            act.wait_ge(s_b, n - 1)
                        else:
                            act.wait_ge(s_one, 1 + s)
                            act.wait_ge(s_mrow, NBLK)
                        act.activation(KLi[s][:, 1::2], KL[1 - s][:, 1:ROWS * M + 1], ACT.Copy).then_inc(s_kli, 1)

                    pairs(act, NBLK, spread)

                @block.vector
                def _(v):
                    n = [0]
                    base = [0]

                    def link(ins):
                        n[0] += 1
                        ins.then_inc(s_v, 1)
                        v.wait_ge(s_v, base[0] + n[0])

                    link(v.memset(border[:, :], NEG))
                    for s in range(2):
                        link(v.memset(KL[s][:, ROWS * M:], 0.0))
                    link(v.memset(prod[:, :], 0.0))
                    link(v.memset(first[:, :], 0.0))
                    link(v.memset(carry[:, :], 0.0))
                    link(v.memset(carry[:, M - 1:M], 1.0))
                    v.wait_ge(s_const, 16 * NCONST)
                    v.tensor_copy(wgapw[:, :, :], wgap[:, :].unsqueeze(2).to_broadcast([D, 2, 128])).then_inc(s_pre_v, 1)
                    v.wait_ge(s_pre_pe, 2)
                    g_ps = psum[1][0:V, 0:V]
                    link(v.tensor_copy(G3[:, 0:V], g_ps))
                    link(v.tensor_tensor(Gr[:, 0, :], g_ps, G3[:, 0:V], ALU.subtract))
                    link(v.tensor_copy(G3[:, V:2 * V], Gr[:, 0, :]))
                    link(v.tensor_tensor(Gr[:, 1, :], Gr[:, 0, :], G3[:, V:2 * V], ALU.subtract))
                    link(v.tensor_copy(G3[:, 2 * V:3 * V], Gr[:, 1, :]))
                    v.wait_ge(s_pre_pe, 3)
                    v.tensor_copy(gapz[:, :].rearrange("p (z a) -> p z a", z=2),
                                  psum[2][:, :].rearrange("p (z n) -> p z n", z=2)[:, :, 0:V]).then_inc(s_pre_v, 1)

                    def one_hot(c, s):
                        v.wait_ge(s_tok[s], c * 16 + (32 - 16 * s))
                        if reused(c):
                            v.wait_ge(s_gx, c - 1)
                        v.tensor_scalar(ox[s], tokx[s], iota[0:V, 0:1], None, ALU.is_equal).then_inc(s_oneh, 1)
                        if reused(c):
                            v.wait_ge(s_th, c - 1)
                        v.tensor_scalar(oy[s], toky[s], iota[:, 0:1], None, ALU.is_equal).then_inc(s_oneh, 1)

                    pairs(v, NCH, one_hot)
                    v.wait_ge(s_pre_v, 2)
                    v.wait_ge(s_tokn, 32)
                    link(v.tensor_copy(tokf[:, :, :], toknat[:, :, :]))
                    for z in range(2):
                        for a in range(V):
                            last = v.tensor_scalar(hit[:, z * V + a, :], tokf[:, z, :], float(a), None, ALU.is_equal, ALU.add,
                                                   accum_out=counts[:, z, a:a + 1])
                    link(last)
                    link(v.tensor_tensor(Asum[:, :].rearrange("p (z a) -> p z a", z=2), gapz[:, :].rearrange("p (z a) -> p z a", z=2),
                                         counts[:, :, :], ALU.mult))
                    link(v.tensor_reduce(Acol[:, 0:1], Asum[:, :], AX.X, ALU.add))
                    link(v.tensor_scalar(Acol[:, 1:2], Acol[:, 0:1], 1.0 / N, bgap[:, 0:1], ALU.mult, ALU.add))
                    link(v.tensor_scalar(neg2A[:, :], Acol[:, 1:2], -2.0, None, ALU.mult))
                    v.wait_ge(s_zero, 5)
                    link(v.memset(P[:, 0, 1:2], 0.0))

                    pre = n[0]
                    PER = 2 * ROWS + (3 * ROWS - 1) + 1
                    def forward(k, s):
                        n[0] = 0
                        base[0] = k * PER + pre
                        v.wait_ge(s_T, k + 1)

                        def less_potential(r):
                            v.tensor_tensor(Wb[:, r - 1:r + 1, :], Tb[s][:, r - 1:r + 1, :], P[:, r:r + 2, 1:], ALU.subtract).then_inc(s_W, 1)

                        for r in range(ROWS):
                            n[0] += 1
                            v.scalar_tensor_tensor(u[:, :], P[:, r, 0:M], (border if r == 0 and isinstance(k, int) and k == 0 else neg2A)[:, 0:1],
                                                   P[:, r, 1:M + 1], ALU.add, ALU.max).then_inc(s_v, 1)
                            if r and r % 2 == 0:
                                less_potential(r - 1)
                            v.wait_ge(s_v, base[0] + n[0])
                            link(v.tensor_tensor_scan(P[:, r + 1, 1:M + 1], u[:, :], Tb[s][:, r, :], NEG, ALU.max, ALU.add))
                        less_potential(ROWS - 1)
                        for r in range(ROWS):
                            if r % 2 == 0:
                                v.wait_ge(s_exp, k * 4 + (r // 2 + 1))
                            if r == 0:
                                src = KK[s][:, 0, :]
                            else:
                                link(v.tensor_tensor(view(prod[:, :], 0, [[M + 1, 2], [1, M]]),
                                                     view(KK[s][:, r, :], 0, [[M + 1, 2], [1, M]]),
                                                     Mb[s][:, r - 1:r, :].to_broadcast([128, 2, M]), ALU.mult))
                                src = prod[:, :]
                            link(v.tensor_tensor(ssum[:, :], src[:, 0:M], src[:, M:2 * M], ALU.add))
                            link(v.tensor_tensor_scan(Mb[s][:, r, :], KL[s][:, r * M:(r + 1) * M], ssum[:, :], 0.0,
                                                      ALU.mult, ALU.add))
                        v.nop().then_inc(s_mrow, 1)
                        v.wait_ge(s_ln, k + 1)
                        link(v.tensor_tensor(P[:, 0, 1:], P[:, ROWS, 1:], lnM[:, :], ALU.add))
                        assert n[0] == PER, (n[0], PER)

                    pairs(v, NBLK, forward)
                    v.nop().then_inc(s_fwd, 1)
                    pre2 = pre + PER * NBLK
                    PER2 = 2 + 2 * ROWS + 1

                    def backward(k, other):
                        s = 1 - other
                        n[0] = 0
                        base[0] = k * PER2 + pre2
                        if reused(k):
                            v.wait_ge(s_load[s], k * 24 - 24 * other)
                        link(v.reciprocal(rec[:, :], Mb[s][:, ROWS - 1, :]))
                        link(v.tensor_tensor(first[:, 1::2], carry[:, :], rec[:, :], ALU.mult))
                        v.wait_ge(s_kli, k + 1)
                        for r in range(ROWS - 1, -1, -1):
                            link(v.tensor_tensor_scan(backwards(Bb[s][:, r, 0:2 * M]), backwards(KLi[other][:, 2 * r * M:2 * (r + 1) * M]),
                                                      backwards((first if r == ROWS - 1 else prod)[:, 0:2 * M]), 0.0, ALU.mult, ALU.add))
                            if r == 0:
                                v.nop().then_inc(s_b, 1)
                            link(v.tensor_tensor(view(prod[:, :], 0, [[1, 2], [2, M]]),
                                                 view(KK[s][:, r, :], 0, [[M + 1, 2], [1, M]]),
                                                 view(Bb[s][:, r, :], 0, [[2, 2], [2, M]]), ALU.mult))
                        link(v.tensor_tensor(carry[:, :], prod[:, 0:2 * M:2], prod[:, 1:2 * M:2], ALU.add))
                        v.nop().then_inc(s_carry, 1)
                        assert n[0] == PER2, (n[0], PER2)

                    pairs(v, NBLK, backward)

        with ExitStack() as p2:
            def sb2(name, shape, dt=f32):
                return p2.enter_context(nc.sbuf_tensor(name, shape, dt))

            wqkvT = sb2("wqkvT", [D, 3 * D])
            wposT = sb2("wposT", [D, D])
            woutT = sb2("woutT", [D, D])
            bout = sb2("bout", [128, D])
            g1 = sb2("g1", [128, D])
            b1 = sb2("b1", [128, D])
            cols = sb2("cols", [128, 4])
            invf = sb2("invf", [128, D // 2])
            Pf = sb2("Pf", [D, N])
            Pc = sb2("Pc", [D, 3, N], bf16)
            PS = sb2("PS", [PAIRS * DK, HEADS, N], bf16)
            Qc = [sb2(f"Qc{z}", [D, 3, 4 * N], bf16) for z in range(2)]
            QS = [sb2(f"QS{z}", [PAIRS * DK, HEADS, 4 * N], bf16) for z in range(2)]
            rest = sb2("rest", [D, 4 * N])
            Hx = sb2("Hx", [128, GB, D])
            Hr = sb2("Hr", [128, GB, D])
            Y = sb2("Y", [128, GB, D])
            Xn = sb2("Xn", [128, GB, D])
            st = sb2("st", [128, GB, 6])
            mv = sb2("mv", [128, GB, 2])
            base_ = sb2("powbase", [128, 3, GB])
            rs = sb2("rs", [128, 3, GB])
            rr = sb2("rr", [128, 3, GB])
            mhalf = sb2("mhalf", [128, GB])
            feature = sb2("feature", [128, 1])
            trig = sb2("trig", [128, 5, D])
            peT = sb2("peT", [128, N])
            XT = sb2("XT", [D, GB * N])
            QU = [sb2(f"QU{s}", [D, GB * N]) for s in range(2)]
            QV = sb2("QV", [D, GB * N])
            KT = sb2("KT", [D, GB * N])
            Vb = [sb2(f"Vb{s}", [128, GB, HEADS, DK + 1]) for s in range(2)]
            KTm = [sb2(f"KTm{s}", [D, HEADS, GB * N]) for s in range(2)]
            FS = [sb2(f"FS{s}", [128, N + 1, HEADS]) for s in range(2)]
            BD = [sb2(f"BD{s}", [128, N, HEADS]) for s in range(4)]
            S = [sb2(f"S{s}", [128, HEADS, N]) for s in range(2)]
            nm = sb2("nm", [128, 2, HEADS])
            idle = sb2("idle", [128, 1])
            mx = sb2("mx", [128, 2, HEADS])
            E = [sb2(f"E{s}", [128, HEADS, N]) for s in range(2)]
            PT = [sb2(f"PT{s}", [128, HEADS, N]) for s in range(2)]
            rd = sb2("rd", [128, HEADS])
            On = sb2("On", [128, GB, D])
            OT = sb2("OT", [D, 4 * N])

            s_c2 = sem("s_c2")
            s_hx = sem("s_hx")
            s_hr = sem("s_hr")
            s_v2 = sem("s_v2")
            s_powin = sem("s_powin")
            s_pow = sem("s_pow")
            s_y0 = sem("s_y0")
            s_y = sem("s_y")
            s_xn = sem("s_xn")
            s_v2w = sem("s_v2w")
            s_pos = sem("s_pos")
            s_pw = sem("s_pw")
            s_ps = sem("s_ps")
            s_sp = sem("s_sp")
            s_sw = [sem(f"s_sw{z}") for z in range(2)]
            s_qst = [sem(f"s_qst{z}") for z in range(2)]
            s_posact = sem("s_posact")
            s_pospe = sem("s_pospe")
            s_xtp = sem("s_xtp")
            s_xt = sem("s_xt")
            s_q = sem("s_q")
            s_qs = sem("s_qs")
            s_k = sem("s_k")
            s_ks = sem("s_ks")
            s_vp = sem("s_vp")
            s_vs = sem("s_vs")
            s_mk = [sem(f"s_mk{s}") for s in range(2)]
            s_f = sem("s_f")
            s_fs = sem("s_fs")
            s_fw = [sem(f"s_fw{s}") for s in range(2)]
            s_bd = [sem(f"s_bd{s}") for s in range(4)]
            s_s = sem("s_s")
            s_a = sem("s_a")
            s_m = sem("s_m")
            s_e = sem("s_e")
            s_pt = sem("s_pt")
            s_pe = sem("s_pe")
            s_o = sem("s_o")
            s_n = sem("s_n")
            s_ot = sem("s_ot")
            s_ots = sem("s_ots")
            s_op = sem("s_op")
            s_res = sem("s_res")
            s_h2 = sem("s_h2")
            s_h2o = sem("s_h2o")

            NC2 = 8
            AHEAD = 4
            sums_bank = psum[3][:, 0:512]
            work_bank = psum[3][:, 512:1024]

            def rounds(eng, body):
                body(0, 0)
                body(1, 1)
                with eng.Fori(1, NG // 2 - 1) as it:
                    body(it * 2, 0)
                    body(it * 2 + 1, 1)
                body(NG - 2, 0)
                body(NG - 1, 1)

            def before(g, bound):
                return not isinstance(g, int) or g < bound

            def after(eng, done, count):
                if not (isinstance(count, int) and count <= 0):
                    eng.wait_ge(done, count)

            with nc.Block() as block:
                @block.sync
                def _(sp):
                    def load(dst, first, done):
                        sp.dma_start(dst[:, :, :], h_dram[ds(first, GB), :, :].rearrange("b i d -> i b d")).then_inc(done, 16)

                    load(Hx, 0, s_hx)
                    for dst, src in ((wqkvT[:, :], t["wqkvT"]), (wposT[:, :], t["wposT"]), (woutT[:, :], t["woutT"]),
                                     (cols[:, :], t["cols"]),
                                     (bout[:, :], t["b_out"].partition_broadcast(128)), (g1[:, :], t["ln1_g"].partition_broadcast(128)),
                                     (b1[:, :], t["ln1_b"].partition_broadcast(128)), (invf[:, :], t["invf"].partition_broadcast(128))):
                        sp.dma_start(dst, src).then_inc(s_c2, 16)

                    def put_scores(g, b):
                        sp.wait_ge(s_fs, g * GB + b + 1)
                        sp.dma_start(f_dram[b % GB, :].rearrange("(q n) -> q n", q=N),
                                     FS[b % 2][:, :, :].rearrange("p c h -> p (c h)")).then_inc(s_fw[b % 2], 16)

                    def get_scores(g, b):
                        sp.wait_ge(s_fw[b % 2], g * 64 + (b // 2) * 16 + 16)
                        sp.dma_start(BD[b % 4][:, :, :].rearrange("p k h -> p (k h)"),
                                     f_dram[b % GB, N * HEADS:].rearrange("(q n) -> q n", q=N)).then_inc(s_bd[b % 4], 16)

                    def put_parts(g, half):
                        sp.wait_ge(s_sp, g * 2 + half + 1)
                        sp.dma_start(qs_dram[half, :, :, :].rearrange("c p n -> p c n"), Qc[half][:, :, :]).then_inc(s_sw[half], 16)

                    def stack_parts(g, half):
                        sp.wait_ge(s_sw[half], g * 16 + 16)
                        for j, part in enumerate(Q_PARTS):
                            sp.dma_start(QS[half][j * DK:(j + 1) * DK, :, :],
                                         qs_dram[half, part, :, :].rearrange("(h d) n -> d h n", h=HEADS)).then_inc(s_qst[half], 16)

                    def mask_keys(g, s):
                        sp.wait_ge(s_ks, g * 2 + 2)
                        if isinstance(g, int) and g == 1:
                            sp.wait_ge(s_v2w, 5)
                        for h in range(HEADS):
                            sp.dma_start(KTm[s][h * DK:(h + 1) * DK, h, :], KT[h * DK:(h + 1) * DK, :]).then_inc(s_mk[s], 16)

                    load(Hr, 0, s_hr)
                    sp.wait_ge(s_v2w, 4)
                    sp.wait_ge(s_y0, 1)
                    sp.wait_ge(s_pos, 1)
                    load(Hx, GB, s_hx)
                    sp.wait_ge(s_pos, 2)
                    sp.dma_start(ps_dram.rearrange("c p n -> p c n"), Pc[:, :, :]).then_inc(s_pw, 16)
                    sp.wait_ge(s_pw, 16)
                    for j, part in enumerate(P_PARTS):
                        sp.dma_start(PS[j * DK:(j + 1) * DK, :, :], ps_dram[part, :, :].rearrange("(h d) n -> d h n", h=HEADS)).then_inc(s_ps, 16)
                    put_parts(0, 0)
                    put_parts(0, 1)
                    stack_parts(0, 0)
                    mask_keys(0, 0)
                    for b in range(AHEAD):
                        put_scores(0, b)
                        if b:
                            get_scores(0, b - 1)
                        if b == 1:
                            stack_parts(0, 1)

                    def round_(g, s):
                        for b in range(GB):
                            if b < 5 or before(g, NG - 1):
                                get_scores(g, b + 3)
                            if b == 3 and before(g, NG - 1):
                                stack_parts(g + 1, 0)
                            if b == 4 and not (isinstance(g, int) and g == 0):
                                written = sp.snap(g - 1)
                                sp.wait_ge(s_h2, g * 2)
                                sp.dma_start(h2_dram[ds(written, 1), :, :].rearrange("g i n -> (g i) n"),
                                             Hr[:, :, :].rearrange("p b d -> p (b d)")).then_inc(s_h2o, 16)
                            if b == 4 and before(g, NG - 1):
                                stack_parts(g + 1, 1)
                            if b < 4 or before(g, NG - 1):
                                put_scores(g, b + AHEAD)
                            if b in (2, 3) and before(g, NG - 1):
                                put_parts(g + 1, b - 2)
                            if b == 4 and not (isinstance(g, int) and g == 0):
                                first = sp.snap(g * GB)
                                sp.wait_ge(s_h2o, g * 16)
                                load(Hr, first, s_hr)
                            if b == 4 and before(g, NG - 1):
                                mask_keys(g + 1, 1 - s)
                            if b == 0 and before(g, NG - 2):
                                first = sp.snap((g + 2) * GB)
                                sp.wait_ge(s_y0, g + 2)
                                load(Hx, first, s_hx)

                    rounds(sp, round_)
                    sp.wait_ge(s_h2, NG * 2)
                    sp.dma_start(h2_dram[NG - 1, :, :], Hr[:, :, :].rearrange("p b d -> p (b d)")).then_inc(s_h2o, 16)
                    sp.wait_ge(s_h2o, NG * 16)

                @block.gpsimd
                def _(pool):
                    pool.memset(mhalf[:, :], -0.5).then_inc(s_v2w, 1)
                    for s in range(2):
                        pool.memset(FS[s][:, 0, :], 0.0).then_inc(s_v2w, 1)
                    pool.memset(KTm[0][:, :, :], 0.0).then_inc(s_v2w, 1)
                    pool.wait_ge(s_v2w, 1)

                    def powers(g, c):
                        pool.wait_ge(s_powin, g * 3 + c + 1)
                        pool.tensor_tensor(rs[:, c, :], base_[:, c, :], mhalf[:, :], ALU.pow).then_inc(s_pow, 1)

                    def affine(g):
                        pool.wait_ge(s_y0, g + 1)
                        pool.wait_ge(s_c2, 16 * NC2)
                        pool.tensor_tensor(Y[:, :, :], Y[:, :, :], g1[:, :].unsqueeze(1).to_broadcast([128, GB, D]), ALU.mult).then_inc(s_y, 1)
                        pool.wait_ge(s_y, g * 2 + 1)
                        pool.tensor_tensor(Y[:, :, :], Y[:, :, :], b1[:, :].unsqueeze(1).to_broadcast([128, GB, D]), ALU.add).then_inc(s_y, 1)

                    def residual(g):
                        pool.wait_ge(s_hr, g * 16 + 16)
                        pool.tensor_tensor(Hr[:, :, :], Hr[:, :, :], bout[:, :].unsqueeze(1).to_broadcast([128, GB, D]), ALU.add).then_inc(s_res, 1)

                    for g in range(2):
                        powers(g, 0)
                        powers(g, 1)
                        affine(g)
                        powers(g, 2)
                    pool.memset(KTm[1][:, :, :], 0.0).then_inc(s_v2w, 1)

                    def round_(g, s):
                        more = before(g, NG - 2)
                        if more:
                            powers(g + 2, 0)
                            powers(g + 2, 1)
                            affine(g + 2)
                        residual(g)
                        if more:
                            powers(g + 2, 2)

                    rounds(pool, round_)

                @block.tensor
                def _(pe):
                    pe.wait_ge(s_c2, 16 * NC2)
                    pe.wait_ge(s_posact, 1)
                    pe.transpose(psum[0][:, 0:N], trig[:, 0, :], ident[:, :]).then_inc(s_pospe, 1)
                    pe.wait_ge(s_posact, 2)
                    pe.matmul(psum[1][:, 0:N], wposT[:, :], peT[:, :], start=True, stop=True).then_inc(s_pospe, 1)

                    def turn_x(g, half):
                        if half == 0:
                            pe.wait_ge(s_xn, g + 1)
                            after(pe, s_h2, g * 2 - 3)
                        else:
                            pe.wait_ge(s_xt, g * 2 + 1)
                        for b in range(4):
                            last = pe.transpose(work_bank[:, b * N:(b + 1) * N], Xn[:, 4 * half + b, :], ident[:, :])
                        last.then_inc(s_xtp, 1)

                    def queries(g, half):
                        if half == 0:
                            pe.wait_ge(s_xt, g * 2 + 2)
                        else:
                            pe.wait_ge(s_qs, g * 2 + 1)
                        pe.matmul(work_bank, wqkvT[:, 0:D], XT[:, half * 512:(half + 1) * 512], start=True, stop=True).then_inc(s_q, 1)

                    def keys(g, half):
                        if half == 0:
                            pe.wait_ge(s_qs, g * 2 + 2)
                            after(pe, s_h2, g * 2 - 2)
                        else:
                            pe.wait_ge(s_ks, g * 2 + 1)
                        pe.matmul(work_bank, wqkvT[:, D:2 * D], XT[:, half * 512:(half + 1) * 512], start=True, stop=True).then_inc(s_k, 1)

                    def values(g, half):
                        if half == 0:
                            pe.wait_ge(s_ks, g * 2 + 2)
                        else:
                            pe.wait_ge(s_vs, g * 2 + 1)
                        for b in range(4):
                            last = pe.matmul(work_bank[:, b * D:(b + 1) * D], XT[:, (4 * half + b) * N:(4 * half + b + 1) * N],
                                             wqkvT[:, 2 * D:3 * D], start=True, stop=True)
                        last.then_inc(s_vp, 1)

                    def turn_o(g, half):
                        pe.wait_ge(s_n, g * GB + 4 * half + 4)
                        if half == 0:
                            pe.wait_ge(s_vs, g * 2 + 4 if before(g, NG - 1) else g * 2 + 2)
                        elif before(g, NG - 2):
                            pe.wait_ge(s_qs, g * 2 + 6)
                        else:
                            pe.wait_ge(s_h2, g * 2 + 1)
                        for b in range(4):
                            last = pe.transpose(work_bank[:, b * N:(b + 1) * N], On[:, 4 * half + b, :], ident[:, :])
                        last.then_inc(s_ot, 1)

                    def project(g, half):
                        pe.wait_ge(s_ots, g * 2 + half + 1)
                        for b in range(4):
                            last = pe.matmul(work_bank[:, b * D:(b + 1) * D], OT[:, b * N:(b + 1) * N], woutT[:, :], start=True, stop=True)
                        last.then_inc(s_op, 1)

                    def position_scores(g, b):
                        after(pe, s_fs, g * GB + b)
                        if b % 4 == 0:
                            pe.wait_ge(s_qst[b // 4], g * (PAIRS * 16) + PAIRS * 16)
                        for h in range(HEADS):
                            last = pe.matmul(psum[0][:, h * N:(h + 1) * N], QS[b // 4][:, h, (b % 4) * N:(b % 4 + 1) * N],
                                             PS[:, h, :], start=True, stop=True)
                        last.then_inc(s_f, 1)

                    def content_scores(g, s, b):
                        after(pe, s_a, g * GB + b)
                        if b == 0:
                            pe.wait_ge(s_qs, g * 2 + 2)
                            pe.wait_ge(s_mk[s], (g - s) * 64 + 128)
                        for half in range(2):
                            last = pe.matmul(psum[1][:, half * 512:(half + 1) * 512], QU[s][:, b * N:(b + 1) * N],
                                             KTm[s][:, 4 * half:4 * half + 4, b * N:(b + 1) * N], start=True, stop=True)
                        last.then_inc(s_s, 1)

                    def turn_e(g, b):
                        after(pe, s_pe, g * GB + b)
                        pe.wait_ge(s_e, g * GB + b + 1)
                        for h in range(HEADS):
                            last = pe.transpose(psum[2][:, h * N:(h + 1) * N], E[b % 2][:, h, :], ident[:, :])
                        last.then_inc(s_pt, 1)

                    def weighted(g, s, b):
                        pe.wait_ge(s_pe, g * GB + b + 1)
                        pe.wait_ge(s_vs, g * 2 + 2)
                        after(pe, s_n, g * GB + b)
                        for h in range(HEADS):
                            last = pe.matmul(sums_bank[:, h * (DK + 1):(h + 1) * (DK + 1)], PT[b % 2][:, h, :], Vb[s][:, b, h, :],
                                             start=True, stop=True)
                        last.then_inc(s_o, 1)

                    for step in (turn_x, queries, keys):
                        step(0, 0)
                        step(0, 1)
                    pe.wait_ge(s_ps, PAIRS * 16)
                    position_scores(0, 0)
                    values(0, 0)
                    position_scores(0, 1)
                    values(0, 1)
                    position_scores(0, 2)
                    content_scores(0, 0, 0)
                    position_scores(0, 3)

                    def round_(g, s):
                        more = before(g, NG - 1)
                        earlier = not (isinstance(g, int) and g == 0)
                        for b in range(GB):
                            if b + 1 < GB:
                                content_scores(g, s, b + 1)
                            elif more:
                                content_scores(g + 1, 1 - s, 0)
                            if more and b in (1, 2):
                                {1: turn_x, 2: queries}[b](g + 1, 1)
                            if earlier and b == 3:
                                turn_o(g - 1, 1)
                            if more and b in (4, 5):
                                {4: keys, 5: values}[b](g + 1, 0)
                            if b == 6:
                                turn_o(g, 0)
                            if b:
                                weighted(g, s, b - 1)
                            elif earlier:
                                weighted(g - 1, 1 - s, GB - 1)
                            if b < 4:
                                position_scores(g, b + AHEAD)
                            elif more:
                                position_scores(g + 1, b - AHEAD)
                            if more and b in (0, 1):
                                {0: turn_x, 1: queries}[b](g + 1, 0)
                            if earlier and b == 3:
                                project(g - 1, 1)
                            if more and b in (4, 5):
                                {4: keys, 5: values}[b](g + 1, 1)
                            if b == 6:
                                project(g, 0)
                            turn_e(g, b)

                    rounds(pe, round_)
                    weighted(NG - 1, 1, GB - 1)
                    turn_o(NG - 1, 1)
                    project(NG - 1, 1)

                @block.scalar
                def _(act):
                    act.wait_ge(s_c2, 16 * NC2)
                    act.wait_ge(s_pos, 1)
                    act.activation(trig[:, 0, :], trig[:, 4, :], ACT.Sin).then_inc(s_posact, 1)
                    act.wait_ge(s_pospe, 1)
                    act.activation(peT[:, :], psum[0][:, 0:N], ACT.Copy).then_inc(s_posact, 1)
                    act.preload_act_table_set("natural_log_exp_and_others")

                    def copy_x(g, half):
                        act.wait_ge(s_xtp, g * 2 + half + 1)
                        act.activation(XT[:, half * 512:(half + 1) * 512], work_bank, ACT.Identity,
                                       scale=cols[:, 0:1], bias=cols[:, 1:2]).then_inc(s_xt, 1)

                    def copy_q(g, s, half):
                        act.wait_ge(s_q, g * 2 + half + 1)
                        act.activation(QU[s][:, half * 512:(half + 1) * 512], work_bank, ACT.Identity, bias=cols[:, 2:3])
                        act.activation(QV[:, half * 512:(half + 1) * 512], work_bank, ACT.Identity, bias=cols[:, 3:4]).then_inc(s_qs, 1)

                    def copy_k(g, half):
                        act.wait_ge(s_k, g * 2 + half + 1)
                        act.activation(KT[:, half * 512:(half + 1) * 512], work_bank, ACT.Copy).then_inc(s_ks, 1)

                    def copy_v(g, s, half):
                        act.wait_ge(s_vp, g * 2 + half + 1)
                        act.activation(Vb[s][:, 4 * half:4 * half + 4, :, 0:DK].rearrange("p b h e -> p (b h) e"),
                                       work_bank.rearrange("p (n e) -> p n e", e=DK), ACT.Copy).then_inc(s_vs, 1)

                    def copy_o(g, half):
                        act.wait_ge(s_ot, g * 2 + half + 1)
                        act.activation(OT[:, :], work_bank, ACT.Copy).then_inc(s_ots, 1)

                    def exponentials(g, b, heads):
                        if heads[0] == 0:
                            act.wait_ge(s_m, g * GB + b + 1)
                            after(act, s_pt, g * GB + b - 1)
                        for h in heads:
                            last = act.activation(E[b % 2][:, h, :], S[b % 2][:, h, :], ACT.Exp, bias=nm[:, b % 2, h:h + 1], scale=DK ** -0.5)
                        if heads[-1] == HEADS - 1:
                            last.then_inc(s_e, 1)

                    def copy_f(g, b):
                        act.wait_ge(s_f, g * GB + b + 1)
                        after(act, s_fw[b % 2], g * 64 + (b // 2) * 16)
                        act.activation(FS[b % 2][:, 1:N + 1, :].rearrange("p c h -> p h c"),
                                       psum[0][:, :].rearrange("p (h c) -> p h c", h=HEADS), ACT.Copy).then_inc(s_fs, 1)

                    def copy_e(g, b):
                        act.wait_ge(s_pt, g * GB + b + 1)
                        after(act, s_o, g * GB + b - 1)
                        act.activation(PT[b % 2][:, :, :], psum[2][:, :].rearrange("p (h n) -> p h n", h=HEADS), ACT.Copy).then_inc(s_pe, 1)

                    copy_x(0, 0)
                    copy_x(0, 1)
                    copy_q(0, 0, 0)
                    copy_q(0, 0, 1)
                    copy_k(0, 0)
                    copy_k(0, 1)
                    copy_f(0, 0)
                    copy_v(0, 0, 0)
                    copy_f(0, 1)
                    copy_v(0, 0, 1)
                    copy_f(0, 2)
                    copy_f(0, 3)

                    def round_(g, s):
                        more = before(g, NG - 1)
                        earlier = not (isinstance(g, int) and g == 0)
                        for b in range(GB):
                            exponentials(g, b, range(HEADS // 2))
                            if more and b == 1:
                                copy_x(g + 1, 1)
                            if more and b == 2:
                                copy_q(g + 1, 1 - s, 1)
                            if earlier and b == 3:
                                copy_o(g - 1, 1)
                            if more and b == 4:
                                copy_k(g + 1, 0)
                            if more and b == 5:
                                copy_v(g + 1, 1 - s, 0)
                            if b == 6:
                                copy_o(g, 0)
                            exponentials(g, b, range(HEADS // 2, HEADS))
                            if more and b == 0:
                                copy_x(g + 1, 0)
                            if more and b == 1:
                                copy_q(g + 1, 1 - s, 0)
                            if more and b == 4:
                                copy_k(g + 1, 1)
                            if more and b == 5:
                                copy_v(g + 1, 1 - s, 1)
                            copy_e(g, b)
                            if b < 4 or more:
                                copy_f(g, b + AHEAD)

                    rounds(act, round_)
                    copy_o(NG - 1, 1)

                @block.vector
                def _(v):
                    n, start = [0], [0]

                    def link(ins):
                        n[0] += 1
                        ins.then_inc(s_v2, 1)
                        v.wait_ge(s_v2, start[0] + n[0])

                    def moments(src):
                        for b in range(GB):
                            last = v.bn_stats(st[:, b, :], src[:, b, :])
                        link(last)
                        v.memset(idle[:, :], 0.0)
                        for b in range(GB):
                            last = v.bn_aggr(mv[:, b, :], st[:, b, :])
                        link(last)

                    def norm_1(g):
                        v.wait_ge(s_hx, g * 16 + 16)
                        moments(Hx)
                        v.tensor_scalar(base_[:, 0, :], mv[:, :, 1], 1e-5, None, ALU.add).then_inc(s_powin, 1)

                    def norm_2(g):
                        v.wait_ge(s_pow, g * 3 + 1)
                        link(v.tensor_tensor(rr[:, 0, :], mv[:, :, 1], rs[:, 0, :], ALU.mult))
                        link(v.tensor_tensor(rr[:, 1, :], rr[:, 0, :], rs[:, 0, :], ALU.mult))
                        v.tensor_scalar(base_[:, 1, :], rr[:, 1, :], 1e-5, None, ALU.add).then_inc(s_powin, 1)

                    def norm_3(g):
                        v.wait_ge(s_pow, g * 3 + 2)
                        link(v.tensor_tensor(rr[:, 2, :], rs[:, 0, :], rs[:, 1, :], ALU.mult))
                        for b in range(GB):
                            last = v.tensor_scalar(Y[:, b, :], Hx[:, b, :], mv[:, b, 0:1], rr[:, 2, b:b + 1], ALU.subtract, ALU.mult)
                        last.then_inc(s_y0, 1)

                    def norm_4(g):
                        v.wait_ge(s_y, g * 2 + 2)
                        moments(Y)
                        v.tensor_scalar(base_[:, 2, :], mv[:, :, 1], 1e-5, None, ALU.add).then_inc(s_powin, 1)

                    def norm_5(g):
                        v.wait_ge(s_pow, g * 3 + 3)
                        after(v, s_xtp, g * 2)
                        for b in range(GB):
                            last = v.tensor_scalar(Xn[:, b, :], Y[:, b, :], mv[:, b, 0:1], rs[:, 2, b:b + 1], ALU.subtract, ALU.mult)
                        last.then_inc(s_xn, 1)

                    def split(x, hi, mid, lo):
                        r = rest[:, 0:x.shape[-1]]
                        link(v.tensor_copy(hi, x))
                        link(v.tensor_tensor(r, x, hi, ALU.subtract))
                        link(v.tensor_copy(mid, r))
                        return v.tensor_tensor(lo, r, mid, ALU.subtract)

                    def split_q(g, half):
                        v.wait_ge(s_qs, g * 2 + half + 1)
                        if half:
                            v.wait_ge(s_sp, g * 2 + 1)
                        else:
                            after(v, s_sp, g * 2)
                        split(QV[:, half * 512:(half + 1) * 512], Qc[half][:, 0, :], Qc[half][:, 1, :], Qc[half][:, 2, :]).then_inc(s_sp, 1)

                    def add_scores(g, b):
                        v.wait_ge(s_s, g * GB + b + 1)
                        v.wait_ge(s_bd[b % 4], g * 32 + (b // 4) * 16 + 16)
                        after(v, s_e, g * GB + b - 1)
                        v.tensor_tensor(S[b % 2][:, :, :], psum[1][:, :].rearrange("p (h k) -> p h k", h=HEADS),
                                        BD[b % 4][:, :, :].rearrange("p k h -> p h k"), ALU.add).then_inc(s_a, 1)
                        v.wait_ge(s_a, g * GB + b + 1)
                        link(v.tensor_reduce(mx[:, b % 2, :], S[b % 2][:, :, :], AX.X, ALU.max))
                        v.tensor_scalar(nm[:, b % 2, :], mx[:, b % 2, :], -DK ** -0.5, None, ALU.mult).then_inc(s_m, 1)

                    def divide(g, b):
                        v.wait_ge(s_o, g * GB + b + 1)
                        sums = sums_bank[:, 0:HEADS * (DK + 1)].rearrange("p (h e) -> p h e", h=HEADS)
                        link(v.reciprocal(rd[:, :], sums[:, :, DK]))
                        v.tensor_tensor(On[:, b, :].rearrange("p (h e) -> p h e", h=HEADS), sums[:, :, 0:DK],
                                        rd[:, :].unsqueeze(2).to_broadcast([128, HEADS, DK]), ALU.mult).then_inc(s_n, 1)

                    def residual(g, half):
                        v.wait_ge(s_res, g + 1)
                        v.wait_ge(s_op, g * 2 + half + 1)
                        rows = Hr[:, 4 * half:4 * half + 4, :]
                        v.tensor_tensor(rows, work_bank.rearrange("p (b d) -> p b d", b=4), rows, ALU.add).then_inc(s_h2, 1)

                    for s in range(2):
                        link(v.memset(Vb[s][:, :, :, :], 1.0))
                    norm_1(0)
                    norm_2(0)
                    v.wait_ge(s_c2, 16 * NC2)
                    norm_3(0)
                    link(v.tensor_scalar(feature[:, :], Hx[:, 0, 0:1], mv[:, 0, 0:1], rs[:, 0, 0:1], ALU.subtract, ALU.mult))
                    H2 = D // 2
                    x_, k_ = trig[:, 1, 0:H2], trig[:, 2, 0:H2]
                    a_ = trig[:, 3, 0:H2]
                    sin_, cos_ = trig[:, 4, 0:H2], trig[:, 4, H2:D]
                    link(v.tensor_scalar(x_, invf[:, :], feature[:, :], None, ALU.mult))
                    link(v.tensor_scalar(k_, x_, 1.0 / TWO_PI, ROUND, ALU.mult, ALU.add))
                    link(v.tensor_scalar(k_, k_, ROUND, None, ALU.subtract))
                    link(v.scalar_tensor_tensor(a_, k_, -TWO_PI_HI, x_, ALU.mult, ALU.add))
                    link(v.scalar_tensor_tensor(a_, k_, -TWO_PI_LO, a_, ALU.mult, ALU.add))
                    link(v.tensor_scalar(sin_, a_, PI_IN, -PI_IN, ALU.min, ALU.max))
                    link(v.tensor_scalar(x_, a_, HALF_PI, None, ALU.add))
                    link(v.tensor_scalar(k_, x_, PI_IN, -TWO_PI, ALU.is_gt, ALU.mult))
                    link(v.tensor_tensor(x_, x_, k_, ALU.add))
                    link(v.tensor_scalar(cos_, x_, PI_IN, -PI_IN, ALU.min, ALU.max))
                    v.nop().then_inc(s_pos, 1)
                    norm_4(0)
                    norm_5(0)
                    v.wait_ge(s_pospe, 2)
                    link(v.tensor_copy(Pf[:, :], psum[1][:, 0:N]))
                    link(split(Pf[:, :], Pc[:, 0, :], Pc[:, 1, :], Pc[:, 2, :]))
                    v.nop().then_inc(s_pos, 1)
                    split_q(0, 0)
                    split_q(0, 1)
                    norm_1(1)
                    norm_2(1)
                    norm_3(1)
                    norm_4(1)
                    add_scores(0, 0)
                    norm_5(1)
                    done = [n[0]]

                    def round_(g, s):
                        if isinstance(g, int):
                            start[0] = done[0] if g < 2 else done[0] + (g - 2) * per_round[0] - passed[0]
                        else:
                            start[0] = (g - 2) * per_round[0] + done[0]
                        n[0] = 0
                        more = before(g, NG - 1)
                        more_2 = before(g, NG - 2)
                        earlier = not (isinstance(g, int) and g == 0)
                        for b in range(GB):
                            if b + 1 < GB:
                                add_scores(g, b + 1)
                            elif more:
                                add_scores(g + 1, 0)
                            if b:
                                divide(g, b - 1)
                            elif earlier:
                                divide(g - 1, GB - 1)
                            if more and b in (2, 3):
                                split_q(g + 1, b - 2)
                            if more_2 and b in (1, 2, 4, 6, 7):
                                {1: norm_1, 2: norm_2, 4: norm_3, 6: norm_4, 7: norm_5}[b](g + 2)
                            if earlier and b == 3:
                                residual(g - 1, 1)
                            if b == 6:
                                residual(g, 0)
                        if isinstance(g, int) and g < 2:
                            done[0] += n[0]
                        elif more_2:
                            assert n[0] == per_round[0], n[0]
                        elif more:
                            passed[0] = per_round[0] - n[0]

                    per_round, passed = [PER_GROUP], [0]
                    rounds(v, round_)
                    start[0] += n[0]
                    n[0] = 0
                    divide(NG - 1, GB - 1)
                    residual(NG - 1, 1)


        with ExitStack() as p3:
            def sb3(name, shape, dt=f32):
                return p3.enter_context(nc.sbuf_tensor(name, shape, dt))

            attnT = sb3("attnT", [D, D])
            nextT = sb3("nextT", [D, D])
            nextb = sb3("nextb", [128, D])
            fcols = sb3("fcols", [128, 3])
            W1 = [sb3(f"W1{s}", [D, FF]) for s in range(2)]
            W2 = [sb3(f"W2{s}", [128, FC, D]) for s in range(2)]
            c1 = [sb3(f"c1{s}", [128, FC]) for s in range(2)]
            c2 = [sb3(f"c2{s}", [128, 1]) for s in range(2)]
            Hn = [sb3(f"Hn{s}", [128, GB, D]) for s in range(2)]
            H3 = [sb3(f"H3{s}", [128, GB, D]) for s in range(2)]
            XF = sb3("XF", [128, GB, D])
            NN = sb3("NN", [128, GB, D])
            XFT = sb3("XFT", [D, GB * N])
            NT = sb3("NT", [D, GB * N])
            XA = [sb3(f"XA{s}", [D, GB * N]) for s in range(2)]
            HG = [sb3(f"HG{s}", [128, FC, 512]) for s in range(2)]
            YT = [sb3(f"YT{s}", [D, 512]) for s in range(2)]
            Z = [sb3(f"Z{s}", [128, 4, D]) for s in range(2)]
            st3 = sb3("st3", [128, GB, 6])
            mv3 = sb3("mv3", [128, GB, 2])
            pw3 = sb3("pw3", [128, 2, GB])
            rs3 = sb3("rs3", [128, 2, GB])
            rr3 = sb3("rr3", [128, 3, GB])
            mhalf3 = sb3("mhalf3", [128, GB])
            idle3 = sb3("idle3", [128, 1])

            s_c3 = sem("s_c3")
            s_mh = sem("s_mh")
            s_hn = [sem(f"s_hn{s}") for s in range(2)]
            s_h3 = [sem(f"s_h3{s}") for s in range(2)]
            s_w = [sem(f"s_w{s}") for s in range(2)]
            s_v3 = sem("s_v3")
            s_pi3 = sem("s_pi3")
            s_po3 = sem("s_po3")
            s_nf = sem("s_nf")
            s_tp = sem("s_tp")
            s_ft = sem("s_ft")
            s_at = sem("s_at")
            s_xa = sem("s_xa")
            s_f1 = sem("s_f1")
            s_gl = sem("s_gl")
            s_y3 = sem("s_y3")
            s_yt = sem("s_yt")
            s_nx = sem("s_nx")
            s_z = sem("s_z")
            s_zg = sem("s_zg")
            s_r3 = sem("s_r3")
            s_out = [sem(f"s_out{s}") for s in range(2)]

            NC3 = 4

            def steps(eng, body):
                body(0, 0, 0, True)
                body(1, 1, 0, True)
                with eng.Fori(1, EXPERTS - 1) as e:
                    body(e * 2, 0, e, True)
                    body(e * 2 + 1, 1, e, True)
                body(NG - 2, 0, EXPERTS - 1, True)
                body(NG - 1, 1, EXPERTS - 1, False)

            out_g = out.rearrange("(g b) i d -> g i b d", b=GB)

            with nc.Block() as block:
                @block.sync
                def _(sp):
                    def load(dst, e, s, done):
                        sp.dma_start(dst[s][:, :, :].rearrange("p b d -> p (b d)"),
                                     h2_dram[ds(e + EXPERTS * s, 1), :, :].rearrange("g i n -> (g i) n")).then_inc(done[s], 16)

                    for s in range(2):
                        load(Hn, 0, s, s_hn)
                    for dst, src in ((attnT[:, :], t["attnT"]), (nextT[:, :], t["nextT"]), (fcols[:, :], t["fcols"]),
                                     (nextb[:, :], t["next_b"].partition_broadcast(128))):
                        sp.dma_start(dst, src).then_inc(s_c3, 16)

                    def weights(e, s):
                        sp.dma_start(W1[s][:, :], t["fc1T"][ds(e, 1), :, :].rearrange("e d h -> (e d) h")).then_inc(s_w[s], 16)
                        sp.dma_start(W2[s][:, :, :], t["fc2T"][ds(e, 1), :, :, :].rearrange("e h c d -> (e h) c d")).then_inc(s_w[s], 16)
                        sp.dma_start(c1[s][:, :], t["fc1b"][ds(e, 1), :, :].rearrange("e h c -> (e h) c")).then_inc(s_w[s], 16)
                        sp.dma_start(c2[s][:, :], t["fc2b"][ds(e, 1), :, :].rearrange("e h c -> (e h) c")).then_inc(s_w[s], 16)

                    for s in range(2):
                        weights(0, s)
                        load(H3, 0, s, s_h3)

                    def step(k, s, e, more):
                        again = not (isinstance(e, int) and e == EXPERTS - 1)
                        if again:
                            sp.wait_ge(s_nf, k * 2 + 2)
                            load(Hn, e + 1, s, s_hn)
                            sp.wait_ge(s_yt, k * 2 + 2)
                            weights(e + 1, s)
                        sp.wait_ge(s_r3, k * 2 + 2)
                        sp.dma_start(out_g[ds(e + EXPERTS * s, 1), :, :, :].rearrange("g i b d -> (g i) b d"), H3[s][:, :, :]).then_inc(s_out[s], 16)
                        if again:
                            sp.wait_ge(s_out[s], e * 16 + 16)
                            load(H3, e + 1, s, s_h3)

                    steps(sp, step)
                    sp.wait_ge(s_out[0], 16 * EXPERTS)
                    sp.wait_ge(s_out[1], 16 * EXPERTS)

                @block.gpsimd
                def _(pool):
                    pool.memset(mhalf3[:, :], -0.5).then_inc(s_mh, 1)
                    pool.wait_ge(s_mh, 1)

                    def norm(k):
                        for c in range(2):
                            pool.wait_ge(s_pi3, k * 2 + c + 1)
                            pool.tensor_tensor(rs3[:, c, :], pw3[:, c, :], mhalf3[:, :], ALU.pow).then_inc(s_po3, 1)

                    norm(0)
                    norm(1)

                    def step(k, s, e, more):
                        pool.wait_ge(s_h3[s], e * 16 + 16)
                        for half in range(2):
                            pool.wait_ge(s_zg, k * 2 + half + 1)
                            pool.tensor_tensor(H3[s][:, 4 * half:4 * half + 4, :], Z[half][:, :, :], H3[s][:, 4 * half:4 * half + 4, :],
                                               ALU.add).then_inc(s_r3, 1)
                        if not (isinstance(e, int) and e == EXPERTS - 1):
                            norm(k + 2)

                    steps(pool, step)

                @block.tensor
                def _(pe):
                    def turn(k, z):
                        if z == 0 and not (isinstance(k, int) and k == 0):
                            pe.wait_ge(s_xa, k * 2)
                        pe.wait_ge(s_nf, k * 2 + z + 1)
                        for b in range(GB):
                            last = pe.transpose(psum[z][:, b * N:(b + 1) * N], (XF, NN)[z][:, b, :], ident[:, :])
                        last.then_inc(s_tp, 1)

                    def project(k):
                        pe.wait_ge(s_ft, k * 2 + 2)
                        for half in range(2):
                            pe.matmul(psum[0][:, half * 512:(half + 1) * 512], attnT[:, :], NT[:, half * 512:(half + 1) * 512],
                                      start=True, stop=True).then_inc(s_at, 1)

                    def hidden(k, s, half, c):
                        i = 4 * half + c
                        if i >= 2 or not (isinstance(k, int) and k == 0):
                            pe.wait_ge(s_gl, k * 8 + (i - 1))
                        pe.matmul(psum[3][:, (c % 2) * 512:(c % 2) * 512 + 512], W1[s][:, c * 128:(c + 1) * 128],
                                  XA[s][:, half * 512:(half + 1) * 512], start=True, stop=True).then_inc(s_f1, 1)

                    def second(k, s, half, c):
                        pe.wait_ge(s_gl, k * 8 + (4 * half + c + 1))
                        if c == 0 and (half or not (isinstance(k, int) and k == 0)):
                            pe.wait_ge(s_yt, k * 2 + half)
                        last = pe.matmul(psum[2][:, 0:512], W2[s][:, c, :], HG[half][:, c, :], start=(c == 0), stop=(c == FC - 1))
                        if c == FC - 1:
                            last.then_inc(s_y3, 1)

                    def final(k, s, half):
                        pe.wait_ge(s_yt, k * 2 + half + 1)
                        if half or not (isinstance(k, int) and k == 0):
                            pe.wait_ge(s_z, k * 2 + half)
                        for b in range(4):
                            last = pe.matmul(psum[2][:, 512 + b * D:512 + (b + 1) * D], YT[half][:, b * N:(b + 1) * N], nextT[:, :],
                                             start=True, stop=True)
                        last.then_inc(s_nx, 1)

                    pe.wait_ge(s_c3, 16 * NC3)
                    turn(0, 0)
                    turn(0, 1)
                    project(0)

                    def step(k, s, e, more):
                        pe.wait_ge(s_w[s], e * 64 + 64)
                        for half in range(2):
                            pe.wait_ge(s_xa, k * 2 + half + 1)
                            hidden(k, s, half, 0)
                            hidden(k, s, half, 1)
                            if half:
                                final(k, s, 0)
                                if more:
                                    turn(k + 1, 1)
                            second(k, s, half, 0)
                            hidden(k, s, half, 2)
                            second(k, s, half, 1)
                            hidden(k, s, half, 3)
                            second(k, s, half, 2)
                            second(k, s, half, 3)
                            if more:
                                project(k + 1) if half else turn(k + 1, 0)
                        final(k, s, 1)

                    steps(pe, step)

                @block.scalar
                def _(act):
                    act.preload_act_table_set("gelu_and_others")
                    act.wait_ge(s_c3, 16 * NC3)

                    def copy_xf(k):
                        act.wait_ge(s_tp, k * 2 + 1)
                        act.activation(XFT[:, :], psum[0][:, :], ACT.Copy).then_inc(s_ft, 1)

                    def copy_nn(k):
                        act.wait_ge(s_tp, k * 2 + 2)
                        act.activation(NT[:, :], psum[1][:, :], ACT.Identity, scale=fcols[:, 0:1], bias=fcols[:, 1:2]).then_inc(s_ft, 1)

                    copy_xf(0)
                    copy_nn(0)

                    def step(k, s, e, more):
                        for half in range(2):
                            for c in range(FC):
                                if half and more and c == 2:
                                    copy_nn(k + 1)
                                act.wait_ge(s_f1, k * 8 + (4 * half + c + 1))
                                if c == 0 and not (isinstance(k, int) and k == 0):
                                    act.wait_ge(s_y3, k * 2 + half - 1)
                                act.activation(HG[half][:, c, :], psum[3][:, (c % 2) * 512:(c % 2) * 512 + 512], ACT.Gelu,
                                               bias=c1[s][:, c:c + 1]).then_inc(s_gl, 1)
                            if not half and more:
                                copy_xf(k + 1)
                            if half:
                                for z in range(2):
                                    act.wait_ge(s_z, k * 2 + z + 1)
                                    act.activation(Z[z][:, :, :], Z[z][:, :, :], ACT.Gelu).then_inc(s_zg, 1)

                    steps(act, step)

                @block.vector
                def _(v):
                    n, start = [0], [0]

                    def link(ins):
                        n[0] += 1
                        ins.then_inc(s_v3, 1)
                        v.wait_ge(s_v3, start[0] + n[0])

                    def norm(k, s, e):
                        v.wait_ge(s_hn[s], e * 16 + 16)
                        for b in range(GB):
                            last = v.bn_stats(st3[:, b, :], Hn[s][:, b, :])
                        link(last)
                        v.memset(idle3[:, :], 0.0)
                        for b in range(GB):
                            last = v.bn_aggr(mv3[:, b, :], st3[:, b, :])
                        link(last)
                        v.tensor_scalar(pw3[:, 0, :], mv3[:, :, 1], 1e-5, None, ALU.add).then_inc(s_pi3, 1)
                        v.wait_ge(s_po3, k * 2 + 1)
                        link(v.tensor_tensor(rr3[:, 0, :], mv3[:, :, 1], rs3[:, 0, :], ALU.mult))
                        link(v.tensor_tensor(rr3[:, 1, :], rr3[:, 0, :], rs3[:, 0, :], ALU.mult))
                        v.tensor_scalar(pw3[:, 1, :], rr3[:, 1, :], 1e-5, None, ALU.add).then_inc(s_pi3, 1)
                        if not (isinstance(k, int) and k == 0):
                            v.wait_ge(s_tp, k * 2)
                        for b in range(GB):
                            last = v.tensor_scalar(XF[:, b, :], Hn[s][:, b, :], mv3[:, b, 0:1], rs3[:, 0, b:b + 1], ALU.subtract, ALU.mult)
                        last.then_inc(s_nf, 1)

                    def norm_again(k, s):
                        v.wait_ge(s_po3, k * 2 + 2)
                        link(v.tensor_tensor(rr3[:, 2, :], rs3[:, 0, :], rs3[:, 1, :], ALU.mult))
                        for b in range(GB):
                            last = v.tensor_scalar(NN[:, b, :], Hn[s][:, b, :], mv3[:, b, 0:1], rr3[:, 2, b:b + 1], ALU.subtract, ALU.mult)
                        last.then_inc(s_nf, 1)

                    def attended(k, s):
                        for half in range(2):
                            v.wait_ge(s_at, k * 2 + half + 1)
                            columns = slice(half * 512, half * 512 + 512)
                            v.scalar_tensor_tensor(XA[s][:, columns], psum[0][:, columns], fcols[:, 2:3], XFT[:, columns],
                                                   ALU.add, ALU.add).then_inc(s_xa, 1)

                    def second(k, s, half):
                        v.wait_ge(s_y3, k * 2 + half + 1)
                        if not (isinstance(k, int) and k == 0):
                            v.wait_ge(s_nx, k * 2 + half - 1)
                        v.tensor_scalar(YT[half][:, :], psum[2][:, 0:512], c2[s][:, 0:1], None, ALU.add).then_inc(s_yt, 1)

                    def final(k, half):
                        v.wait_ge(s_nx, k * 2 + half + 1)
                        if not (isinstance(k, int) and k == 0):
                            v.wait_ge(s_r3, k * 2 + half - 1)
                        v.tensor_tensor(Z[half][:, :, :], psum[2][:, 512:1024].rearrange("p (b d) -> p b d", b=4),
                                        nextb[:, :].unsqueeze(1).to_broadcast([128, 4, D]), ALU.add).then_inc(s_z, 1)

                    v.wait_ge(s_c3, 16 * NC3)
                    norm(0, 0, 0)
                    norm_again(0, 0)
                    attended(0, 0)
                    norm(1, 1, 0)
                    pre = n[0]

                    def step(k, s, e, more):
                        n[0] = 0
                        start[0] = k * NORM_STEPS + pre
                        second(k, s, 0)
                        if more:
                            norm_again(k + 1, 1 - s)
                        final(k, 0)
                        second(k, s, 1)
                        if more:
                            attended(k + 1, 1 - s)
                        final(k, 1)
                        if not (isinstance(e, int) and e == EXPERTS - 1):
                            norm(k + 2, s, e + 1)
                            assert n[0] == NORM_STEPS, n[0]

                    steps(v, step)
    return nc


def kernel(**inputs):
    import concourse.bacc as bacc
    from concourse import mybir
    from concourse.bass_utils import run_bass_kernel_spmd

    c = lambda a: np.ascontiguousarray(a)
    a = {k: np.asarray(v) for k, v in inputs.items()}
    arrays = {
        "x": c(a["x"]), "y": c(a["itok_BS_0_21"]),
        "ident": np.eye(128, dtype=np.float32),
        "iota": (np.arange(3 * V) % V).astype(np.float32).reshape(3 * V, 1),
        "embT": c(a["L0_tok_W_embed"].T), "wproj": c(a["L0_tok_W_proj"]),
        "bproj": c(a["L0_tok_b_proj"].reshape(D, 1)),
        "wgap": c(a["L0_tok_W_gap"].reshape(2, D).T), "bgap": c(a["L0_tok_b_gap"]),
        "wqkvT": c(a["L0_attn_W_qkv"].T), "wposT": c(a["L0_attn_W_pos"].T), "woutT": c(a["L0_attn_W_out"].T),
        "cols": c(np.stack([a["L0_attn_ln2_g"], a["L0_attn_ln2_b"], a["L0_attn_pos_bias_u"].reshape(D),
                            a["L0_attn_pos_bias_v"].reshape(D)], axis=1)),
        "attnT": c(a["L0_ffn_attn_w"].T), "nextT": c(a["L0_ffn_next_w"].T), "next_b": c(a["L0_ffn_next_b"]),
        "fcols": c(np.stack([a["L0_ffn_ln_g"], a["L0_ffn_ln_b"], a["L0_ffn_attn_b"]], axis=1)),
        "fc1T": c(a["L0_ffn_fc1_w"].transpose(0, 2, 1)),
        "fc2T": c(a["L0_ffn_fc2_w"].reshape(EXPERTS, D, FC, 128).transpose(0, 3, 2, 1)),
        "fc1b": c(a["L0_ffn_fc1_b"].reshape(EXPERTS, FC, 128).transpose(0, 2, 1)),
        "fc2b": c(a["L0_ffn_fc2_b"].reshape(EXPERTS, D, 1)),
        "b_out": c(a["L0_attn_b_out"]), "ln1_g": c(a["L0_attn_ln1_g"]), "ln1_b": c(a["L0_attn_ln1_b"]),
        "invf": (1.0 / 10000.0 ** (np.arange(0, D, 2, dtype=np.float32) / D)).astype(np.float32),
    }
    nc = bacc.Bacc("TRN2", target_bir_lowering=False, num_devices=1)
    feeds, t = {}, {}
    for k, v in arrays.items():
        feeds[k + "_in"] = v
        t[k] = nc.dram_tensor(k + "_in", v.shape, mybir.dt.from_np(v.dtype), kind="ExternalInput").ap()
    out = nc.dram_tensor("out_dram", (B, N, M), mybir.dt.float32, kind="ExternalOutput").ap()
    build(nc, t, out)
    r = run_bass_kernel_spmd(nc, [feeds], core_ids=[0])
    return r.results[0]["out_dram"]
```
